# Optimizing a Trainium2 kernel written in Bass

```python
import numpy as np
import jax
import jax.numpy as jnp

def _softmax(x, axis=-1):
    return jax.nn.softmax(x, axis=axis)

def _gelu(x):
    return jax.nn.gelu(x, approximate=True)

def _silu(x):
    return jax.nn.silu(x)

def _sigmoid(x):
    return jax.nn.sigmoid(x)

def _layernorm(x, axis=-1, eps=1e-05):
    m = jnp.mean(x, axis=axis, keepdims=True)
    v = jnp.var(x, axis=axis, keepdims=True)
    return (x - m) / jnp.sqrt(v + eps)

def _scatter_add(tgt, idx, src, axis=0):
    return tgt.at[idx].add(src)

def _segment_sum(src, seg, n):
    return jax.ops.segment_sum(src, seg, n)
kernel_name = 'mk_decoder_postln_d2_seqx_r8_3e023a'

def setup_inputs(seed: int=0):
    np.random.seed(seed)
    _w = jnp.asarray

    def _rec_inputs():
        import jax
        import jax.numpy as jnp
        _rk = jax.random.key(seed)
        x = 7.22e-05 + 1 * jax.random.normal(jax.random.fold_in(_rk, 1), (4, 512, 128), jnp.float32)
        _lenS = 512 - jax.random.randint(jax.random.fold_in(_rk, 7), (4,), 0, max(1, 512 // 4) + 1, jnp.int32)
        _lenS2 = 77 - jax.random.randint(jax.random.fold_in(_rk, 8), (4,), 0, max(1, 77 // 4) + 1, jnp.int32)
        _ctx_1024P = jax.random.normal(jax.random.fold_in(_rk, 11), (4, 16, 128), jnp.float32)
        _ctx_1024c = jax.random.dirichlet(jax.random.fold_in(_rk, 511), 0.3 * jnp.ones((16,), jnp.float32), (4, 77))
        _ctx_1024t = jnp.einsum('bsk,bkd->bsd', _ctx_1024c, _ctx_1024P)
        _ctx_1024t = _ctx_1024t * jax.lax.rsqrt(jnp.mean(jnp.square(_ctx_1024t)) + 1e-12) * 0.953939
        ctx_1024 = 4.13588e-05 + 0.999923 * (_ctx_1024t + 0.3 * jax.random.normal(jax.random.fold_in(_rk, 611), (4, 77, 128), jnp.float32))
        return (x, ctx_1024)
    x, ctx_1024 = _rec_inputs()

    def _L0_attn_setup():
        import jax, jax.numpy as jnp
        import numpy as np
        DIM = 128
        HEADS = 16
        DIM_HEAD = 64
        B, S = (4, 256)
        key = jax.random.key(seed)
        ks = jax.random.split(key, 6)
        sd = 1.0 / np.sqrt(DIM)
        return {'latents': jax.random.normal(ks[0], (B, S, DIM), dtype=jnp.float32), 'ln_gamma': jnp.ones((DIM,), dtype=jnp.float32), 'ln_beta': jnp.zeros((DIM,), dtype=jnp.float32), 'Wq': jax.random.normal(ks[1], (DIM, HEADS * DIM_HEAD), dtype=jnp.float32) * sd, 'Wk': jax.random.normal(ks[2], (DIM, HEADS * DIM_HEAD), dtype=jnp.float32) * sd, 'Wv': jax.random.normal(ks[3], (DIM, HEADS * DIM_HEAD), dtype=jnp.float32) * sd, 'Wo': jax.random.normal(ks[4], (HEADS * DIM_HEAD, DIM), dtype=jnp.float32) * sd}
    _L0_attn_all = _L0_attn_setup()
    _L0_attn_in = {k: v for k, v in _L0_attn_all.items() if k in ('ln_gamma', 'ln_beta', 'Wq', 'Wk', 'Wv', 'Wo')}
    del _L0_attn_all

    def _L0_xattn_setup():
        import jax, jax.numpy as jnp
        import numpy as np
        N_HEAD, MODEL_DIM, KEY_DIM, VALUE_DIM = (16, 128, 64, 64)
        B, S = (4, 256)
        EPS = 1e-05
        TEMP = float(np.sqrt(KEY_DIM))
        key = jax.random.key(seed)
        ks = jax.random.split(key, 12)
        d = {'query': jax.random.normal(ks[0], (B, S, MODEL_DIM), jnp.float32), 'key': jax.random.normal(ks[1], (B, S, MODEL_DIM), jnp.float32), 'value': jax.random.normal(ks[2], (B, S, MODEL_DIM), jnp.float32), 'Wq': jax.random.normal(ks[3], (MODEL_DIM, N_HEAD * KEY_DIM), jnp.float32) * np.sqrt(2.0 / (MODEL_DIM + KEY_DIM)), 'bq': jnp.zeros((N_HEAD * KEY_DIM,), jnp.float32), 'Wk': jax.random.normal(ks[4], (MODEL_DIM, N_HEAD * KEY_DIM), jnp.float32) * np.sqrt(2.0 / (MODEL_DIM + KEY_DIM)), 'bk': jnp.zeros((N_HEAD * KEY_DIM,), jnp.float32), 'Wv': jax.random.normal(ks[5], (MODEL_DIM, N_HEAD * VALUE_DIM), jnp.float32) * np.sqrt(2.0 / (MODEL_DIM + VALUE_DIM)), 'bv': jnp.zeros((N_HEAD * VALUE_DIM,), jnp.float32), 'Wo': jax.random.normal(ks[6], (N_HEAD * VALUE_DIM, MODEL_DIM), jnp.float32) * np.sqrt(2.0 / (N_HEAD * VALUE_DIM + MODEL_DIM)), 'bo': jnp.zeros((MODEL_DIM,), jnp.float32), 'ln_gamma': jnp.ones((MODEL_DIM,), jnp.float32), 'ln_beta': jnp.zeros((MODEL_DIM,), jnp.float32)}
        return d
    _L0_xattn_all = _L0_xattn_setup()
    _L0_xattn_in = {k: v for k, v in _L0_xattn_all.items() if k in ('Wq', 'bq', 'Wk', 'bk', 'Wv', 'bv', 'Wo', 'bo', 'ln_gamma', 'ln_beta')}
    del _L0_xattn_all

    def _L0_ffn_setup():
        import jax, jax.numpy as jnp
        import numpy as np
        TOP_K = 2
        key = jax.random.key(seed)
        ks = jax.random.split(key, 6)
        B, T, H, E, F = (2, 256, 128, 8, 512)
        s = 0.02
        return {'hidden_states': jax.random.normal(ks[0], (B, T, H), dtype=jnp.float32), 'router_w': jax.random.normal(ks[1], (E, H), dtype=jnp.float32) * s, 'w1': jax.random.normal(ks[2], (E, F, H), dtype=jnp.float32) * s, 'b1': jax.random.normal(ks[3], (E, F), dtype=jnp.float32) * s, 'w2': jax.random.normal(ks[4], (E, H, F), dtype=jnp.float32) * s, 'b2': jax.random.normal(ks[5], (E, H), dtype=jnp.float32) * s}
    _L0_ffn_all = _L0_ffn_setup()
    _L0_ffn_in = {k: v for k, v in _L0_ffn_all.items() if k in ('router_w', 'w1', 'b1', 'w2', 'b2')}
    del _L0_ffn_all

    def _L1_attn_setup():
        import jax, jax.numpy as jnp
        import numpy as np
        B, S, D_MODEL = (2, 256, 128)
        H, D = (16, 64)
        D_INNER = H * D
        EPS = 1e-05
        key = jax.random.key(seed)
        ks = jax.random.split(key, 10)
        sc = 0.02
        return {'x': jax.random.normal(ks[0], (B, S, D_MODEL), dtype=jnp.float32), 'Wq': jax.random.normal(ks[1], (D_MODEL, D_INNER), dtype=jnp.float32) * sc, 'Wk': jax.random.normal(ks[2], (D_MODEL, D_INNER), dtype=jnp.float32) * sc, 'Wv': jax.random.normal(ks[3], (D_MODEL, D_INNER), dtype=jnp.float32) * sc, 'Wg': jax.random.normal(ks[4], (D_MODEL, D_INNER), dtype=jnp.float32) * sc, 'Wa': jax.random.normal(ks[5], (D_MODEL, H), dtype=jnp.float32) * sc, 'ba': jax.random.normal(ks[6], (H,), dtype=jnp.float32) * sc, 'Wo': jax.random.normal(ks[7], (D_INNER, D_MODEL), dtype=jnp.float32) * sc, 'gn_w': jnp.ones((D_INNER,), dtype=jnp.float32), 'gn_b': jnp.zeros((D_INNER,), dtype=jnp.float32)}
    _L1_attn_all = _L1_attn_setup()
    _L1_attn_in = {k: v for k, v in _L1_attn_all.items() if k in ('Wq', 'Wk', 'Wv', 'Wg', 'Wa', 'ba', 'Wo', 'gn_w', 'gn_b')}
    del _L1_attn_all

    def _L1_xattn_setup():
        import jax, jax.numpy as jnp
        import numpy as np
        DIM = 128
        NUM_HEADS = 8
        HEAD_DIM = 64
        INNER = NUM_HEADS * HEAD_DIM
        key = jax.random.key(seed)
        ks = jax.random.split(key, 7)
        B, N, M = (8, 64, 512)
        x = jax.random.normal(ks[0], (B, N, DIM), dtype=jnp.float32)
        context = jax.random.normal(ks[1], (B, M, DIM), dtype=jnp.float32)
        s_in = 1.0 / np.sqrt(DIM)
        s_inner = 1.0 / np.sqrt(INNER)
        Wq = jax.random.normal(ks[2], (DIM, INNER), dtype=jnp.float32) * s_in
        Wk = jax.random.normal(ks[3], (DIM, INNER), dtype=jnp.float32) * s_in
        Wv = jax.random.normal(ks[4], (DIM, INNER), dtype=jnp.float32) * s_in
        Wo = jax.random.normal(ks[5], (INNER, DIM), dtype=jnp.float32) * s_inner
        bo = jax.random.normal(ks[6], (DIM,), dtype=jnp.float32) * 0.01
        return {'x': x, 'context': context, 'Wq': Wq, 'Wk': Wk, 'Wv': Wv, 'Wo': Wo, 'bo': bo}
    _L1_xattn_all = _L1_xattn_setup()
    _L1_xattn_in = {k: v for k, v in _L1_xattn_all.items() if k in ('Wq', 'Wk', 'Wv', 'Wo', 'bo')}
    del _L1_xattn_all

    def _L1_ffn_setup():
        import jax, jax.numpy as jnp
        import numpy as np
        B, S, D, H, E = (4, 256, 128, 256, 8)
        key = jax.random.key(seed)
        ks = jax.random.split(key, 8)
        scale = 0.02
        return {'x': jax.random.normal(ks[0], (B, S, D), dtype=jnp.float32), 'Wr': jax.random.normal(ks[1], (D, E), dtype=jnp.float32) * scale, 'br': jnp.zeros((E,), dtype=jnp.float32), 'W1': jax.random.normal(ks[2], (E, D, H), dtype=jnp.float32) * scale, 'b1': jnp.zeros((E, H), dtype=jnp.float32), 'W2': jax.random.normal(ks[3], (E, H, D), dtype=jnp.float32) * scale, 'b2': jnp.zeros((E, D), dtype=jnp.float32)}
    _L1_ffn_all = _L1_ffn_setup()
    _L1_ffn_in = {k: v for k, v in _L1_ffn_all.items() if k in ('Wr', 'br', 'W1', 'b1', 'W2', 'b2')}
    del _L1_ffn_all
    return {'x': x, 'ctx_1024': ctx_1024, 'L0_attn_ln_gamma': _L0_attn_in['ln_gamma'], 'L0_attn_ln_beta': _L0_attn_in['ln_beta'], 'L0_attn_Wq': _L0_attn_in['Wq'], 'L0_attn_Wk': _L0_attn_in['Wk'], 'L0_attn_Wv': _L0_attn_in['Wv'], 'L0_attn_Wo': _L0_attn_in['Wo'], 'L0_xattn_Wq': _L0_xattn_in['Wq'], 'L0_xattn_bq': _L0_xattn_in['bq'], 'L0_xattn_Wk': _L0_xattn_in['Wk'], 'L0_xattn_bk': _L0_xattn_in['bk'], 'L0_xattn_Wv': _L0_xattn_in['Wv'], 'L0_xattn_bv': _L0_xattn_in['bv'], 'L0_xattn_Wo': _L0_xattn_in['Wo'], 'L0_xattn_bo': _L0_xattn_in['bo'], 'L0_xattn_ln_gamma': _L0_xattn_in['ln_gamma'], 'L0_xattn_ln_beta': _L0_xattn_in['ln_beta'], 'L0_ffn_router_w': _L0_ffn_in['router_w'], 'L0_ffn_w1': _L0_ffn_in['w1'], 'L0_ffn_b1': _L0_ffn_in['b1'], 'L0_ffn_w2': _L0_ffn_in['w2'], 'L0_ffn_b2': _L0_ffn_in['b2'], 'L1_attn_Wq': _L1_attn_in['Wq'], 'L1_attn_Wk': _L1_attn_in['Wk'], 'L1_attn_Wv': _L1_attn_in['Wv'], 'L1_attn_Wg': _L1_attn_in['Wg'], 'L1_attn_Wa': _L1_attn_in['Wa'], 'L1_attn_ba': _L1_attn_in['ba'], 'L1_attn_Wo': _L1_attn_in['Wo'], 'L1_attn_gn_w': _L1_attn_in['gn_w'], 'L1_attn_gn_b': _L1_attn_in['gn_b'], 'L1_xattn_Wq': _L1_xattn_in['Wq'], 'L1_xattn_Wk': _L1_xattn_in['Wk'], 'L1_xattn_Wv': _L1_xattn_in['Wv'], 'L1_xattn_Wo': _L1_xattn_in['Wo'], 'L1_xattn_bo': _L1_xattn_in['bo'], 'L1_ffn_Wr': _L1_ffn_in['Wr'], 'L1_ffn_br': _L1_ffn_in['br'], 'L1_ffn_W1': _L1_ffn_in['W1'], 'L1_ffn_b1': _L1_ffn_in['b1'], 'L1_ffn_W2': _L1_ffn_in['W2'], 'L1_ffn_b2': _L1_ffn_in['b2']}

def reference(x, ctx_1024, L0_attn_ln_gamma, L0_attn_ln_beta, L0_attn_Wq, L0_attn_Wk, L0_attn_Wv, L0_attn_Wo, L0_xattn_Wq, L0_xattn_bq, L0_xattn_Wk, L0_xattn_bk, L0_xattn_Wv, L0_xattn_bv, L0_xattn_Wo, L0_xattn_bo, L0_xattn_ln_gamma, L0_xattn_ln_beta, L0_ffn_router_w, L0_ffn_w1, L0_ffn_b1, L0_ffn_w2, L0_ffn_b2, L1_attn_Wq, L1_attn_Wk, L1_attn_Wv, L1_attn_Wg, L1_attn_Wa, L1_attn_ba, L1_attn_Wo, L1_attn_gn_w, L1_attn_gn_b, L1_xattn_Wq, L1_xattn_Wk, L1_xattn_Wv, L1_xattn_Wo, L1_xattn_bo, L1_ffn_Wr, L1_ffn_br, L1_ffn_W1, L1_ffn_b1, L1_ffn_W2, L1_ffn_b2):
    import jax
    import jax.numpy as jnp

    def _L0_attn_ref(latents, ln_gamma, ln_beta, Wq, Wk, Wv, Wo):
        import jax, jax.numpy as jnp
        import numpy as np
        DIM = 128
        HEADS = 16
        DIM_HEAD = 64
        B, S = (4, 256)
        mu = jnp.mean(latents, axis=-1, keepdims=True)
        var = jnp.mean((latents - mu) ** 2, axis=-1, keepdims=True)
        x = (latents - mu) * jax.lax.rsqrt(var + 1e-05) * ln_gamma + ln_beta
        b, s, _ = x.shape
        q = (x @ Wq).reshape(b, s, HEADS, DIM_HEAD).transpose(0, 2, 1, 3)
        k = (x @ Wk).reshape(b, s, HEADS, DIM_HEAD).transpose(0, 2, 1, 3)
        v = (x @ Wv).reshape(b, s, HEADS, DIM_HEAD).transpose(0, 2, 1, 3)
        scale = 1.0 / np.sqrt(np.sqrt(DIM_HEAD))
        scores = jnp.einsum('bhqd,bhkd->bhqk', q * scale, k * scale)
        weights = jax.nn.softmax(scores.astype(jnp.float32), axis=-1).astype(scores.dtype)
        out = jnp.einsum('bhqk,bhkd->bhqd', weights, v)
        out = out.transpose(0, 2, 1, 3).reshape(b, s, HEADS * DIM_HEAD)
        return out @ Wo

    def _L0_xattn_ref(query, key, value, Wq, bq, Wk, bk, Wv, bv, Wo, bo, ln_gamma, ln_beta):
        import jax, jax.numpy as jnp
        import numpy as np
        N_HEAD, MODEL_DIM, KEY_DIM, VALUE_DIM = (16, 128, 64, 64)
        B, S = (4, 256)
        EPS = 1e-05
        TEMP = float(np.sqrt(KEY_DIM))
        b, sq, _ = query.shape
        residual = query
        q = (query @ Wq + bq).reshape(b, sq, N_HEAD, KEY_DIM)
        k = (key @ Wk + bk).reshape(b, key.shape[1], N_HEAD, KEY_DIM)
        v = (value @ Wv + bv).reshape(b, value.shape[1], N_HEAD, VALUE_DIM)
        scores = jnp.einsum('bqhd,bkhd->bhqk', q, k) / TEMP
        attn = jax.nn.softmax(scores, axis=-1)
        out = jnp.einsum('bhqk,bkhd->bqhd', attn, v).reshape(b, sq, N_HEAD * VALUE_DIM)
        out = out @ Wo + bo + residual
        mu = jnp.mean(out, axis=-1, keepdims=True)
        var = jnp.var(out, axis=-1, keepdims=True)
        return (out - mu) * jax.lax.rsqrt(var + EPS) * ln_gamma + ln_beta

    def _L0_ffn_ref(hidden_states, router_w, w1, b1, w2, b2):
        import jax, jax.numpy as jnp
        import numpy as np
        TOP_K = 2
        x = hidden_states
        router_logits = jnp.einsum('bth,eh->bte', x, router_w)
        topk_values, topk_indices = jax.lax.top_k(router_logits, TOP_K)
        topk_weights = jax.nn.softmax(topk_values.astype(jnp.float32), axis=-1).astype(x.dtype)
        h1 = jnp.einsum('bth,efh->btef', x, w1) + b1
        h1 = jax.nn.gelu(h1, approximate=False)
        expert_outputs = jnp.einsum('btef,ehf->bteh', h1, w2) + b2
        gather_idx = topk_indices[..., None]
        topk_expert_outputs = jnp.take_along_axis(expert_outputs, gather_idx, axis=2)
        mixed_output = jnp.sum(topk_expert_outputs * topk_weights[..., None], axis=2)
        return mixed_output

    def _L1_attn_ref(x, Wq, Wk, Wv, Wg, Wa, ba, Wo, gn_w, gn_b):
        import jax, jax.numpy as jnp
        import numpy as np
        B, S, D_MODEL = (2, 256, 128)
        H, D = (16, 64)
        D_INNER = H * D
        EPS = 1e-05
        b, s, _ = x.shape
        q = jax.nn.silu(jnp.einsum('bsm,md->bsd', x, Wq).reshape(b, s, H, D).transpose(0, 2, 1, 3))
        k = jax.nn.silu(jnp.einsum('bsm,md->bsd', x, Wk).reshape(b, s, H, D).transpose(0, 2, 1, 3))
        v = jnp.einsum('bsm,md->bsd', x, Wv).reshape(b, s, H, D).transpose(0, 2, 1, 3)
        log_alpha = -jax.nn.softplus(jnp.einsum('bsm,mh->bsh', x, Wa) + ba)
        cum = jnp.cumsum(log_alpha, axis=1).transpose(0, 2, 1)
        diff = cum[:, :, :, None] - cum[:, :, None, :]
        causal = jnp.tril(jnp.ones((s, s), dtype=bool))
        decay = jnp.exp(jnp.where(causal, diff, -jnp.inf))
        attn = jnp.einsum('bhid,bhjd->bhij', q, k) * decay
        o = jnp.einsum('bhij,bhjd->bhid', attn, v)
        o = o.transpose(0, 2, 1, 3)
        mean = jnp.mean(o, axis=(1, 3), keepdims=True)
        var = jnp.var(o, axis=(1, 3), keepdims=True)
        o = (o - mean) / jnp.sqrt(var + EPS)
        o = o * gn_w.reshape(H, D) + gn_b.reshape(H, D)
        o = o.reshape(b, s, H * D)
        gate = jax.nn.sigmoid(jnp.einsum('bsm,md->bsd', x, Wg))
        return jnp.einsum('bsd,dm->bsm', o * gate, Wo)

    def _L1_xattn_ref(x, context, Wq, Wk, Wv, Wo, bo):
        import jax, jax.numpy as jnp
        import numpy as np
        DIM = 128
        NUM_HEADS = 8
        HEAD_DIM = 64
        INNER = NUM_HEADS * HEAD_DIM
        B, N, _ = x.shape
        M = context.shape[1]
        scale = HEAD_DIM ** (-0.5)
        q = (x @ Wq).reshape(B, N, NUM_HEADS, HEAD_DIM).transpose(0, 2, 1, 3)
        k = (context @ Wk).reshape(B, M, NUM_HEADS, HEAD_DIM).transpose(0, 2, 1, 3)
        v = (context @ Wv).reshape(B, M, NUM_HEADS, HEAD_DIM).transpose(0, 2, 1, 3)
        attn = jax.nn.softmax(jnp.einsum('bhnd,bhmd->bhnm', q, k) * scale, axis=-1)
        out = jnp.einsum('bhnm,bhmd->bhnd', attn, v)
        out = out.transpose(0, 2, 1, 3).reshape(B, N, INNER)
        return out @ Wo + bo

    def _L1_ffn_ref(x, Wr, br, W1, b1, W2, b2):
        import jax, jax.numpy as jnp
        import numpy as np
        B, S, D, H, E = (4, 256, 128, 256, 8)
        d = x.shape[-1]
        tokens = x.reshape(-1, d)
        logits = tokens @ Wr + br
        probs = jax.nn.softmax(logits, axis=-1)
        expert = jnp.argmax(probs, axis=-1)
        max_prob = jnp.take_along_axis(probs, expert[:, None], axis=-1)
        h = jax.nn.relu(jnp.einsum('td,edh->teh', tokens, W1) + b1[None])
        y = jnp.einsum('teh,ehd->ted', h, W2) + b2[None]
        out = jnp.take_along_axis(y, expert[:, None, None], axis=1)[:, 0, :]
        return (out * max_prob).reshape(x.shape)
    x = _layernorm(x + _L0_attn_ref(x, L0_attn_ln_gamma, L0_attn_ln_beta, L0_attn_Wq, L0_attn_Wk, L0_attn_Wv, L0_attn_Wo), axis=-1)
    x = _layernorm(x + _L0_xattn_ref(x, ctx_1024, ctx_1024, L0_xattn_Wq, L0_xattn_bq, L0_xattn_Wk, L0_xattn_bk, L0_xattn_Wv, L0_xattn_bv, L0_xattn_Wo, L0_xattn_bo, L0_xattn_ln_gamma, L0_xattn_ln_beta), axis=-1)
    x = _layernorm(x + _L0_ffn_ref(x, L0_ffn_router_w, L0_ffn_w1, L0_ffn_b1, L0_ffn_w2, L0_ffn_b2), axis=-1)
    x = _layernorm(x + _L1_attn_ref(x, L1_attn_Wq, L1_attn_Wk, L1_attn_Wv, L1_attn_Wg, L1_attn_Wa, L1_attn_ba, L1_attn_Wo, L1_attn_gn_w, L1_attn_gn_b), axis=-1)
    x = _layernorm(x + _L1_xattn_ref(x, ctx_1024, L1_xattn_Wq, L1_xattn_Wk, L1_xattn_Wv, L1_xattn_Wo, L1_xattn_bo), axis=-1)
    x = _layernorm(x + _L1_ffn_ref(x, L1_ffn_Wr, L1_ffn_br, L1_ffn_W1, L1_ffn_b1, L1_ffn_W2, L1_ffn_b2), axis=-1)
    return x

_drawn_inputs = setup_inputs


def setup_inputs(seed=0):
    import zlib

    import numpy as np

    out = dict(_drawn_inputs(seed))
    spreads = {'L0_attn_ln_gamma': (1.0, 0.2),
     'L0_attn_ln_beta': (0.0, 0.1),
     'L0_xattn_bq': (0.0, 0.365),
     'L0_xattn_bk': (0.0, 0.8),
     'L0_xattn_bv': (0.0, 0.1),
     'L0_xattn_bo': (0.0, 0.1),
     'L0_xattn_ln_gamma': (1.0, 0.2),
     'L0_xattn_ln_beta': (0.0, 0.1),
     'L1_attn_gn_w': (1.0, 0.2),
     'L1_attn_gn_b': (0.0, 0.292),
     'L1_ffn_br': (0.0, 0.577),
     'L1_ffn_b1': (0.0, 0.8),
     'L1_ffn_b2': (0.0, 0.458)}
    factors = {'L0_ffn_b1': 8.0,
     'L0_ffn_b2': 3.908,
     'L1_attn_Wa': 2.853,
     'L1_attn_ba': 8.0,
     'L1_xattn_bo': 5.859,
     'L1_ffn_Wr': 3.037,
     'L1_ffn_W1': 7.626,
     'L1_ffn_W2': 6.018}
    for name, (base, spread) in spreads.items():
        noise = np.random.default_rng([zlib.crc32(name.encode()), seed]).standard_normal(out[name].shape)
        drawn = base * np.exp(spread * noise) if base else spread * noise
        out[name] = jnp.asarray(drawn.astype(out[name].dtype))
    for name, factor in factors.items():
        out[name] = (out[name] * factor).astype(out[name].dtype)
    return out
```

```python
from contextlib import ExitStack

import concourse.bass as bass
from concourse import mybir

P = 128
ALU = mybir.AluOpType
ACT = mybir.ActivationFunctionType
AX = mybir.AxisListType.X
F32 = mybir.dt.float32
BF16 = mybir.dt.bfloat16
U32 = mybir.dt.uint32

NB = 4
S = 512
NT = S // P
D = 128
DH = 64
C = 77
H = 16
NPAIR = H // 2
HX1 = 8
E = 8
FT0 = 4
FT1 = 2
EPS = 1e-5
UNITS = H * NT
PB, PC, PD, PE_, PF = 4, 8, 12, 16, 20
WORKS = 24

COLS = {}
_n = 0
for _name, _w in (("ln_g", 1), ("ln_b", 1), ("bq", 8), ("bk", 8), ("bv", 8), ("bo0", 1), ("b1_0", 32),
                  ("gn_w", 8), ("gn_b", 8), ("bo1", 1), ("b1_1", 16)):
    COLS[_name] = (_n, _n + _w)
    _n += _w
NCOLS = _n
ROWS = {"xg": (0, 128), "xb": (128, 256), "ba": (256, 272), "br": (272, 280)}
NROWS = 280
CONSTS = {"ident": (0, 128), "upto": (128, 256), "after": (256, 384), "block": (384, 512), "iota": (512, 520),
          "sel": (520, 536), "mask": (536, 1048)}
NCONSTS = 1048


def decoder(nc, T):
    with ExitStack() as ctx:
        def sb(name, shape, dt=F32):
            return ctx.enter_context(nc.sbuf_tensor(name, shape, dt))

        sems = {}

        def sem(name):
            if name not in sems:
                sems[name] = ctx.enter_context(nc.semaphore(name))
            return sems[name]

        bank = [ctx.enter_context(nc.psum_tensor(f"bank{i}", [P, S], F32)) for i in range(8)]
        x_all = sb("x_all", [P, NB * NT, D])
        xT_all = sb("xT_all", [P, NB, S])
        yT = sb("yT", [P, S])
        res = sb("res", [P, NT, D])
        OT = sb("OT", [P, NPAIR, S])
        W0 = sb("W0", [P, 8192])
        W1 = sb("W1", [P, 5120])
        cols = sb("cols", [P, NCOLS])
        rows = sb("rows", [P, NROWS])
        cst = sb("cst", [P, NCONSTS - 512])
        mask = sb("mask", [P, S], BF16)
        ident_b = sb("ident_b", [P, P], BF16)
        sel = sb("sel", [P, H], BF16)
        rw = sb("rw", [P, 32])
        b2 = sb("b2", [E, 2, D])
        bn = sb("bn", [P, NT, 6])
        mv = sb("mv", [P, NT, 2])
        lnv = sb("lnv", [P, 6, NT])
        rt = sb("rt", [P, 12, 4, 8])
        ri = sb("ri", [P, 4, 8], U32)
        work = sb("work", [P, 27136])

        def col(name, i=0):
            return cols[:, COLS[name][0] + i:COLS[name][0] + i + 1]

        ident = cst[:, 0:128]
        upto = cst[:, 128:256]
        after = cst[:, 256:384]
        block = cst[:, 384:512]
        iota = cst[:, 512:520]

        def carve(at, n, count=1):
            return [work[:, at + i * n:at + (i + 1) * n] for i in range(count)], at + n * count

        (xn,), a = carve(0, S)
        xnT, a = carve(a, S, 2)
        vA, a = carve(a, NT * H * DH, 2)
        qTA, a = carve(a, S, 2)
        kzA, a = carve(a, 2 * S, 2)
        pA, a = carve(a, S, 3)
        ptA, a = carve(a, NT * S, 4)
        rsum, a = carve(a, 8, 2)
        nmax, a = carve(a, 8)
        assert a <= 27136
        nmax = nmax[0]
        (kdB,), a = carve(0, NPAIR * NB * 2 * C)
        (vcB,), a = carve(a, NB * H * DH)
        (qTB,), a = carve(a, NPAIR * S)
        pB, a = carve(a, H * P, 2)
        (ptB,), a = carve(a, H * S)
        statB, a = carve(a, 16, 6)
        assert a <= 27136
        hsC, a = carve(0, S, 3)
        hwC, a = carve(a, S, 3)
        (wT_C,), a = carve(a, 2 * S)
        (wselC,), a = carve(a, S)
        tmpC, a = carve(a, S, 2)
        vD, a = carve(0, NT * S, 2)
        qTD, a = carve(a, S, 2)
        qbD, a = carve(a, 2 * S, 2)
        kTD, a = carve(a, S, 2)
        qeD, a = carve(a, S, 2)
        elD, a = carve(a, S, 2)
        dmD, a = carve(a, 2 * S, 2)
        atD, a = carve(a, 2 * S, 2)
        kdD, a = carve(a, S, 2)
        stD, a = carve(a, 3 * P, 2)
        oxD, a = carve(a, S, 4)
        thD, a = carve(a, S, 12)
        tqD, a = carve(a, S, 2)
        spD, a = carve(a, 64, 4)
        (lselD,), a = carve(a, S)
        lcD, a = carve(a, 128, 2)
        kdecD, a = carve(a, 64, 2)
        gnD, a = carve(a, 16, 8)
        (gn6,), a = carve(a, 8)
        assert a <= 27136, a
        tmpD = [yT, res]

        wsel_b = [wselC[:, i * 256:(i + 1) * 256].bitcast(BF16) for i in range(2)]
        lsel_b = [lselD[:, i * 256:(i + 1) * 256].bitcast(BF16) for i in range(2)]
        spl_r = sb("spl_r", [16, S])
        spl_m = sb("spl_m", [16, S], BF16)

        def v3(ap, n):
            return ap.rearrange("p (n k) -> p n k", n=n)

        wqA, wkA, wvA, woA = (W0[:, i * 1024:(i + 1) * 1024] for i in range(4))
        wqB, wkB, wvB, woB = (W1[:, i * 1024:(i + 1) * 1024] for i in range(4))
        w1C, w2C = W0[:, 0:4096], W0[:, 4096:8192]
        wqD, wkD, wvD, wgD, woD = (W1[:, i * 1024:(i + 1) * 1024] for i in range(5))
        wqE, wkE, wvE, woE = (W0[:, i * 512:(i + 1) * 512] for i in range(4))
        w1F, w2F = W1[:, 0:2048], W1[:, 2048:4096]

        ctxT = sb("ctxT", [P, NB * C])

        def out_w(ph):
            return {0: woA, 1: woB, 3: woD, 4: woE}[ph]

        def o_slot(w, p):
            if w // NB == 3:
                s = (8 * (w % NB) + p) % 12
                return OT[:, s, :] if s < 8 else oxD[s - 8]
            return OT[:, p, :]

        CROSS = {1: dict(n="B", w0=PB, np=NPAIR, wq=wqB, wk=wkB, wv=wvB, bias=True),
                 4: dict(n="E", w0=PE_, np=HX1 // 2, wq=wqE, wk=wkE, wv=wvE, bias=False)}
        MOE = {2: dict(n="C", w0=PC, ft=FT0, w1=w1C, w2=w2C, b1="b1_0", r=0, func=ACT.Gelu),
               5: dict(n="F", w0=PF, ft=FT1, w1=w1F, w2=w2F, b1="b1_1", r=1, func=ACT.Relu)}

        TAIL = {0: (9, 13, 14, 15, 20), 1: (1, 3, 4, 5, 8), 2: (3, 5, 6, 8, 11), 3: (3, 4, 5, 5, 6),
                4: (1, 3, 4, 5, 8), 5: (3, 5, 6, 8, 11)}

        def tail_steps(w):
            return (0, 1, 2, 2, 3) if w == PD - 1 else TAIL[min((w + 1) // NB, 5)]

        y_ready, yT_ready, yt_ready = sem("y_ready"), sem("yT_ready"), sem("yt_ready")
        x_ready, xTp_ready, xT_ready = sem("x_ready"), sem("xTp_ready"), sem("xT_ready")
        ln_var, ln_rsqrt = sem("ln_var"), sem("ln_rsqrt")
        dve_chain, act_chain, pool_chain = sem("dve_chain"), sem("act_chain"), sem("pool_chain")
        dma_in = {k: sem("dma_" + k) for k in ("x", "small", "A", "B", "C", "D", "E", "F", "out")}
        consts_ready = sem("consts_ready")

        def loaded(eng, what, n=1):
            eng.wait_ge(dma_in[what], 16 * n)

        DMA_COUNT = {"x": 4, "small": 7, "A": 4, "B": 5, "C": 2, "D": 5, "E": 4, "F": 2}

        ENDS = {0: [("a_pv", 32), ("a_s", 256), ("a_pt", 256), ("a_o", 32)],
                1: [("B_pv", 32), ("B_o", 32)],
                2: [("y_ready", 12), ("C_hw", 128)],
                3: [("y_ready", 15), ("d_og", 32), ("d_pv", 32), ("d_x", 1)],
                4: [("E_pv", 16), ("E_o", 16)]}

        def enter(eng, ph):
            for name, value in ENDS[ph - 1]:
                eng.wait_ge(sem(name), value)

        owner = {}
        where = {}

        def take(pe, i, reader, value):
            if i in owner:
                s, n = owner[i]
                pe.wait_ge(s, n)
            owner[i] = (reader, value)
            return bank[i]

        turn = [0]

        def take_next(pe, key, reader, value):
            i = 6 + turn[0] % 2
            turn[0] += 1
            where[key] = bank[i]
            return take(pe, i, reader, value)

        block_ctx = ctx.enter_context(nc.Block())

        @block_ctx.sync
        def _(sp):
            sp.dma_start(x_all[:, 0:4, :], T["x"][0].rearrange("(t p) d -> p t d", p=P)).then_inc(dma_in["x"], 16)
            sp.dma_start(cst[:, 0:NCONSTS - 512 - 16], T["consts"][:, 0:520]).then_inc(dma_in["small"], 16)
            sp.dma_start(work[:, 20000:20528], T["consts"][:, 520:1048]).then_inc(dma_in["small"], 16)
            sp.dma_start(cols[:, :], T["cols"]).then_inc(dma_in["small"], 16)
            for i, n in enumerate(("L0_attn_Wq", "L0_attn_Wk", "L0_attn_Wv")):
                sp.dma_start(W0[:, i * 1024:(i + 1) * 1024], T[n]).then_inc(dma_in["A"], 16)
            for b in range(1, NB):
                sp.dma_start(x_all[:, 4 * b:4 * b + 4, :], T["x"][b].rearrange("(t p) d -> p t d", p=P))\
                    .then_inc(dma_in["x"], 16)
            sp.dma_start(v3(woA, 8), T["L0_attn_Wo"].rearrange("(n p) d -> p n d", p=P)).then_inc(dma_in["A"], 16)
            sp.dma_start(rows[:, :], T["rows"].partition_broadcast(P)).then_inc(dma_in["small"], 16)
            sp.dma_start(rw[:, :], T["narrow"]).then_inc(dma_in["small"], 16)
            sp.dma_start(b2[:, 0, :], T["L0_ffn_b2"]).then_inc(dma_in["small"], 16)
            sp.dma_start(b2[:, 1, :], T["L1_ffn_b2"]).then_inc(dma_in["small"], 16)
            sp.dma_start(ctxT[:, :], T["ctxT"]).then_inc(dma_in["B"], 16)
            for i, n in enumerate(("L0_xattn_Wq", "L0_xattn_Wk", "L0_xattn_Wv")):
                sp.dma_start(W1[:, i * 1024:(i + 1) * 1024], T[n]).then_inc(dma_in["B"], 16)
            sp.dma_start(v3(woB, 8), T["L0_xattn_Wo"].rearrange("(n p) d -> p n d", p=P)).then_inc(dma_in["B"], 16)
            sp.wait_ge(y_ready, 4)
            sp.dma_start(w1C, T["w1T"]).then_inc(dma_in["C"], 16)
            sp.dma_start(w2C.rearrange("p (e d) -> p e d", d=D), T["w2T"].rearrange("(e p) d -> p e d", p=P))\
                .then_inc(dma_in["C"], 16)
            sp.wait_ge(y_ready, 8)
            for i, n in enumerate(("L1_attn_Wq", "L1_attn_Wk", "L1_attn_Wv", "L1_attn_Wg")):
                sp.dma_start(W1[:, i * 1024:(i + 1) * 1024], T[n]).then_inc(dma_in["D"], 16)
            sp.dma_start(v3(woD, 8), T["L1_attn_Wo"].rearrange("(n p) d -> p n d", p=P)).then_inc(dma_in["D"], 16)
            sp.wait_ge(y_ready, 12)
            for i, n in enumerate(("L1_xattn_Wq", "L1_xattn_Wk", "L1_xattn_Wv")):
                sp.dma_start(W0[:, i * 512:(i + 1) * 512], T[n]).then_inc(dma_in["E"], 16)
            sp.dma_start(v3(woE, 4), T["L1_xattn_Wo"].rearrange("(n p) d -> p n d", p=P)).then_inc(dma_in["E"], 16)
            sp.wait_ge(y_ready, 16)
            sp.dma_start(w1F.rearrange("p (e h) -> p e h", e=E), T["L1_ffn_W1"].rearrange("e d h -> d e h"))\
                .then_inc(dma_in["F"], 16)
            sp.dma_start(w2F.rearrange("p (e d) -> p e d", d=D),
                         T["L1_ffn_W2"].rearrange("e (t p) d -> p (e t) d", p=P)).then_inc(dma_in["F"], 16)
            for b in range(NB):
                sp.wait_ge(x_ready, PF + b + 1)
                sp.dma_start(T["out"][b].rearrange("(t p) d -> p t d", p=P), x_all[:, 4 * b:4 * b + 4, :])\
                    .then_inc(dma_in["out"], 16)
            sp.wait_ge(dma_in["out"], 16 * NB)

        @block_ctx.tensor
        def _(pe):
            mm = nc.tensor.matmul

            def tail(w, s, last=False):
                ph = w // NB
                at = tail_steps(w)
                if s == at[0] and ph in (0, 1, 3, 4):
                    n = 4 if ph == 4 else 8
                    pe.wait_ge(sem({0: "a_o", 1: "B_o", 3: "d_og", 4: "E_o"}[ph]), n * (w % NB + 1))
                    out = take_next(pe, ("y", w), yT_ready, w + 1)
                    for p in range(n):
                        m = mm(out[:, :], out_w(ph)[:, p * P:(p + 1) * P], o_slot(w, p), start=(p == 0), stop=(p == n - 1))
                    m.then_inc(y_ready, 1)
                if s == at[1]:
                    pe.wait_ge(yT_ready, w + 1)
                    out = take_next(pe, ("yt", w), sem("sum_done"), w + 1)
                    for t in range(NT):
                        m = nc.tensor.transpose(out[:, t * P:(t + 1) * P], yT[:, t * P:(t + 1) * P], ident)
                    m.then_inc(yt_ready, 1)
                if s == at[4] and w < PF:
                    pe.wait_ge(x_ready, w + 1)
                    out = take_next(pe, ("xT", w), xT_ready, w + 1)
                    b = w % NB
                    for t in range(NT):
                        m = nc.tensor.transpose(out[:, t * P:(t + 1) * P], x_all[:, 4 * b + t, :], ident)
                    m.then_inc(xTp_ready, 1)

            def a_norm_T(b):
                pe.wait_ge(sem("a_xn"), b + 1)
                out = take_next(pe, ("a_xn", b), sem("a_xnT"), b + 1)
                for t in range(NT):
                    m = nc.tensor.transpose(out[:, t * P:(t + 1) * P], v3(xn, NT)[:, t, :], ident)
                m.then_inc(sem("a_xnp"), 1)

            def a_v(b, i):
                t, hf = i // 2, i % 2
                if i == 0:
                    pe.wait_ge(sem("a_xnT"), b + 1)
                n = 8 * b + i
                out = take_next(pe, ("a_v", n), sem("a_vs"), n + 1)
                mm(out[:, :], xnT[b % 2][:, t * P:(t + 1) * P], wvA[:, hf * S:(hf + 1) * S], start=True, stop=True)\
                    .then_inc(sem("a_vp"), 1)

            def a_qk(g, w, ready, done):
                b, p = g // 8, g % 8
                pe.wait_ge(sem("a_xnT"), b + 1)
                out = take_next(pe, (ready, g), sem(done), g + 1)
                mm(out[:, :], w[:, p * P:(p + 1) * P], xnT[b % 2], start=True, stop=True).then_inc(sem(ready), 1)

            def a_scores(u):
                g, hh, t = u // 8, (u // 4) % 2, u % 4
                if u % 8 == 0:
                    pe.wait_ge(sem("a_qs"), g + 1)
                    pe.wait_ge(sem("a_ks"), g + 1)
                out = take(pe, u % 3, sem("a_e"), u + 1)
                mm(out[:, :], qTA[g % 2][:, t * P:(t + 1) * P], kzA[g % 2][:, hh * S:(hh + 1) * S], start=True, stop=True)\
                    .then_inc(sem("a_s"), 1)

            def a_turn(u):
                pe.wait_ge(sem("a_n"), u + 1)
                out = take(pe, 3 + u % 2, sem("a_pt"), u + 1)
                for k in range(NT):
                    m = nc.tensor.transpose(out[:, k * P:(k + 1) * P], pA[u % 3][:, k * P:(k + 1) * P], ident)
                m.then_inc(sem("a_t"), 1)

            def a_out(g, k):
                b, p = g // 8, g % 8
                if k == 0:
                    pe.wait_ge(sem("a_pt"), 8 * g + 8)
                    pe.wait_ge(sem("a_vs"), 8 * b + 8)
                    take(pe, 5, sem("a_o"), g + 1)
                for hh in range(2):
                    m = mm(bank[5][hh * DH:(hh + 1) * DH, :], v3(vA[b % 2], NT)[:, k, (2 * p + hh) * DH:(2 * p + hh + 1) * DH],
                           v3(ptA[(2 * g + hh) % 4], NT)[:, k, :], start=(k == 0), stop=(k == NT - 1))
                if k == NT - 1:
                    m.then_inc(sem("a_pv"), 1)

            loaded(pe, "small", 7)
            loaded(pe, "A", 4)
            a_norm_T(0)
            for i in range(8):
                a_v(0, i)
            a_qk(0, wqA, "a_qp", "a_qs")
            a_qk(0, wkA, "a_kp", "a_ks")
            NU = NB * UNITS
            for u in range(NU + 8):
                b, s, g, j = u // UNITS, u % UNITS, u // 8, u % 8
                if u < NU:
                    if b:
                        tail(b - 1, s)
                    if s == 24 and b + 1 < NB:
                        a_norm_T(b + 1)
                    if j == 0 and g + 1 < 32:
                        a_qk(g + 1, wqA, "a_qp", "a_qs")
                    if j == 1 and g + 1 < 32:
                        a_qk(g + 1, wkA, "a_kp", "a_ks")
                    if 32 <= s < 48 and s % 2 and b + 1 < NB:
                        a_v(b + 1, (s - 32) // 2)
                    a_scores(u)
                if 2 <= u < NU + 2:
                    a_turn(u - 2)
                if 3 <= j <= 6 and g >= 1:
                    a_out(g - 1, j - 3)

            def cross_kv(c):
                n = c["n"]
                for p in range(c["np"]):
                    out = take_next(pe, (n + "k", p), sem(n + "_ks"), p + 1)
                    mm(out[:, 0:NB * C], c["wk"][:, p * P:(p + 1) * P], ctxT[:, :], start=True, stop=True)\
                        .then_inc(sem(n + "_kp"), 1)
                nh = c["np"] * P // S
                for i in range(NB * nh):
                    b, hf = i // nh, i % nh
                    out = take_next(pe, (n + "v", i), sem(n + "_vs"), i + 1)
                    mm(out[0:C, :], ctxT[:, b * C:(b + 1) * C], c["wv"][:, hf * S:(hf + 1) * S], start=True, stop=True)\
                        .then_inc(sem(n + "_vp"), 1)

            def cross_q(c, b):
                n, np_ = c["n"], c["np"]
                pe.wait_ge(xT_ready, c["w0"] - NB + b + 1)
                for p in range(np_):
                    k = np_ * b + p
                    out = take_next(pe, (n + "q", k), sem(n + "_qs"), k + 1)
                    mm(out[:, :], c["wq"][:, p * P:(p + 1) * P], xT_all[:, b, :], start=True, stop=True)\
                        .then_inc(sem(n + "_qp"), 1)

            def cross_scores(c, b, t):
                n, np_ = c["n"], c["np"]
                if t == 0:
                    pe.wait_ge(sem(n + "_qs"), np_ * (b + 1))
                    if b == 0:
                        pe.wait_ge(sem(n + "_ks"), np_)
                u = NT * b + t
                for p in range(np_):
                    if p % 3 == 0:
                        out = take(pe, p // 3, sem(n + "_sub"), u + 1)
                    kd = kdB[:, (p * NB + b) * 2 * C:(p * NB + b + 1) * 2 * C]
                    m = mm(out[:, (p % 3) * 2 * C:(p % 3 + 1) * 2 * C],
                           v3(qTB, NPAIR)[:, p, t * P:(t + 1) * P], kd, start=True, stop=True)
                m.then_inc(sem(n + "_s"), 1)

            def cross_turn(c, b, t):
                n, np_ = c["n"], c["np"]
                u = NT * b + t
                nq = np_ * 2 // 4
                pe.wait_ge(sem(n + "_n"), u + 1)
                for q in range(nq):
                    k = nq * u + q
                    out = take(pe, 3 + k % 2, sem(n + "_pt"), k + 1)
                    for i in range(4):
                        m = nc.tensor.transpose(out[:, i * P:(i + 1) * P], v3(pB[t % 2], H)[:, 4 * q + i, :], ident)
                    m.then_inc(sem(n + "_t"), 1)

            def cross_out(c, b):
                n, np_ = c["n"], c["np"]
                nq = np_ * 2 // 4
                pe.wait_ge(sem(n + "_pt"), nq * NT * (b + 1))
                if b == 0:
                    pe.wait_ge(sem(n + "_vs"), NB * np_ * P // S)
                for p in range(np_):
                    k = np_ * b + p
                    out = take_next(pe, (n + "o", k), sem(n + "_o"), k + 1)
                    for hh in range(2):
                        h = 2 * p + hh
                        m = mm(out[hh * DH:(hh + 1) * DH, :], v3(vcB, NB)[:, b, h * DH:(h + 1) * DH],
                               v3(ptB, H)[:, h, :], start=True, stop=True)
                    m.then_inc(sem(n + "_pv"), 1)

            def cross(ph):
                c = CROSS[ph]
                loaded(pe, c["n"], DMA_COUNT[c["n"]])
                cross_kv(c)
                cross_q(c, 0)
                for b in range(NB):
                    w = c["w0"] + b
                    for s in range(10):
                        tail(w - 1, s)
                        if s in (0, 1, 3, 5):
                            cross_scores(c, b, (0, 1, None, 2, None, 3)[s])
                        if s in (2, 4, 6, 8):
                            cross_turn(c, b, s // 2 - 1)
                        if s == 7 and b + 1 < NB:
                            cross_q(c, b + 1)
                        if s == 9:
                            cross_out(c, b)

            def moe_logits(m_, b):
                n, r = m_["n"], m_["r"]
                pe.wait_ge(xT_ready, m_["w0"] - NB + b + 1)
                out = take_next(pe, (n + "lg", b), sem(n + "_lg"), b + 1)
                for t in range(NT):
                    m = mm(out[:, t * E:(t + 1) * E], xT_all[:, b, t * P:(t + 1) * P], rw[:, r * E:(r + 1) * E],
                           start=True, stop=True)
                m.then_inc(sem(n + "_lgp"), 1)

            def moe_wT(m_, b):
                n = m_["n"]
                pe.wait_ge(sem(n + "_wt"), b + 1)
                out = take_next(pe, (n + "wT", b), sem(n + "_sel"), b + 1)
                for t in range(NT):
                    m = nc.tensor.transpose(out[0:E, t * P:(t + 1) * P], rt[:, 11, t, :], ident)
                m.then_inc(sem(n + "_wTp"), 1)

            def moe(ph):
                m_ = MOE[ph]
                n, ft, r = m_["n"], m_["ft"], m_["r"]
                steps = E * ft
                loaded(pe, n, DMA_COUNT[n])
                moe_logits(m_, 0)
                moe_wT(m_, 0)

                def contract(i):
                    b, k = i // steps, i % steps
                    if k == 0:
                        take(pe, 5, yT_ready, m_["w0"] + b + 1)
                        mm(bank[5][:, :], b2[:, r, :], wT_C[0:E, (b % 2) * S:(b % 2 + 1) * S], start=True, stop=False)
                    pe.wait_ge(sem(n + "_hw"), i + 1)
                    m = mm(bank[5][:, :], m_["w2"][:, k * D:(k + 1) * D], hwC[i % 3], start=False, stop=(k == steps - 1))
                    if k == steps - 1:
                        m.then_inc(y_ready, 1)
                    else:
                        m.then_inc(sem(n + "_c"), 1)

                for i in range(NB * steps + 2):
                    b, s = i // steps, i % steps
                    if b < NB:
                        tail(m_["w0"] + b - 1, s)
                        if b + 1 < NB and s == 12:
                            moe_logits(m_, b + 1)
                        if b + 1 < NB and s == 15:
                            moe_wT(m_, b + 1)
                        if s % ft == 0:
                            e = s // ft
                            if s == 0:
                                pe.wait_ge(sem(n + "_sel"), b + 1)
                            out = take(pe, 3 + e % 2, sem(n + "_hw"), i + ft)
                            mm(out[:, :], sel[:, e:e + 1].to_broadcast([P, P]), wsel_b[b % 2], start=True, stop=True)\
                                .then_inc(sem(n + "_wb"), 1)
                        out = take(pe, i % 3, sem(n + "_h"), i + 1)
                        mm(out[:, :], m_["w1"][:, s * P:(s + 1) * P], xT_all[:, b, :], start=True, stop=True)\
                            .then_inc(sem(n + "_hp"), 1)
                    if i >= 2:
                        contract(i - 2)

            def d_alpha(b):
                pe.wait_ge(xT_ready, PC + b + 1)
                out = take_next(pe, ("d_al", b), sem("d_z"), b + 1)
                for t in range(NT):
                    m = mm(out[:, t * H:(t + 1) * H], xT_all[:, b, t * P:(t + 1) * P], rw[:, 16:32], start=True, stop=True)
                m.then_inc(sem("d_al"), 1)

            def d_sums(b):
                pe.wait_ge(sem("d_sp"), b + 1)
                out = take_next(pe, ("d_LT", b), sem("d_lsel"), b + 1)
                for t in range(NT):
                    m = mm(out[0:H, t * P:(t + 1) * P], v3(spD[3], NT)[:, t, :], upto, start=True, stop=True)
                m.then_inc(sem("d_LT"), 1)
                out = take_next(pe, ("d_lc", b), sem("d_lcs"), b + 1)
                mm(out[:, 0:64], upto, spD[3], start=True, stop=True)
                mm(out[:, 64:128], after, spD[3], start=True, stop=True).then_inc(sem("d_lcp"), 1)

            def d_v(b, hf, t):
                n = 8 * b + 4 * hf + t
                if n >= 8 and t == 0:
                    pe.wait_ge(sem("d_pv"), 8 * b - 8 + 4 * hf + 4)
                out = take_next(pe, ("d_v", n), sem("d_vs"), n + 1)
                mm(out[:, :], xT_all[:, b, t * P:(t + 1) * P], wvD[:, hf * S:(hf + 1) * S], start=True, stop=True)\
                    .then_inc(sem("d_vp"), 1)

            def d_decays(g):
                b, p = g // 8, g % 8
                if p == 0:
                    pe.wait_ge(sem("d_lsel"), b + 1)
                out = take(pe, 0, sem("d_el"), g + 1)
                for hh in range(2):
                    m = mm(out[hh * DH:(hh + 1) * DH, :], sel[:, 2 * p + hh:2 * p + hh + 1].to_broadcast([P, DH]),
                           lsel_b[b % 2], start=True, stop=True)
                m.then_inc(sem("d_lp"), 1)
                for hh in range(2):
                    out = take(pe, 1, sem("d_arg"), 2 * g + hh + 1)
                    mm(out[:, :], sel[:, 2 * p + hh:2 * p + hh + 1].to_broadcast([P, P]), lsel_b[b % 2],
                       start=True, stop=False)
                    mm(out[:, :], ident_b[:, :], mask[:, :], start=False, stop=True).then_inc(sem("d_la"), 1)

            def d_proj(g, i):
                b, p = g // 8, g % 8
                w = (wqD, wkD, wgD)[i]
                k = 3 * g + i
                out = take_next(pe, ("d_p", k), sem("d_th") if i == 2 else sem("d_silu"), g + 1 if i == 2 else 2 * g + i + 1)
                mm(out[:, :], w[:, p * P:(p + 1) * P], xT_all[:, b, :], start=True, stop=True).then_inc(sem("d_pp"), 1)

            def d_scores(g):
                pe.wait_ge(sem("d_qb"), 2 * g + 2)
                for c2 in range(2):
                    out = take(pe, 2 + c2, sem("d_at"), 2 * g + c2 + 1)
                    for c in (2 * c2, 2 * c2 + 1):
                        m = mm(out[:, (c % 2) * 256:(c % 2 + 1) * 256], kTD[g % 2][:, c * P:(c + 1) * P],
                               qbD[g % 2][:, c * 256:(c + 1) * 256], start=True, stop=True)
                    m.then_inc(sem("d_s"), 1)

            def d_kturn(g):
                pe.wait_ge(sem("d_silu"), 2 * g + 2)
                out = take(pe, 4, sem("d_kd"), g + 1)
                for c in range(NT):
                    m = nc.tensor.transpose(out[:, c * P:(c + 1) * P], kTD[g % 2][:, c * P:(c + 1) * P], ident)
                m.then_inc(sem("d_kt"), 1)

            def d_state(g):
                b, p = g // 8, g % 8
                pe.wait_ge(sem("d_kd"), g + 1)
                pe.wait_ge(sem("d_vs"), 8 * b + 4 * (p // 4) + 4)
                out = take(pe, 4, sem("d_st"), g + 1)
                for c in range(NT - 1):
                    m = mm(out[:, c * P:(c + 1) * P], kdD[g % 2][:, c * P:(c + 1) * P],
                           v3(vD[p // 4], NT)[:, c, (p % 4) * P:(p % 4 + 1) * P], start=True, stop=True)
                m.then_inc(sem("d_dl"), 1)

            def d_out(g):
                p = g % 8
                pe.wait_ge(sem("d_at"), 2 * g + 2)
                pe.wait_ge(sem("d_st"), g + 1)
                pe.wait_ge(sem("d_qe"), g + 1)
                out = take(pe, 5, sem("d_o"), g + 1)
                for c in range(NT):
                    if c:
                        mm(out[:, c * P:(c + 1) * P], stD[g % 2][:, (c - 1) * P:c * P], qeD[g % 2][:, c * P:(c + 1) * P],
                           start=True, stop=False, skip_group_check=True)
                    for hh in range(2):
                        at = c * 256 + hh * P
                        m = mm(out[hh * DH:(hh + 1) * DH, c * P:(c + 1) * P],
                               v3(vD[p // 4], NT)[:, c, (p % 4) * P + hh * DH:(p % 4) * P + (hh + 1) * DH],
                               atD[g % 2][:, at:at + P], start=(c == 0), stop=True, skip_group_check=True)
                m.then_inc(sem("d_pv"), 1)

            def d_mean(b, i):
                pe.wait_ge(sem("d_gs"), 2 * b + i + 1)
                out = take_next(pe, ("d_gn", 2 * b + i), sem("d_gr"), 2 * b + i + 1)
                src = gnD[0][:, 8 * (b % 2):8 * (b % 2) + 8] if i == 0 else gnD[2][:, 0:8]
                mm(out[:, 0:8], block, src, start=True, stop=True).then_inc(sem("d_gp"), 1)

            def phase_d():
                loaded(pe, "D", DMA_COUNT["D"])
                d_alpha(0)
                for t in range(NT):
                    d_v(0, 0, t)
                d_sums(0)
                for t in range(NT):
                    d_v(0, 1, t)
                d_decays(0)
                for i in range(3):
                    d_proj(0, i)
                for g in range(33):
                    b, s = g // 8, g % 8
                    if g < 32:
                        if g + 1 < 32:
                            d_decays(g + 1)
                            if (g + 1) % 8 == 0:
                                pe.wait_ge(xT_ready, PC + (g + 1) // 8 + 1)
                            d_proj(g + 1, 0)
                            d_proj(g + 1, 1)
                        d_scores(g)
                        if g + 1 < 32:
                            d_proj(g + 1, 2)
                        d_kturn(g)
                    if g >= 1:
                        d_out(g - 1)
                    if g < 32:
                        d_state(g)
                        tail(PD + b - 1, s)
                        if b and s in (1, 2):
                            d_mean(b - 1, s - 1)
                        if b and s in (1, 2):
                            d_v(b, 1, 2 * s - 2)
                            d_v(b, 1, 2 * s - 1)
                        if b + 1 < NB:
                            if s == 2:
                                d_alpha(b + 1)
                            if s == 4:
                                d_sums(b + 1)
                            if s in (5, 6):
                                d_v(b + 1, 0, 2 * s - 10)
                                d_v(b + 1, 0, 2 * s - 9)
                d_mean(3, 0)
                d_mean(3, 1)

            cross(1)
            moe(2)
            phase_d()
            cross(4)
            moe(5)
            for s in range(32):
                tail(WORKS - 1, s)

        @block_ctx.scalar
        def _(act):
            A = nc.scalar.activation
            ln_no = [0]
            chain = [0]

            def link(ins):
                chain[0] += 1
                ins.then_inc(act_chain, 1)
                act.wait_ge(act_chain, chain[0])

            def rsqrt():
                n = ln_no[0]
                ln_no[0] += 1
                act.wait_ge(ln_var, n + 1)
                link(A(lnv[:, 1, :], lnv[:, 0, :], ACT.Ln))
                A(lnv[:, 2, :], lnv[:, 1, :], ACT.Exp, scale=-0.5).then_inc(ln_rsqrt, 1)

            def tail(w, s):
                ph, b = w // NB, w % NB
                at = tail_steps(w)
                if s == at[0]:
                    act.wait_ge(y_ready, w + 1)
                    if w:
                        act.wait_ge(yt_ready, w)
                    src = bank[5] if ph in (2, 5) else where["y", w]
                    if ph in (1, 4):
                        A(yT[:, :], src[:, :], ACT.Identity, bias=col("bo0" if ph == 1 else "bo1")).then_inc(yT_ready, 1)
                    else:
                        A(yT[:, :], src[:, :], ACT.Copy).then_inc(yT_ready, 1)
                if s == at[1]:
                    rsqrt()
                if s == at[2] and ph == 1:
                    rsqrt()
                if s == at[4] and w < PF:
                    act.wait_ge(xTp_ready, w + 1)
                    A(xT_all[:, b, :], where["xT", w][:, :], ACT.Copy).then_inc(xT_ready, 1)

            def a_norm_T(b):
                act.wait_ge(sem("a_xnp"), b + 1)
                if b >= 2:
                    act.wait_ge(sem("a_kp"), 8 * (b - 1))
                    act.wait_ge(sem("a_vp"), 8 * (b - 1))
                A(xnT[b % 2], where["a_xn", b][:, :], ACT.Identity, bias=col("ln_b"), scale=col("ln_g"))\
                    .then_inc(sem("a_xnT"), 1)

            def a_v(b, i):
                n = 8 * b + i
                act.wait_ge(sem("a_vp"), n + 1)
                if b >= 2 and i == 0:
                    act.wait_ge(sem("a_pv"), 8 * (b - 1))
                A(v3(vA[b % 2], NT)[:, i // 2, (i % 2) * S:(i % 2 + 1) * S], where["a_v", n][:, :], ACT.Copy)\
                    .then_inc(sem("a_vs"), 1)

            def a_q(g):
                act.wait_ge(sem("a_qp"), g + 1)
                if g >= 2:
                    act.wait_ge(sem("a_s"), 8 * (g - 1))
                A(qTA[g % 2], where["a_qp", g][:, :], ACT.Copy, scale=0.125).then_inc(sem("a_qs"), 1)

            def a_exp(u):
                act.wait_ge(sem("a_mx"), u + 1)
                if u >= 3:
                    act.wait_ge(sem("a_t"), u - 2)
                A(pA[u % 3], bank[u % 3][:, :], ACT.Exp, bias=nmax[:, u % 8:u % 8 + 1],
                  accum_out=rsum[0][:, u % 8:u % 8 + 1]).then_inc(sem("a_e"), 1)

            def a_pt(u):
                h = u // 4
                act.wait_ge(sem("a_t"), u + 1)
                if u >= 16 and u % 8 == 0:
                    act.wait_ge(sem("a_pv"), u // 8 - 1)
                A(v3(ptA[h % 4], NT)[:, :, (u % 4) * P:(u % 4 + 1) * P], v3(bank[3 + u % 2][:, :], NT), ACT.Copy)\
                    .then_inc(sem("a_pt"), 1)

            loaded(act, "small", 7)
            rsqrt()
            a_norm_T(0)
            for i in range(8):
                a_v(0, i)
            a_q(0)
            NU = NB * UNITS
            for u in range(NU + 2):
                b, s, g, j = u // UNITS, u % UNITS, u // 8, u % 8
                if u < NU:
                    if b:
                        tail(b - 1, s)
                    if s == 22 and b + 1 < NB:
                        rsqrt()
                    if s == 24 and b + 1 < NB:
                        a_norm_T(b + 1)
                    if 32 <= s < 48 and s % 2 and b + 1 < NB:
                        a_v(b + 1, (s - 32) // 2)
                    if j == 0 and g + 1 < 32:
                        a_q(g + 1)
                    a_exp(u)
                if u >= 2:
                    a_pt(u - 2)

            def cross_v(c):
                n = c["n"]
                nh = c["np"] * P // S
                act.wait_ge(sem(n + "_zero"), 1)
                for i in range(NB * nh):
                    act.wait_ge(sem(n + "_vp"), i + 1)
                    b, hf = i // nh, i % nh
                    A(v3(vcB, NB)[0:C, b, hf * S:(hf + 1) * S], where[n + "v", i][0:C, :], ACT.Copy)\
                        .then_inc(sem(n + "_vs"), 1)

            def cross_q(c, b):
                n, np_ = c["n"], c["np"]
                if b:
                    act.wait_ge(sem(n + "_s"), NT * b)
                for p in range(np_):
                    k = np_ * b + p
                    act.wait_ge(sem(n + "_qp"), k + 1)
                    src = where[n + "q", k][:, :]
                    if c["bias"]:
                        i = A(v3(qTB, NPAIR)[:, p, :], src, ACT.Identity, bias=col("bq", p))
                    else:
                        i = A(v3(qTB, NPAIR)[:, p, :], src, ACT.Copy)
                    i.then_inc(sem(n + "_qs"), 1)

            def cross_exp(c, b, t):
                n = c["n"]
                u = NT * b + t
                hs = 2 * c["np"]
                act.wait_ge(sem(n + "_sub"), u + 1)
                p = v3(pB[t % 2], H)[:, 0:hs, 0:C]
                A(p, p, ACT.Exp, scale=0.125).then_inc(sem(n + "_e"), 1)

            def cross_pt(c, b, t):
                n = c["n"]
                nq = c["np"] * 2 // 4
                u = NT * b + t
                if t == 0 and b:
                    act.wait_ge(sem(n + "_pv"), c["np"] * b)
                for q in range(nq):
                    k = nq * u + q
                    act.wait_ge(sem(n + "_t"), k + 1)
                    A(v3(ptB, H)[:, 4 * q:4 * q + 4, t * P:(t + 1) * P], v3(bank[3 + k % 2][:, :], NT), ACT.Copy)\
                        .then_inc(sem(n + "_pt"), 1)

            def cross(ph):
                c = CROSS[ph]
                enter(act, ph)
                cross_v(c)
                cross_q(c, 0)
                for b in range(NB):
                    for s in range(10):
                        tail(c["w0"] + b - 1, s)
                        if s in (0, 1, 3, 5):
                            cross_exp(c, b, (0, 1, None, 2, None, 3)[s])
                        if s in (2, 4, 6, 8):
                            cross_pt(c, b, s // 2 - 1)
                        if s == 7 and b + 1 < NB:
                            cross_q(c, b + 1)

            def moe_exp(m_, b):
                n = m_["n"]
                act.wait_ge(sem(n + "_d"), b + 1)
                if n == "C":
                    A(lnv[:, 4, :], lnv[:, 3, :], ACT.Exp).then_inc(sem(n + "_e"), 1)
                else:
                    A(rt[:, 2, :, :], rt[:, 1, :, :], ACT.Exp).then_inc(sem(n + "_e"), 1)

            def moe(ph):
                m_ = MOE[ph]
                n, ft = m_["n"], m_["ft"]
                steps = E * ft
                enter(act, ph)
                moe_exp(m_, 0)
                for i in range(NB * steps):
                    b, s = i // steps, i % steps
                    tail(m_["w0"] + b - 1, s)
                    if s == 13 and b + 1 < NB:
                        moe_exp(m_, b + 1)
                    act.wait_ge(sem(n + "_hp"), i + 1)
                    if i >= 3:
                        act.wait_ge(sem(n + "_hw"), i - 2)
                    A(hsC[i % 3], bank[i % 3][:, :], m_["func"], bias=col(m_["b1"], s)).then_inc(sem(n + "_h"), 1)

            def d_softplus(b):
                act.wait_ge(sem("d_az"), b + 1)
                link(A(spD[2], spD[1], ACT.Exp, scale=-1.0))
                A(spD[2], spD[2], ACT.Ln, bias=1.0).then_inc(sem("d_ln"), 1)

            def d_kdec(b):
                act.wait_ge(sem("d_lcs"), b + 1)
                if b >= 2:
                    act.wait_ge(sem("d_kd"), 8 * (b - 1))
                A(kdecD[b % 2], lcD[b % 2][:, 64:128], ACT.Exp, scale=-1.0).then_inc(sem("d_kdec"), 1)

            def d_v(b, hf, t):
                n = 8 * b + 4 * hf + t
                act.wait_ge(sem("d_vp"), n + 1)
                A(v3(vD[hf], NT)[:, t, :], where["d_v", n][:, :], ACT.Copy).then_inc(sem("d_vs"), 1)

            def d_el(g):
                act.wait_ge(sem("d_lp"), g + 1)
                if g >= 2:
                    act.wait_ge(sem("d_st"), g - 1)
                    act.wait_ge(sem("d_qe"), g - 1)
                A(elD[g % 2], bank[0][:, :], ACT.Exp, scale=-1.0).then_inc(sem("d_el"), 1)

            def d_dm(g):
                act.wait_ge(sem("d_arg"), 2 * g + 2)
                A(dmD[g % 2], dmD[g % 2], ACT.Exp).then_inc(sem("d_dm"), 1)

            def d_tanh(g, i):
                act.wait_ge(sem("d_pp"), 3 * g + i + 1)
                src = where["d_p", 3 * g + i][:, :]
                if i < 2:
                    if g:
                        act.wait_ge(sem("d_silu"), 2 * g - 1 + i)
                    A(tqD[i], src, ACT.Tanh, scale=0.5).then_inc(sem("d_tq"), 1)
                else:
                    if g >= 12:
                        act.wait_ge(sem("d_og"), g - 11)
                    A(thD[g % 12], src, ACT.Tanh, scale=0.5).then_inc(sem("d_th"), 1)

            def d_o(g):
                act.wait_ge(sem("d_pv"), g + 1)
                act.wait_ge(sem("d_bs"), g + 1)
                s = g % 12
                if g >= 12:
                    act.wait_ge(y_ready, PD + (g - 12) // 8 + 1)
                elif g == 0:
                    act.wait_ge(y_ready, PB + 4)
                A(OT[:, s, :] if s < 8 else oxD[s - 8], bank[5][:, :], ACT.Copy).then_inc(sem("d_o"), 1)

            def d_gn(b):
                act.wait_ge(sem("d_gr"), 2 * b + 2)
                link(A(gnD[4][:, 0:8], gnD[3][:, 0:8], ACT.Ln))
                A(gnD[5][:, 0:8], gnD[4][:, 0:8], ACT.Exp, scale=-0.5).then_inc(sem("d_g0"), 1)

            def phase_d():
                enter(act, 3)
                d_softplus(0)
                for t in range(NT):
                    d_v(0, 0, t)
                d_kdec(0)
                for t in range(NT):
                    d_v(0, 1, t)
                d_el(0)
                for i in range(3):
                    d_tanh(0, i)
                d_dm(0)
                for g in range(33):
                    b, s = g // 8, g % 8
                    if g + 1 < 32:
                        d_el(g + 1)
                        d_tanh(g + 1, 0)
                        d_tanh(g + 1, 1)
                        d_tanh(g + 1, 2)
                    if g >= 1:
                        d_o(g - 1)
                    if g + 1 < 32:
                        d_dm(g + 1)
                    if g < 32:
                        tail(PD + b - 1, s)
                        if b and s == 2:
                            d_gn(b - 1)
                        if b and s in (1, 2):
                            d_v(b, 1, 2 * s - 2)
                            d_v(b, 1, 2 * s - 1)
                        if b + 1 < NB:
                            if s == 2:
                                d_softplus(b + 1)
                            if s == 4:
                                d_kdec(b + 1)
                            if s in (5, 6):
                                d_v(b + 1, 0, 2 * s - 10)
                                d_v(b + 1, 0, 2 * s - 9)
                d_gn(3)

            cross(1)
            moe(2)
            phase_d()
            cross(4)
            moe(5)
            for s in range(32):
                tail(WORKS - 1, s)

        @block_ctx.vector
        def _(dve):
            V = nc.vector
            ln_no = [0]
            chain = [0]

            def link(ins):
                chain[0] += 1
                ins.then_inc(dve_chain, 1)
                dve.wait_ge(dve_chain, chain[0])

            def ln_stats(src):
                for t in range(NT):
                    i = V.bn_stats(bn[:, t, :], src[:, t, :])
                link(i)
                for t in range(NT):
                    i = V.bn_aggr(mv[:, t, :], bn[:, t, :])
                link(i)
                V.tensor_scalar(lnv[:, 0, :], mv[:, :, 1], EPS, None, ALU.add).then_inc(ln_var, 1)

            def newton(var, y0, tmp, out):
                link(V.tensor_tensor(tmp, y0, y0, ALU.mult))
                link(V.scalar_tensor_tensor(out=tmp, in0=tmp, scalar=-0.5, in1=var, op0=ALU.mult, op1=ALU.mult))
                link(V.scalar_tensor_tensor(out=out, in0=tmp, scalar=1.5, in1=y0, op0=ALU.add, op1=ALU.mult))

            def ln_apply(src, dst):
                n = ln_no[0]
                ln_no[0] += 1
                dve.wait_ge(ln_rsqrt, n + 1)
                newton(lnv[:, 0, :], lnv[:, 2, :], lnv[:, 5, :], lnv[:, 1, :])
                for t in range(NT):
                    i = V.tensor_scalar(dst[:, t, :], src[:, t, :], mv[:, t, 0:1], lnv[:, 1, t:t + 1],
                                        ALU.subtract, ALU.mult)
                return i

            def tail(w, s):
                ph, b = w // NB, w % NB
                at = tail_steps(w)
                x = x_all[:, 4 * b:4 * b + 4, :]
                if s == at[1]:
                    dve.wait_ge(yt_ready, w + 1)
                    V.tensor_tensor(res[:, :, :], x, v3(where["yt", w][:, :], NT), ALU.add).then_inc(sem("sum_done"), 1)
                    dve.wait_ge(sem("sum_done"), w + 1)
                    ln_stats(res)
                if ph == 1:
                    if s == at[2]:
                        link(ln_apply(res, res))
                        g, bb = (rows[:, ROWS[k][0]:ROWS[k][1]].unsqueeze(1).to_broadcast([P, NT, D]) for k in ("xg", "xb"))
                        link(V.tensor_tensor(res[:, :, :], res[:, :, :], g, ALU.mult))
                        link(V.tensor_tensor(res[:, :, :], res[:, :, :], bb, ALU.add))
                        link(V.tensor_tensor(res[:, :, :], res[:, :, :], x, ALU.add))
                        ln_stats(res)
                    if s == at[3]:
                        ln_apply(res, x).then_inc(x_ready, 1)
                elif s == at[2]:
                    ln_apply(res, x).then_inc(x_ready, 1)

            def split_rows(src, n, dst):
                link(V.tensor_copy(dst[0:n, :], src))
                link(V.tensor_tensor(spl_r[0:n, :], src, dst[0:n, :], ALU.subtract))
                link(V.tensor_copy(spl_m[0:n, :], spl_r[0:n, :]))
                V.tensor_copy(dst[32:32 + n, :], spl_m[0:n, :])
                return V.tensor_tensor(dst[64:64 + n, :], spl_r[0:n, :], spl_m[0:n, :], ALU.subtract)

            def a_k(g):
                dve.wait_ge(sem("a_kp"), g + 1)
                if g >= 2:
                    dve.wait_ge(sem("a_s"), 8 * (g - 1))
                src = where["a_kp", g]
                V.tensor_copy(kzA[g % 2][0:DH, 0:S], src[0:DH, :])
                V.tensor_copy(kzA[g % 2][DH:P, S:2 * S], src[DH:P, :]).then_inc(sem("a_ks"), 1)

            def a_max(u):
                dve.wait_ge(sem("a_s"), u + 1)
                if u >= 8:
                    dve.wait_ge(sem("a_e"), u - 7)
                V.tensor_reduce(nmax[:, u % 8:u % 8 + 1], bank[u % 3][:, :], AX, ALU.max, negate=True)\
                    .then_inc(sem("a_mx"), 1)

            def a_norm(u):
                r = slice(u % 8, u % 8 + 1)
                dve.wait_ge(sem("a_e"), u + 1)
                link(V.reciprocal(rsum[1][:, r], rsum[0][:, r]))
                V.tensor_scalar(pA[u % 3], pA[u % 3], rsum[1][:, r], None, ALU.mult).then_inc(sem("a_n"), 1)

            def a_o(g):
                b = g // 8
                dve.wait_ge(sem("a_pv"), g + 1)
                if b and g % 8 == 0:
                    dve.wait_ge(y_ready, b)
                V.tensor_copy(OT[:, g % 8, :], bank[5][:, :]).then_inc(sem("a_o"), 1)

            loaded(dve, "small", 7)
            V.tensor_copy(ident_b[:, :], ident)
            V.tensor_copy(sel[:, :], work[:, 20000:20016])
            V.tensor_copy(mask[:, :], work[:, 20016:20528]).then_inc(consts_ready, 1)
            loaded(dve, "x", 4)
            ln_stats(x_all[:, 0:4, :])
            ln_apply(x_all[:, 0:4, :], v3(xn, NT)).then_inc(sem("a_xn"), 1)
            dve.wait_ge(sem("a_zero"), 1)
            a_k(0)
            NU = NB * UNITS
            for u in range(NU + 8):
                b, s, g, j = u // UNITS, u % UNITS, u // 8, u % 8
                if u < NU:
                    if b:
                        tail(b - 1, s)
                    if b + 1 < NB and s == 22:
                        ln_stats(x_all[:, 4 * b + 4:4 * b + 8, :])
                    if b + 1 < NB and s == 23:
                        dve.wait_ge(sem("a_xnp"), b + 1)
                        ln_apply(x_all[:, 4 * b + 4:4 * b + 8, :], v3(xn, NT)).then_inc(sem("a_xn"), 1)
                    if j == 1 and g + 1 < 32:
                        a_k(g + 1)
                    a_max(u)
                if 1 <= u < NU + 1:
                    a_norm(u - 1)
                if j == 7 and g >= 1:
                    a_o(g - 1)

            def cross_k(c):
                n = c["n"]
                dve.wait_ge(sem(n + "_zero"), 1)
                kd = kdB.rearrange("p (q b h c) -> p q b h c", q=NPAIR, b=NB, h=2)
                for p in range(c["np"]):
                    dve.wait_ge(sem(n + "_kp"), p + 1)
                    src = where[n + "k", p]
                    for hh in range(2):
                        r = slice(hh * DH, (hh + 1) * DH)
                        s_ = src[r, 0:NB * C].rearrange("p (b c) -> p b c", b=NB)
                        if c["bias"]:
                            i = V.tensor_scalar(kd[r, p, :, hh, :], s_, col("bk", p)[r, :], None, ALU.add)
                        else:
                            i = V.tensor_copy(kd[r, p, :, hh, :], s_)
                    i.then_inc(sem(n + "_ks"), 1)

            def cross_sub(c, b, t):
                n, np_ = c["n"], c["np"]
                u = NT * b + t
                dve.wait_ge(sem(n + "_s"), u + 1)
                m = statB[u % 2]
                parts = [(q, min(3, np_ - 3 * q)) for q in range((np_ + 2) // 3)]
                for q, k in parts:
                    i = V.tensor_reduce(m[:, 6 * q:6 * q + 2 * k], v3(bank[q][:, 0:2 * k * C], 2 * k), AX, ALU.max)
                link(i)
                if u >= 2:
                    dve.wait_ge(sem(n + "_t"), (np_ // 2) * (u - 1))
                for q, k in parts:
                    i = V.tensor_tensor(v3(pB[t % 2], H)[:, 6 * q:6 * q + 2 * k, 0:C], v3(bank[q][:, 0:2 * k * C], 2 * k),
                                        m[:, 6 * q:6 * q + 2 * k].unsqueeze(2).to_broadcast([P, 2 * k, C]), ALU.subtract)
                i.then_inc(sem(n + "_sub"), 1)

            def cross_norm(c, b, t):
                n, hs = c["n"], 2 * c["np"]
                u = NT * b + t
                dve.wait_ge(sem(n + "_e"), u + 1)
                p = v3(pB[t % 2], H)[:, 0:hs, 0:C]
                link(V.tensor_reduce(statB[2][:, 0:hs], p, AX, ALU.add))
                link(V.reciprocal(statB[3][:, 0:hs], statB[2][:, 0:hs]))
                V.tensor_tensor(p, p, statB[3][:, 0:hs].unsqueeze(2).to_broadcast([P, hs, C]), ALU.mult)\
                    .then_inc(sem(n + "_n"), 1)

            def cross_o(c, b):
                n, np_ = c["n"], c["np"]
                w = c["w0"] + b
                dve.wait_ge(y_ready, w)
                for p in range(np_):
                    k = np_ * b + p
                    dve.wait_ge(sem(n + "_pv"), k + 1)
                    src = where[n + "o", k][:, :]
                    if c["bias"]:
                        i = V.tensor_scalar(OT[:, p, :], src, col("bv", p), None, ALU.add)
                    else:
                        i = V.tensor_copy(OT[:, p, :], src)
                    i.then_inc(sem(n + "_o"), 1)

            def cross(ph):
                c = CROSS[ph]
                enter(dve, ph)
                cross_k(c)
                for b in range(NB):
                    for s in range(10):
                        tail(c["w0"] + b - 1, s)
                        if s in (0, 1, 3, 5):
                            cross_sub(c, b, (0, 1, None, 2, None, 3)[s])
                        if s in (1, 3, 5, 6):
                            cross_norm(c, b, {1: 0, 3: 1, 5: 2, 6: 3}[s])
                        if s == 9:
                            cross_o(c, b)

            def bc(ap):
                return ap.to_broadcast([P, 4, 8])

            def moe_route1(m_, b):
                n = m_["n"]
                dve.wait_ge(sem(n + "_lgp"), b + 1)
                lg = rt[:, 0, :, :]
                src = v3(where[n + "lg", b][:, 0:4 * E], 4)
                if n == "C":
                    V.tensor_copy(lg, src).then_inc(sem(n + "_lg"), 1)
                    dve.wait_ge(sem(n + "_lg"), b + 1)
                    for t in range(NT):
                        i = V.max(out=rt[:, 1, t, :], in_=rt[:, 0, t, :])
                    link(i)
                    V.tensor_tensor(lnv[:, 3, :], rt[:, 1, :, 1], rt[:, 1, :, 0], ALU.subtract).then_inc(sem(n + "_d"), 1)
                    for t in range(NT):
                        i = V.max_index(out=ri[:, t, :], in_max=rt[:, 1, t, :], in_values=rt[:, 0, t, :])
                    link(i)
                    link(V.tensor_copy(rt[:, 3, :, :], ri[:, :, :]))
                else:
                    br = rows[:, ROWS["br"][0]:ROWS["br"][1]].unsqueeze(1).to_broadcast([P, 4, 8])
                    V.tensor_tensor(lg, src, br, ALU.add).then_inc(sem(n + "_lg"), 1)
                    dve.wait_ge(sem(n + "_lg"), b + 1)
                    link(V.tensor_reduce(rt[:, 3, :, 0], lg, AX, ALU.max))
                    V.tensor_tensor(rt[:, 1, :, :], lg, bc(rt[:, 3, :, 0:1]), ALU.subtract).then_inc(sem(n + "_d"), 1)

            def moe_route2(m_, b):
                n = m_["n"]
                dve.wait_ge(sem(n + "_e"), b + 1)
                if b:
                    dve.wait_ge(sem(n + "_wTp"), b)
                io = iota.unsqueeze(1).to_broadcast([P, 4, 8])
                if n == "C":
                    e = lnv[:, 4, :]
                    link(V.tensor_scalar(rt[:, 4, :, 0], e, 1.0, None, ALU.add))
                    link(V.reciprocal(rt[:, 5, :, 0], rt[:, 4, :, 0]))
                    link(V.tensor_tensor(rt[:, 5, :, 1], rt[:, 5, :, 0], e, ALU.mult))
                    for k in range(2):
                        link(V.tensor_tensor(rt[:, 6 + k, :, :], io, bc(rt[:, 3, :, k:k + 1]), ALU.is_equal))
                        link(V.tensor_tensor(rt[:, 8 + k, :, :], rt[:, 6 + k, :, :], bc(rt[:, 5, :, k:k + 1]), ALU.mult))
                    V.tensor_tensor(rt[:, 11, :, :], rt[:, 8, :, :], rt[:, 9, :, :], ALU.add).then_inc(sem(n + "_wt"), 1)
                else:
                    link(V.tensor_reduce(rt[:, 4, :, 0], rt[:, 2, :, :], AX, ALU.add))
                    link(V.reciprocal(rt[:, 5, :, 0], rt[:, 4, :, 0]))
                    link(V.tensor_tensor(rt[:, 6, :, :], rt[:, 2, :, :], bc(rt[:, 5, :, 0:1]), ALU.mult))
                    for t in range(NT):
                        i = V.max(out=rt[:, 7, t, :], in_=rt[:, 6, t, :])
                    link(i)
                    for t in range(NT):
                        i = V.max_index(out=ri[:, t, :], in_max=rt[:, 7, t, :], in_values=rt[:, 6, t, :])
                    link(i)
                    link(V.tensor_copy(rt[:, 8, :, :], ri[:, :, :]))
                    link(V.tensor_tensor(rt[:, 9, :, :], io, bc(rt[:, 8, :, 0:1]), ALU.is_equal))
                    V.tensor_tensor(rt[:, 11, :, :], rt[:, 9, :, :], bc(rt[:, 7, :, 0:1]), ALU.mult)\
                        .then_inc(sem(n + "_wt"), 1)

            def moe_route3(m_, b):
                n = m_["n"]
                dve.wait_ge(sem(n + "_wTp"), b + 1)
                src = where[n + "wT", b][0:E, :]
                V.tensor_copy(wT_C[0:E, (b % 2) * S:(b % 2 + 1) * S], src)
                split_rows(src, E, wsel_b[b % 2]).then_inc(sem(n + "_sel"), 1)

            def moe(ph):
                m_ = MOE[ph]
                n, ft = m_["n"], m_["ft"]
                steps = E * ft
                enter(dve, ph)
                dve.wait_ge(sem(n + "_zero"), 1)
                moe_route1(m_, 0)
                moe_route2(m_, 0)
                moe_route3(m_, 0)
                for i in range(NB * steps):
                    b, s = i // steps, i % steps
                    tail(m_["w0"] + b - 1, s)
                    if b + 1 < NB:
                        if s == 12:
                            moe_route1(m_, b + 1)
                        if s == 14:
                            moe_route2(m_, b + 1)
                        if s == 15:
                            moe_route3(m_, b + 1)
                    dve.wait_ge(sem(n + "_h"), i + 1)
                    dve.wait_ge(sem(n + "_wb"), i // ft + 1)
                    if i >= 3:
                        k = i - 3
                        if k % steps == steps - 1:
                            dve.wait_ge(y_ready, m_["w0"] + k // steps + 1)
                        else:
                            dve.wait_ge(sem(n + "_c"), k + 1 - k // steps)
                    V.tensor_tensor(hwC[i % 3], hsC[i % 3], bank[3 + (s // ft) % 2][:, :], ALU.mult)\
                        .then_inc(sem(n + "_hw"), 1)

            def d_z(b):
                dve.wait_ge(sem("d_al"), b + 1)
                ba = rows[:, ROWS["ba"][0]:ROWS["ba"][1]].unsqueeze(1).to_broadcast([P, NT, H])
                V.tensor_tensor(v3(spD[0], NT), v3(where["d_al", b][:, 0:64], NT), ba, ALU.add).then_inc(sem("d_z"), 1)
                dve.wait_ge(sem("d_z"), b + 1)
                link(V.tensor_scalar(spD[1], spD[0], -1.0, None, ALU.mult))
                V.tensor_tensor(spD[1], spD[1], spD[0], ALU.max).then_inc(sem("d_az"), 1)

            def d_sp(b):
                dve.wait_ge(sem("d_ln"), b + 1)
                V.scalar_tensor_tensor(out=spD[3], in0=spD[0], scalar=0.0, in1=spD[2], op0=ALU.max, op1=ALU.add)\
                    .then_inc(sem("d_sp"), 1)

            def d_lsel(b):
                dve.wait_ge(sem("d_LT"), b + 1)
                split_rows(where["d_LT", b][0:H, :], H, lsel_b[b % 2]).then_inc(sem("d_lsel"), 1)
                dve.wait_ge(sem("d_lcp"), b + 1)
                V.tensor_copy(lcD[b % 2], where["d_lc", b][:, 0:128]).then_inc(sem("d_lcs"), 1)

            def d_args(g):
                b, p = g // 8, g % 8
                lc = v3(lcD[b % 2][:, 0:64], NT)
                dm = dmD[g % 2].rearrange("p (c h i) -> p c h i", c=NT, h=2)
                if p == 0:
                    dve.wait_ge(sem("d_lcs"), b + 1)
                if g >= 2:
                    dve.wait_ge(sem("d_at"), 2 * (g - 1))
                for hh in range(2):
                    h = 2 * p + hh
                    dve.wait_ge(sem("d_la"), 2 * g + hh + 1)
                    V.tensor_tensor(dm[:, :, hh, :], lc[:, :, h:h + 1].to_broadcast([P, NT, P]), v3(bank[1][:, :], NT),
                                    ALU.subtract).then_inc(sem("d_arg"), 1)

            def d_silu(g, i):
                dve.wait_ge(sem("d_tq"), 2 * g + i + 1)
                if g >= 2:
                    dve.wait_ge(sem("d_s"), 2 * (g - 1))
                    if i:
                        dve.wait_ge(sem("d_kt"), g - 1)
                    else:
                        dve.wait_ge(sem("d_qb"), 2 * (g - 1))
                th = tqD[i]
                out = qTD[g % 2] if i == 0 else kTD[g % 2]
                V.scalar_tensor_tensor(out=out, in0=th, scalar=1.0, in1=where["d_p", 3 * g + i][:, :],
                                       op0=ALU.add, op1=ALU.mult).then_inc(sem("d_silu"), 1)

            def d_qe(g):
                dve.wait_ge(sem("d_el"), g + 1)
                dve.wait_ge(sem("d_silu"), 2 * g + 1)
                if g >= 2:
                    dve.wait_ge(sem("d_pv"), g - 1)
                V.scalar_tensor_tensor(out=qeD[g % 2], in0=qTD[g % 2], scalar=0.25, in1=elD[g % 2],
                                       op0=ALU.mult, op1=ALU.mult).then_inc(sem("d_qe"), 1)

            def d_kd(g):
                b, p = g // 8, g % 8
                dve.wait_ge(sem("d_kt"), g + 1)
                dve.wait_ge(sem("d_kdec"), b + 1)
                if g >= 2:
                    dve.wait_ge(sem("d_dl"), g - 1)
                kdec = v3(kdecD[b % 2], NT)[:, :, 2 * p:2 * p + 2].unsqueeze(3).to_broadcast([P, NT, 2, DH])
                V.tensor_tensor(kdD[g % 2].rearrange("p (c h d) -> p c h d", c=NT, h=2),
                                bank[4][:, :].rearrange("p (c h d) -> p c h d", c=NT, h=2), kdec, ALU.mult)\
                    .then_inc(sem("d_kd"), 1)

            def d_at(g):
                dve.wait_ge(sem("d_dm"), g + 1)
                if g >= 2:
                    dve.wait_ge(sem("d_pv"), g - 1)
                for c2 in range(2):
                    dve.wait_ge(sem("d_s"), 2 * g + c2 + 1)
                    r = slice(c2 * S, (c2 + 1) * S)
                    V.scalar_tensor_tensor(out=atD[g % 2][:, r], in0=bank[2 + c2][:, :], scalar=0.25, in1=dmD[g % 2][:, r],
                                           op0=ALU.mult, op1=ALU.mult).then_inc(sem("d_at"), 1)

            def d_st(g):
                dve.wait_ge(sem("d_dl"), g + 1)
                if g >= 2:
                    dve.wait_ge(sem("d_pv"), g - 1)
                for c in range(NT - 1):
                    for hh in range(2):
                        r = slice(hh * DH, (hh + 1) * DH)
                        k = slice(c * P + hh * DH, c * P + (hh + 1) * DH)
                        if c == 0:
                            i = V.tensor_copy(stD[g % 2][r, k], bank[4][r, k])
                        else:
                            o = slice((c - 1) * P + hh * DH, (c - 1) * P + (hh + 1) * DH)
                            i = V.scalar_tensor_tensor(out=stD[g % 2][r, k], in0=stD[g % 2][r, o],
                                                       scalar=elD[g % 2][r, c * P + P - 1:c * P + P], in1=bank[4][r, k],
                                                       op0=ALU.mult, op1=ALU.add)
                    if c < NT - 2:
                        link(i)
                i.then_inc(sem("d_st"), 1)

            def d_stats(g):
                dve.wait_ge(sem("d_pv"), g + 1)
                V.bn_stats(gn6[:, 0:6], bank[5][:, :]).then_inc(sem("d_bs"), 1)
                dve.wait_ge(sem("d_bs"), g + 1)
                i = V.bn_aggr(gnD[6][:, 0:2], gn6[:, 0:6])
                link(i)
                p, k = g % 8, g % 16
                V.tensor_copy(gnD[0][:, k:k + 1], gnD[6][:, 0:1])
                i = V.tensor_copy(gnD[1][:, k:k + 1], gnD[6][:, 1:2])
                if p == 7:
                    i.then_inc(sem("d_gs"), 1)
                else:
                    link(i)

            def d_spread(b):
                dve.wait_ge(sem("d_gp"), 2 * b + 1)
                dve.wait_ge(sem("d_gs"), 2 * b + 1)
                V.tensor_copy(gnD[7][:, 0:8], where["d_gn", 2 * b][:, 0:8]).then_inc(sem("d_gr"), 1)
                dve.wait_ge(sem("d_gr"), 2 * b + 1)
                r = slice(8 * (b % 2), 8 * (b % 2) + 8)
                link(V.tensor_tensor(gnD[2][:, 0:8], gnD[0][:, r], gnD[7][:, 0:8], ALU.subtract))
                link(V.tensor_tensor(gnD[2][:, 0:8], gnD[2][:, 0:8], gnD[2][:, 0:8], ALU.mult))
                V.tensor_tensor(gnD[2][:, 0:8], gnD[2][:, 0:8], gnD[1][:, r], ALU.add).then_inc(sem("d_gs"), 1)

            def d_gvar(b):
                dve.wait_ge(sem("d_gp"), 2 * b + 2)
                V.tensor_scalar(gnD[3][:, 0:8], where["d_gn", 2 * b + 1][:, 0:8], EPS, None, ALU.add)\
                    .then_inc(sem("d_gr"), 1)

            def d_gate(b):
                dve.wait_ge(sem("d_g0"), b + 1)
                newton(gnD[3][:, 0:8], gnD[5][:, 0:8], gnD[4][:, 8:16], gnD[6][:, 8:16])
                gw, gb = (cols[:, COLS[k][0]:COLS[k][1]] for k in ("gn_w", "gn_b"))
                A_, B_ = gnD[4][:, 0:8], gnD[5][:, 8:16]
                link(V.scalar_tensor_tensor(out=A_, in0=gw, scalar=0.5, in1=gnD[6][:, 8:16], op0=ALU.mult, op1=ALU.mult))
                link(V.tensor_tensor(B_, gnD[7][:, 0:8], A_, ALU.mult))
                link(V.scalar_tensor_tensor(out=B_, in0=gb, scalar=0.5, in1=B_, op0=ALU.mult, op1=ALU.subtract))
                dve.wait_ge(sem("d_o"), 8 * b + 8)
                dve.wait_ge(sem("d_th"), 8 * b + 8)
                for p in range(8):
                    o = o_slot(PD + b, p)
                    link(V.tensor_scalar(o, o, A_[:, p:p + 1], B_[:, p:p + 1], ALU.mult, ALU.add))
                    V.scalar_tensor_tensor(out=o, in0=thD[(8 * b + p) % 12], scalar=1.0, in1=o, op0=ALU.add, op1=ALU.mult)\
                        .then_inc(sem("d_og"), 1)

            def phase_d():
                enter(dve, 3)
                dve.wait_ge(sem("d_zero"), 1)
                d_z(0)
                d_sp(0)
                d_lsel(0)
                d_args(0)
                d_silu(0, 0)
                d_silu(0, 1)
                d_qe(0)
                for g in range(33):
                    b, s = g // 8, g % 8
                    if g + 1 < 32:
                        d_args(g + 1)
                        d_silu(g + 1, 0)
                        d_silu(g + 1, 1)
                        d_qe(g + 1)
                    if g < 32:
                        d_kd(g)
                        d_at(g)
                    if g >= 1:
                        d_stats(g - 1)
                    if g < 32:
                        d_st(g)
                        tail(PD + b - 1, s)
                        if b and s == 1:
                            d_spread(b - 1)
                        if b and s == 2:
                            d_gvar(b - 1)
                            d_gate(b - 1)
                        if b + 1 < NB:
                            if s == 2:
                                d_z(b + 1)
                                d_sp(b + 1)
                            if s == 4:
                                d_lsel(b + 1)
                d_spread(3)
                d_gvar(3)
                d_gate(3)

            cross(1)
            moe(2)
            phase_d()
            cross(4)
            moe(5)
            for s in range(32):
                tail(WORKS - 1, s)

        @block_ctx.gpsimd
        def _(pool):
            G = nc.gpsimd

            G.memset(kzA[0], 0.0)
            G.memset(kzA[1], 0.0).then_inc(sem("a_zero"), 1)

            def cross(ph):
                c = CROSS[ph]
                enter(pool, ph)
                G.memset(kdB, 0.0)
                G.memset(vcB, 0.0)
                G.memset(pB[0], 0.0)
                G.memset(pB[1], 0.0).then_inc(sem(c["n"] + "_zero"), 1)

            def moe(ph):
                enter(pool, ph)
                G.memset(wselC, 0.0).then_inc(sem(MOE[ph]["n"] + "_zero"), 1)

            def phase_d():
                enter(pool, 3)
                G.memset(lselD, 0.0)
                for i in range(2):
                    G.memset(qbD[i], 0.0)
                    z = G.memset(stD[i], 0.0)
                z.then_inc(sem("d_zero"), 1)
                pool.wait_ge(sem("d_zero"), 1)
                for g in range(32):
                    pool.wait_ge(sem("d_silu"), 2 * g + 1)
                    if g >= 2:
                        pool.wait_ge(sem("d_s"), 2 * (g - 1))
                    qb = qbD[g % 2].rearrange("p (c h i) -> p c h i", c=NT, h=2)
                    for hh in range(2):
                        r = slice(hh * DH, (hh + 1) * DH)
                        G.tensor_copy(qb[r, :, hh, :], v3(qTD[g % 2], NT)[r, :, :]).then_inc(sem("d_qb"), 1)
                pool.wait_ge(sem("d_qb"), 64)
                G.memset(gnD[7][:, 8:16], 0.0).then_inc(sem("d_x"), 1)

            cross(1)
            moe(2)
            phase_d()
            cross(4)
            moe(5)


def kernel(**inputs):
    import numpy as np
    import concourse.bacc as bacc
    from concourse.bass_utils import run_bass_kernel_spmd

    I = {k: np.asarray(v) for k, v in inputs.items()}

    def by_partition(v, n):
        return v.reshape(n, P).T

    arrays = {"x": I["x"]}
    arrays["ctxT"] = I["ctx_1024"].reshape(NB * C, D).T
    for k in ("L0_attn_Wq", "L0_attn_Wk", "L0_attn_Wv", "L0_attn_Wo", "L0_xattn_Wq", "L0_xattn_Wk", "L0_xattn_Wv",
              "L0_xattn_Wo", "L1_attn_Wq", "L1_attn_Wk", "L1_attn_Wv", "L1_attn_Wg", "L1_attn_Wo", "L1_xattn_Wq",
              "L1_xattn_Wk", "L1_xattn_Wv", "L1_xattn_Wo", "L1_ffn_W1", "L1_ffn_W2", "L0_ffn_b2", "L1_ffn_b2"):
        arrays[k] = I[k]
    arrays["w1T"] = I["L0_ffn_w1"].reshape(E * FT0 * P, D).T
    arrays["w2T"] = I["L0_ffn_w2"].transpose(0, 2, 1).reshape(E * FT0 * P, D)
    arrays["cols"] = np.concatenate([by_partition(I[k], n) for k, n in (
        ("L0_attn_ln_gamma", 1), ("L0_attn_ln_beta", 1), ("L0_xattn_bq", 8), ("L0_xattn_bk", 8), ("L0_xattn_bv", 8),
        ("L0_xattn_bo", 1), ("L0_ffn_b1", 32), ("L1_attn_gn_w", 8), ("L1_attn_gn_b", 8), ("L1_xattn_bo", 1),
        ("L1_ffn_b1", 16))], axis=1)
    arrays["rows"] = np.concatenate([I["L0_xattn_ln_gamma"], I["L0_xattn_ln_beta"], I["L1_attn_ba"], I["L1_ffn_br"]])
    arrays["narrow"] = np.concatenate([I["L0_ffn_router_w"].T, I["L1_ffn_Wr"], I["L1_attn_Wa"]], axis=1)

    i = np.arange(P)
    c = np.zeros((P, NCONSTS), np.float32)
    c[:, 0:128] = np.eye(P)
    c[:, 128:256] = i[:, None] <= i[None, :]
    c[:, 256:384] = i[:, None] > i[None, :]
    c[:, 384:512] = (i[:, None] // DH == i[None, :] // DH) * (1.0 / DH)
    c[:, 512:520] = np.arange(E)
    for h in range(H):
        c[[h, 32 + h, 64 + h], 520 + h] = 1.0
    c[:, 536:1048] = np.tile((i[:, None] > i[None, :]) * 1e30, (1, NT))
    arrays["consts"] = c

    nc = bacc.Bacc("TRN2", target_bir_lowering=False, num_devices=1)
    T = {}
    feed = {}
    for k, a in arrays.items():
        a = np.ascontiguousarray(a)
        feed[f"in_{k}"] = a
        T[k] = nc.dram_tensor(f"in_{k}", a.shape, mybir.dt.from_np(a.dtype), kind="ExternalInput").ap()
    T["out"] = nc.dram_tensor("out_0", (NB, S, D), F32, kind="ExternalOutput").ap()
    decoder(nc, T)
    r = run_bass_kernel_spmd(nc, [feed], core_ids=[0])
    return r.results[0]["out_0"]
```

```python
from contextlib import ExitStack

import concourse.bass as bass
from concourse import mybir

P = 128
ALU = mybir.AluOpType
ACT = mybir.ActivationFunctionType
AX = mybir.AxisListType.X
F32 = mybir.dt.float32
BF16 = mybir.dt.bfloat16
U32 = mybir.dt.uint32

NB = 4
S = 512
NT = S // P
D = 128
DH = 64
C = 77
H = 16
NPAIR = H // 2
HX1 = 8
E = 8
FT0 = 4
FT1 = 2
EPS = 1e-5
UNITS = H * NT
PB, PC, PD, PE_, PF = 4, 8, 12, 16, 20
WORKS = 24
WORK = 27136
PW = H * C + P - C + 1

COLS = {}
_n = 0
for _name, _w in (("ln_g", 1), ("ln_b", 1), ("bq", 8), ("bk", 8), ("bv", 8), ("bo0", 1), ("b1_0", 32),
                  ("gn_w", 8), ("gn_b", 8), ("bo1", 1), ("b1_1", 16)):
    COLS[_name] = (_n, _n + _w)
    _n += _w
NCOLS = _n
ROWS = {"xg": (0, 128), "xb": (128, 256), "ba": (256, 272), "br": (272, 280)}
NROWS = 280
CONSTS = {"ident": (0, 128), "upto": (128, 256), "after": (256, 384), "block": (384, 512), "iota": (512, 520),
          "sel": (520, 536), "mask": (536, 1048), "heads": (1048, 1050)}
NCONSTS = 1050


def decoder(nc, T):
    with ExitStack() as ctx:
        def sb(name, shape, dt=F32):
            return ctx.enter_context(nc.sbuf_tensor(name, shape, dt))

        sems = {}

        def sem(name):
            if name not in sems:
                sems[name] = ctx.enter_context(nc.semaphore(name))
            return sems[name]

        bank = [ctx.enter_context(nc.psum_tensor(f"bank{i}", [P, S], F32)) for i in range(8)]
        x_all = sb("x_all", [P, NB * NT, D])
        xT_all = sb("xT_all", [P, NB, S])
        yT = sb("yT", [P, S])
        res = sb("res", [P, NT, D])
        OT = sb("OT", [P, NPAIR, S])
        W0 = sb("W0", [P, 8192])
        W1 = sb("W1", [P, 5120])
        cols = sb("cols", [P, NCOLS])
        rows = sb("rows", [P, NROWS])
        cst = sb("cst", [P, 520])
        heads = sb("heads", [P, 2])
        mask = sb("mask", [P, S], BF16)
        ident_b = sb("ident_b", [P, P], BF16)
        sel = sb("sel", [P, H], BF16)
        rw = sb("rw", [P, 32])
        b2 = sb("b2", [E, 2, D])
        bn = sb("bn", [P, NT, 6])
        mv = sb("mv", [P, NT, 2])
        lnv = sb("lnv", [P, 6, NT])
        rt = sb("rt", [P, 12, 4, 8])
        ri = sb("ri", [P, 4, 8], U32)
        work = sb("work", [P, WORK])

        def col(name, i=0):
            return cols[:, COLS[name][0] + i:COLS[name][0] + i + 1]

        ident = cst[:, 0:128]
        upto = cst[:, 128:256]
        after = cst[:, 256:384]
        block = cst[:, 384:512]
        iota = cst[:, 512:520]

        def carve(at, n, count=1):
            return [work[:, at + i * n:at + (i + 1) * n] for i in range(count)], at + n * count

        (xn,), a = carve(0, S)
        xnT, a = carve(a, S, 2)
        qTA, a = carve(a, S, 2)
        kzA, a = carve(a, 2 * S, 2)
        pA, a = carve(a, S, 4)
        ptA, a = carve(a, NT * S, 4)
        vA, a = carve(a, NT * S, 2)
        rsum, a = carve(a, 8, 2)
        (nmax,), a = carve(a, 8)
        end_a = a
        (kdB,), a = carve(0, NPAIR * NB * 2 * C)
        (vcB,), a = carve(a, NB * H * DH)
        (ptB,), a = carve(a, H * S)
        pB, a = carve(a, PW, 3)
        q_at = a
        (qTB,), a = carve(a, NPAIR * S)
        statB, a = carve(a, 16, 6)
        assert a <= WORK - 1536 and end_a <= q_at
        hsC, a = carve(q_at, S, 3)
        hwC, a = carve(a, S, 3)
        (wT_C,), a = carve(WORK - 1536, 2 * S)
        (wselC,), a = carve(a, S)
        vD, a = carve(0, NT * S, 2)
        qTD, a = carve(a, S, 2)
        qbD, a = carve(a, 2 * S, 2)
        kTD, a = carve(a, S, 2)
        qeD, a = carve(a, S, 3)
        elD, a = carve(a, S, 3)
        dmD, a = carve(a, 2 * S, 2)
        atD, a = carve(a, 2 * S, 3)
        kdD, a = carve(a, S, 2)
        stD, a = carve(a, 3 * P, 2)
        oxD, a = carve(a, S, 4)
        thD, a = carve(a, S, 8)
        tqD, a = carve(a, S, 2)
        spD, a = carve(a, 64, 4)
        (lselD,), a = carve(a, S)
        lcD, a = carve(a, 128, 2)
        kdecD, a = carve(a, 64, 2)
        gnD, a = carve(a, 16, 8)
        (gn6,), a = carve(a, 8)
        assert a <= WORK, a

        wsel_b = [wselC[:, i * 256:(i + 1) * 256].bitcast(BF16) for i in range(2)]
        lsel_b = [lselD[:, i * 256:(i + 1) * 256].bitcast(BF16) for i in range(2)]
        spl_r = sb("spl_r", [16, S])
        spl_m = sb("spl_m", [16, S], BF16)

        def v3(ap, n):
            return ap.rearrange("p (n k) -> p n k", n=n)

        wqA, wkA, wvA, woA = (W0[:, i * 1024:(i + 1) * 1024] for i in range(4))
        wqB, wkB, wvB, woB = (W1[:, i * 1024:(i + 1) * 1024] for i in range(4))
        w1C, w2C = W0[:, 0:4096], W0[:, 4096:8192]
        wqD, wkD, wvD, wgD, woD = (W1[:, i * 1024:(i + 1) * 1024] for i in range(5))
        wqE, wkE, wvE, woE = (W0[:, i * 512:(i + 1) * 512] for i in range(4))
        w1F, w2F = W1[:, 0:2048], W1[:, 2048:4096]

        ctxT = sb("ctxT", [P, NB * C])

        def out_w(ph):
            return {0: woA, 1: woB, 3: woD, 4: woE}[ph]

        def o_slot(w, p):
            if w // NB == 3:
                s = (8 * (w % NB) + p) % 12
                return OT[:, s, :] if s < 8 else oxD[s - 8]
            return OT[:, p, :]

        CROSS = {1: dict(n="B", w0=PB, np=NPAIR, wq=wqB, wk=wkB, wv=wvB, bias=True),
                 4: dict(n="E", w0=PE_, np=HX1 // 2, wq=wqE, wk=wkE, wv=wvE, bias=False)}
        MOE = {2: dict(n="C", w0=PC, ft=FT0, w1=w1C, w2=w2C, b1="b1_0", r=0, func=ACT.Gelu),
               5: dict(n="F", w0=PF, ft=FT1, w1=w1F, w2=w2F, b1="b1_1", r=1, func=ACT.Relu)}

        TAIL = {0: (9, 13, 14, 15, 20), 1: (1, 3, 4, 5, 8), 2: (3, 5, 6, 8, 11), 3: (4, 5, 6, 6, 7),
                4: (1, 3, 4, 5, 8), 5: (3, 5, 6, 8, 11)}

        def cross_tail(tail, w0, u):
            for b in range(NB - 1):
                k = u - 4 * b - 6
                if 0 <= k < 4:
                    for s in range(2 * k, 2 * k + 2):
                        tail(w0 + b, s)

        def tail_steps(w):
            if w // NB in (1, 4) and w % NB < NB - 1:
                return (0, 2, 4, 5, 6)
            return (0, 1, 2, 2, 3) if w == PD - 1 else TAIL[min((w + 1) // NB, 5)]

        y_ready, yT_ready, yt_ready = sem("y_ready"), sem("yT_ready"), sem("yt_ready")
        x_ready, xTp_ready, xT_ready = sem("x_ready"), sem("xTp_ready"), sem("xT_ready")
        dve_chain, act_chain, pool_chain = sem("dve_chain"), sem("act_chain"), sem("pool_chain")
        dma_in = {k: sem("dma_" + k) for k in ("x", "small", "A", "B", "C", "D", "E", "F", "out")}
        consts_ready = sem("consts_ready")

        def loaded(eng, what, n=1):
            eng.wait_ge(dma_in[what], 16 * n)

        DMA_COUNT = {"x": 4, "small": 7, "A": 4, "B": 5, "C": 2, "D": 5, "E": 4, "F": 2}

        ENDS = {0: [("a_pv", 32), ("a_o", 32)],
                1: [("B_s", 16)],
                2: [("y_ready", 12), ("C_hw", 128)],
                3: [("y_ready", 15), ("d_og", 32)],
                4: [("E_s", 16)]}

        def enter(eng, ph):
            for name, value in ENDS[ph - 1]:
                eng.wait_ge(sem(name), value)

        owner = {}
        where = {}

        def take(pe, i, reader, value):
            if i in owner:
                s, n = owner[i]
                pe.wait_ge(s, n)
            owner[i] = (reader, value)
            return bank[i]

        turn = [0]

        def take_next(pe, key, reader, value):
            i = 6 + turn[0] % 2
            turn[0] += 1
            where[key] = bank[i]
            return take(pe, i, reader, value)

        block_ctx = ctx.enter_context(nc.Block())

        @block_ctx.sync
        def _(sp):
            sp.dma_start(x_all[:, 0:4, :], T["x"][0].rearrange("(t p) d -> p t d", p=P)).then_inc(dma_in["x"], 16)
            sp.dma_start(cst[:, 0:520], T["consts"][:, 0:520]).then_inc(dma_in["small"], 16)
            sp.dma_start(work[:, 26000:26530], T["consts"][:, 520:1050]).then_inc(dma_in["small"], 16)
            sp.dma_start(cols[:, :], T["cols"]).then_inc(dma_in["small"], 16)
            for i, n in enumerate(("L0_attn_Wq", "L0_attn_Wk", "L0_attn_Wv")):
                sp.dma_start(W0[:, i * 1024:(i + 1) * 1024], T[n]).then_inc(dma_in["A"], 16)
            for b in range(1, NB):
                sp.dma_start(x_all[:, 4 * b:4 * b + 4, :], T["x"][b].rearrange("(t p) d -> p t d", p=P))\
                    .then_inc(dma_in["x"], 16)
            sp.dma_start(v3(woA, 8), T["L0_attn_Wo"].rearrange("(n p) d -> p n d", p=P)).then_inc(dma_in["A"], 16)
            sp.dma_start(rows[:, :], T["rows"].partition_broadcast(P)).then_inc(dma_in["small"], 16)
            sp.dma_start(rw[:, :], T["narrow"]).then_inc(dma_in["small"], 16)
            sp.dma_start(b2[:, 0, :], T["L0_ffn_b2"]).then_inc(dma_in["small"], 16)
            sp.dma_start(b2[:, 1, :], T["L1_ffn_b2"]).then_inc(dma_in["small"], 16)
            sp.dma_start(ctxT[:, :], T["ctxT"]).then_inc(dma_in["B"], 16)
            for i, n in enumerate(("L0_xattn_Wq", "L0_xattn_Wk", "L0_xattn_Wv")):
                sp.dma_start(W1[:, i * 1024:(i + 1) * 1024], T[n]).then_inc(dma_in["B"], 16)
            sp.dma_start(v3(woB, 8), T["L0_xattn_Wo"].rearrange("(n p) d -> p n d", p=P)).then_inc(dma_in["B"], 16)
            sp.wait_ge(y_ready, 4)
            sp.dma_start(w1C, T["w1T"]).then_inc(dma_in["C"], 16)
            sp.dma_start(w2C.rearrange("p (e d) -> p e d", d=D), T["w2T"].rearrange("(e p) d -> p e d", p=P))\
                .then_inc(dma_in["C"], 16)
            sp.wait_ge(y_ready, 8)
            for i, n in enumerate(("L1_attn_Wq", "L1_attn_Wk", "L1_attn_Wv", "L1_attn_Wg")):
                sp.dma_start(W1[:, i * 1024:(i + 1) * 1024], T[n]).then_inc(dma_in["D"], 16)
            sp.dma_start(v3(woD, 8), T["L1_attn_Wo"].rearrange("(n p) d -> p n d", p=P)).then_inc(dma_in["D"], 16)
            sp.wait_ge(y_ready, 12)
            for i, n in enumerate(("L1_xattn_Wq", "L1_xattn_Wk", "L1_xattn_Wv")):
                sp.dma_start(W0[:, i * 512:(i + 1) * 512], T[n]).then_inc(dma_in["E"], 16)
            sp.dma_start(v3(woE, 4), T["L1_xattn_Wo"].rearrange("(n p) d -> p n d", p=P)).then_inc(dma_in["E"], 16)
            sp.wait_ge(y_ready, 16)
            sp.dma_start(w1F.rearrange("p (e h) -> p e h", e=E), T["L1_ffn_W1"].rearrange("e d h -> d e h"))\
                .then_inc(dma_in["F"], 16)
            sp.dma_start(w2F.rearrange("p (e d) -> p e d", d=D),
                         T["L1_ffn_W2"].rearrange("e (t p) d -> p (e t) d", p=P)).then_inc(dma_in["F"], 16)
            for b in range(NB):
                sp.wait_ge(x_ready, PF + b + 1)
                sp.dma_start(T["out"][b].rearrange("(t p) d -> p t d", p=P), x_all[:, 4 * b:4 * b + 4, :])\
                    .then_inc(dma_in["out"], 16)
            sp.wait_ge(dma_in["out"], 16 * NB)

        @block_ctx.tensor
        def _(pe):
            mm = nc.tensor.matmul

            def tail(w, s, last=False):
                ph = w // NB
                at = tail_steps(w)
                if s == at[0] and ph in (0, 1, 3, 4):
                    n = 4 if ph == 4 else 8
                    pe.wait_ge(sem({0: "a_o", 1: "B_o", 3: "d_og", 4: "E_o"}[ph]), n * (w % NB + 1))
                    out = take_next(pe, ("y", w), yT_ready, w + 1)
                    for p in range(n):
                        m = mm(out[:, :], out_w(ph)[:, p * P:(p + 1) * P], o_slot(w, p), start=(p == 0), stop=(p == n - 1))
                    m.then_inc(y_ready, 1)
                if s == at[1]:
                    pe.wait_ge(yT_ready, w + 1)
                    out = take_next(pe, ("yt", w), sem("sum_done"), w + 1)
                    for t in range(NT):
                        m = nc.tensor.transpose(out[:, t * P:(t + 1) * P], yT[:, t * P:(t + 1) * P], ident)
                    m.then_inc(yt_ready, 1)
                if s == at[4] and w < PF:
                    pe.wait_ge(x_ready, w + 1)
                    out = take_next(pe, ("xT", w), xT_ready, w + 1)
                    b = w % NB
                    for t in range(NT):
                        m = nc.tensor.transpose(out[:, t * P:(t + 1) * P], x_all[:, 4 * b + t, :], ident)
                    m.then_inc(xTp_ready, 1)

            def a_norm_T(b):
                pe.wait_ge(sem("a_xn"), b + 1)
                out = take_next(pe, ("a_xn", b), sem("a_xnT"), b + 1)
                for t in range(NT):
                    m = nc.tensor.transpose(out[:, t * P:(t + 1) * P], v3(xn, NT)[:, t, :], ident)
                m.then_inc(sem("a_xnp"), 1)

            def a_v(b, hf, t):
                n = 8 * b + 4 * hf + t
                pe.wait_ge(sem("a_xnT"), b + 1)
                out = take_next(pe, ("a_v", n), sem("a_vs"), n + 1)
                mm(out[:, :], xnT[b % 2][:, t * P:(t + 1) * P], wvA[:, hf * S:(hf + 1) * S], start=True, stop=True)\
                    .then_inc(sem("a_vp"), 1)

            def a_qk(g, w, ready, done):
                b, p = g // 8, g % 8
                pe.wait_ge(sem("a_xnT"), b + 1)
                out = take_next(pe, (ready, g), sem(done), g + 1)
                mm(out[:, :], w[:, p * P:(p + 1) * P], xnT[b % 2], start=True, stop=True).then_inc(sem(ready), 1)

            def a_scores(u):
                g, hh, t = u // 8, (u // 4) % 2, u % 4
                if u % 8 == 0:
                    pe.wait_ge(sem("a_qs"), g + 1)
                    pe.wait_ge(sem("a_ks"), g + 1)
                out = take(pe, u % 3, sem("a_e"), u + 1)
                mm(out[:, :], qTA[g % 2][:, t * P:(t + 1) * P], kzA[g % 2][:, hh * S:(hh + 1) * S], start=True, stop=True)\
                    .then_inc(sem("a_s"), 1)

            def a_turn(u):
                pe.wait_ge(sem("a_n"), u + 1)
                out = take(pe, 3 + u % 2, sem("a_pt"), u + 1)
                for k in range(NT):
                    m = nc.tensor.transpose(out[:, k * P:(k + 1) * P], pA[u % 4][:, k * P:(k + 1) * P], ident)
                m.then_inc(sem("a_t"), 1)

            def a_out(g, k):
                b, p = g // 8, g % 8
                if k == 0:
                    pe.wait_ge(sem("a_pt"), 8 * g + 8)
                    pe.wait_ge(sem("a_vs"), 8 * b + 4 * (p // 4) + 4)
                    take(pe, 5, sem("a_o"), g + 1)
                for hh in range(2):
                    m = mm(bank[5][hh * DH:(hh + 1) * DH, :], v3(vA[p // 4], NT)[:, k, (2 * (p % 4) + hh) * DH:(2 * (p % 4) + hh + 1) * DH],
                           v3(ptA[(2 * g + hh) % 4], NT)[:, k, :], start=(k == 0), stop=(k == NT - 1))
                if k == NT - 1:
                    m.then_inc(sem("a_pv"), 1)

            loaded(pe, "small", 7)
            loaded(pe, "A", 4)
            a_norm_T(0)
            a_qk(0, wqA, "a_qp", "a_qs")
            a_qk(0, wkA, "a_kp", "a_ks")
            for t in range(NT):
                a_v(0, 0, t)
            NU = NB * UNITS
            for u in range(NU + 8):
                b, s, g, j = u // UNITS, u % UNITS, u // 8, u % 8
                if u < NU:
                    if b:
                        tail(b - 1, s)
                    if s == 24 and b + 1 < NB:
                        a_norm_T(b + 1)
                    if j == 0 and g + 1 < 32:
                        a_qk(g + 1, wqA, "a_qp", "a_qs")
                    if j == 1 and g + 1 < 32:
                        a_qk(g + 1, wkA, "a_kp", "a_ks")
                    if 48 <= s < 56 and s % 2 and b + 1 < NB:
                        a_v(b + 1, 0, (s - 48) // 2)
                    if 16 <= s < 24 and s % 2:
                        a_v(b, 1, (s - 16) // 2)
                    a_scores(u)
                if 3 <= u < NU + 3:
                    a_turn(u - 3)
                if 4 <= j <= 7 and g >= 1:
                    a_out(g - 1, j - 4)

            def cross_kv(c):
                n = c["n"]
                for p in range(c["np"]):
                    out = take_next(pe, (n + "k", p), sem(n + "_ks"), p + 1)
                    mm(out[:, 0:NB * C], c["wk"][:, p * P:(p + 1) * P], ctxT[:, :], start=True, stop=True)\
                        .then_inc(sem(n + "_kp"), 1)
                nh = c["np"] * P // S
                for i in range(NB * nh):
                    b, hf = i // nh, i % nh
                    out = take_next(pe, (n + "v", i), sem(n + "_vs"), i + 1)
                    mm(out[0:C, :], ctxT[:, b * C:(b + 1) * C], c["wv"][:, hf * S:(hf + 1) * S], start=True, stop=True)\
                        .then_inc(sem(n + "_vp"), 1)

            def cross_q(c, b):
                n, np_ = c["n"], c["np"]
                pe.wait_ge(xT_ready, c["w0"] - NB + b + 1)
                for p in range(np_):
                    k = np_ * b + p
                    out = take_next(pe, (n + "q", k), sem(n + "_qs"), k + 1)
                    mm(out[:, :], c["wq"][:, p * P:(p + 1) * P], xT_all[:, b, :], start=True, stop=True)\
                        .then_inc(sem(n + "_qp"), 1)

            def cross_scores(c, b, t):
                n, np_ = c["n"], c["np"]
                if t == 0:
                    pe.wait_ge(sem(n + "_qs"), np_ * (b + 1))
                    if b == 0:
                        pe.wait_ge(sem(n + "_ks"), np_)
                u = NT * b + t
                for p in range(np_):
                    if p % 3 == 0:
                        out = take(pe, p // 3, sem(n + "_sub"), u + 1)
                    kd = kdB[:, (p * NB + b) * 2 * C:(p * NB + b + 1) * 2 * C]
                    m = mm(out[:, (p % 3) * 2 * C:(p % 3 + 1) * 2 * C],
                           v3(qTB, NPAIR)[:, p, t * P:(t + 1) * P], kd, start=True, stop=True)
                m.then_inc(sem(n + "_s"), 1)

            def cross_turn(c, b, t):
                n, np_ = c["n"], c["np"]
                u = NT * b + t
                nq = np_ * 2 // 4
                pe.wait_ge(sem(n + "_n"), u + 1)
                for q in range(nq):
                    k = nq * u + q
                    out = take(pe, 3 + k % 2, sem(n + "_pt"), k + 1)
                    for i in range(4):
                        h = 4 * q + i
                        m = nc.tensor.transpose(out[:, i * P:(i + 1) * P], pB[u % 3][:, h * C:h * C + P], ident)
                    m.then_inc(sem(n + "_t"), 1)

            def cross_out(c, b):
                n, np_ = c["n"], c["np"]
                nq = np_ * 2 // 4
                pe.wait_ge(sem(n + "_pt"), nq * NT * (b + 1))
                if b == 0:
                    pe.wait_ge(sem(n + "_vs"), NB * np_ * P // S)
                for p in range(np_):
                    k = np_ * b + p
                    out = take_next(pe, (n + "o", k), sem(n + "_o"), k + 1)
                    for hh in range(2):
                        h = 2 * p + hh
                        m = mm(out[hh * DH:(hh + 1) * DH, :], v3(vcB, NB)[:, b, h * DH:(h + 1) * DH],
                               v3(ptB, H)[:, h, :], start=True, stop=True)
                    m.then_inc(sem(n + "_pv"), 1)

            def cross(ph):
                c = CROSS[ph]
                n, w0 = c["n"], c["w0"]
                loaded(pe, n, DMA_COUNT[n])
                cross_q(c, 0)
                cross_kv(c)
                for u in range(NB * NT + 3):
                    b, t = u // NT, u % NT
                    if b < NB:
                        cross_scores(c, b, t)
                        if t == 3 and b + 1 < NB:
                            cross_q(c, b + 1)
                    if u < NT:
                        for s in range(3 * u, 3 * u + 3):
                            tail(w0 - 1, s)
                    cross_tail(tail, w0, u)
                    if 2 <= u < NB * NT + 2:
                        cross_turn(c, (u - 2) // NT, (u - 2) % NT)
                    if t == 1 and b >= 1:
                        cross_out(c, b - 1)
                    if u == NB * NT + 1:
                        moe_logits(MOE[ph + 1], 0)

            def moe_logits(m_, b):
                n, r = m_["n"], m_["r"]
                pe.wait_ge(xT_ready, m_["w0"] - NB + b + 1)
                out = take_next(pe, (n + "lg", b), sem(n + "_lg"), b + 1)
                for t in range(NT):
                    m = mm(out[:, t * E:(t + 1) * E], xT_all[:, b, t * P:(t + 1) * P], rw[:, r * E:(r + 1) * E],
                           start=True, stop=True)
                m.then_inc(sem(n + "_lgp"), 1)

            def moe_wT(m_, b):
                n = m_["n"]
                pe.wait_ge(sem(n + "_wt"), b + 1)
                out = take_next(pe, (n + "wT", b), sem(n + "_sel"), b + 1)
                for t in range(NT):
                    m = nc.tensor.transpose(out[0:E, t * P:(t + 1) * P], rt[:, 11, t, :], ident)
                m.then_inc(sem(n + "_wTp"), 1)

            def moe_h(m_, i):
                n, steps = m_["n"], E * m_["ft"]
                b, s = i // steps, i % steps
                pe.wait_ge(xT_ready, m_["w0"] - NB + b + 1)
                out = take(pe, i % 3, sem(n + "_h"), i + 1)
                mm(out[:, :], m_["w1"][:, s * P:(s + 1) * P], xT_all[:, b, :], start=True, stop=True)\
                    .then_inc(sem(n + "_hp"), 1)

            def moe(ph):
                m_ = MOE[ph]
                n, ft, r = m_["n"], m_["ft"], m_["r"]
                steps = E * ft
                loaded(pe, n, DMA_COUNT[n])

                def contract(i):
                    b, k = i // steps, i % steps
                    if k == 0:
                        take(pe, 5, yT_ready, m_["w0"] + b + 1)
                        mm(bank[5][:, :], b2[:, r, :], wT_C[0:E, (b % 2) * S:(b % 2 + 1) * S], start=True, stop=False)
                    pe.wait_ge(sem(n + "_hw"), i + 1)
                    m = mm(bank[5][:, :], m_["w2"][:, k * D:(k + 1) * D], hwC[i % 3], start=False, stop=(k == steps - 1))
                    if k == steps - 1:
                        m.then_inc(y_ready, 1)
                    else:
                        m.then_inc(sem(n + "_c"), 1)

                for i in range(NB * steps + 2):
                    b, s = i // steps, i % steps
                    if b < NB:
                        tail(m_["w0"] + b - 1, s)
                        if b + 1 < NB and s == 12:
                            moe_logits(m_, b + 1)
                        if b + 1 < NB and s == 15:
                            moe_wT(m_, b + 1)
                        if i == 0:
                            moe_h(m_, 0)
                            moe_h(m_, 1)
                            moe_wT(m_, 0)
                        if s % ft == 0:
                            e = s // ft
                            if s == 0:
                                pe.wait_ge(sem(n + "_sel"), b + 1)
                            out = take(pe, 3 + e % 2, sem(n + "_hw"), i + ft)
                            mm(out[:, :], sel[:, e:e + 1].to_broadcast([P, P]), wsel_b[b % 2], start=True, stop=True)\
                                .then_inc(sem(n + "_wb"), 1)
                        if i >= 2:
                            moe_h(m_, i)
                    if i >= 2:
                        contract(i - 2)

            def d_alpha(b):
                pe.wait_ge(xT_ready, PC + b + 1)
                out = take_next(pe, ("d_al", b), sem("d_z"), b + 1)
                for t in range(NT):
                    m = mm(out[:, t * H:(t + 1) * H], xT_all[:, b, t * P:(t + 1) * P], rw[:, 16:32], start=True, stop=True)
                m.then_inc(sem("d_al"), 1)

            def d_sums(b):
                pe.wait_ge(sem("d_sp"), b + 1)
                out = take_next(pe, ("d_LT", b), sem("d_lsel"), b + 1)
                for t in range(NT):
                    m = mm(out[0:H, t * P:(t + 1) * P], v3(spD[3], NT)[:, t, :], upto, start=True, stop=True)
                m.then_inc(sem("d_LT"), 1)
                out = take_next(pe, ("d_lc", b), sem("d_lcs"), b + 1)
                mm(out[:, 0:64], upto, spD[3], start=True, stop=True)
                mm(out[:, 64:128], after, spD[3], start=True, stop=True).then_inc(sem("d_lcp"), 1)

            def d_v(b, hf, t):
                n = 8 * b + 4 * hf + t
                out = take_next(pe, ("d_v", n), sem("d_vs"), n + 1)
                mm(out[:, :], xT_all[:, b, t * P:(t + 1) * P], wvD[:, hf * S:(hf + 1) * S], start=True, stop=True)\
                    .then_inc(sem("d_vp"), 1)

            def d_decays(g):
                b, p = g // 8, g % 8
                if p == 0:
                    pe.wait_ge(sem("d_lsel"), b + 1)
                out = take(pe, 0, sem("d_el"), g + 1)
                for hh in range(2):
                    m = mm(out[hh * DH:(hh + 1) * DH, :], sel[:, 2 * p + hh:2 * p + hh + 1].to_broadcast([P, DH]),
                           lsel_b[b % 2], start=True, stop=True)
                m.then_inc(sem("d_lp"), 1)
                for hh in range(2):
                    out = take(pe, 1 - hh, sem("d_dm"), 2 * g + hh + 1)
                    mm(out[:, :], sel[:, 2 * p + hh:2 * p + hh + 1].to_broadcast([P, P]), lsel_b[b % 2],
                       start=True, stop=False)
                    mm(out[:, :], ident_b[:, :], mask[:, :], start=False, stop=True).then_inc(sem("d_la"), 1)

            def d_proj(g, i):
                b, p = g // 8, g % 8
                pe.wait_ge(xT_ready, PC + b + 1)
                reader = (sem("d_silu"), 2 * g + i + 1) if i < 2 else (sem("d_th"), g + 1)
                out = take_next(pe, ("d_p", g, i), *reader)
                mm(out[:, :], (wqD, wkD, wgD)[i][:, p * P:(p + 1) * P], xT_all[:, b, :], start=True, stop=True)\
                    .then_inc(sem("d_gp_" if i == 2 else "d_pp"), 1)

            def d_scores(g):
                pe.wait_ge(sem("d_qb"), g + 1)
                for c2 in range(2):
                    out = take(pe, 2 + c2, sem("d_at"), 2 * g + c2 + 1)
                    for c in (2 * c2, 2 * c2 + 1):
                        m = mm(out[:, (c % 2) * 256:(c % 2 + 1) * 256], kTD[g % 2][:, c * P:(c + 1) * P],
                               qbD[g % 2][:, c * 256:(c + 1) * 256], start=True, stop=True)
                    m.then_inc(sem("d_s"), 1)

            def d_kturn(g):
                pe.wait_ge(sem("d_silu"), 2 * g + 2)
                out = take(pe, 4, sem("d_kd"), g + 1)
                for c in range(NT):
                    m = nc.tensor.transpose(out[:, c * P:(c + 1) * P], kTD[g % 2][:, c * P:(c + 1) * P], ident)
                m.then_inc(sem("d_kt"), 1)

            def d_state(g):
                b, p = g // 8, g % 8
                pe.wait_ge(sem("d_kd"), g + 1)
                pe.wait_ge(sem("d_vs"), 8 * b + 4 * (p // 4) + 4)
                out = take(pe, 4, sem("d_st"), g + 1)
                for c in range(NT - 1):
                    m = mm(out[:, c * P:(c + 1) * P], kdD[g % 2][:, c * P:(c + 1) * P],
                           v3(vD[p // 4], NT)[:, c, (p % 4) * P:(p % 4 + 1) * P], start=True, stop=True)
                m.then_inc(sem("d_dl"), 1)

            def d_out(g):
                p = g % 8
                pe.wait_ge(sem("d_at"), 2 * g + 2)
                pe.wait_ge(sem("d_st"), g + 1)
                pe.wait_ge(sem("d_qe"), g + 1)
                out = take(pe, 5, sem("d_o"), g + 1)
                for c in range(NT):
                    if c:
                        mm(out[:, c * P:(c + 1) * P], stD[g % 2][:, (c - 1) * P:c * P], qeD[g % 3][:, c * P:(c + 1) * P],
                           start=True, stop=False, skip_group_check=True)
                    for hh in range(2):
                        at = c * 256 + hh * P
                        m = mm(out[hh * DH:(hh + 1) * DH, c * P:(c + 1) * P],
                               v3(vD[p // 4], NT)[:, c, (p % 4) * P + hh * DH:(p % 4) * P + (hh + 1) * DH],
                               atD[g % 3][:, at:at + P], start=(c == 0), stop=True, skip_group_check=True)
                m.then_inc(sem("d_pv"), 1)

            def d_mean(k, i):
                pe.wait_ge(sem("d_gs"), 2 * k + i + 1)
                out = take_next(pe, ("d_gn", 2 * k + i), sem("d_gr"), 2 * k + i + 1)
                src = gnD[0][:, 4 * (k % 2):4 * (k % 2) + 4] if i == 0 else gnD[2][:, 0:4]
                mm(out[:, 0:4], block, src, start=True, stop=True).then_inc(sem("d_gp"), 1)

            def phase_d():
                loaded(pe, "D", DMA_COUNT["D"])
                d_alpha(0)
                for t in range(NT):
                    d_v(0, 0, t)
                d_sums(0)
                d_proj(0, 0)
                d_proj(0, 1)
                d_decays(0)
                for g in range(32 + 4):
                    b, s = g // 8, g % 8
                    if 1 <= g <= 32:
                        d_state(g - 1)
                    if g + 1 < 32:
                        d_proj(g + 1, 0)
                        d_proj(g + 1, 1)
                        d_decays(g + 1)
                    if g < 32:
                        d_scores(g)
                    if 1 <= g <= 32:
                        d_proj(g - 1, 2)
                    if g < 32:
                        d_kturn(g)
                    if 2 <= g < 34:
                        d_out(g - 2)
                    if s in (2, 6) and g >= 6:
                        d_mean((g - 6) // 4, 0)
                    if s in (3, 7) and g >= 7:
                        d_mean((g - 7) // 4, 1)
                    if g < 32:
                        tail(PD + b - 1, s)
                        if s in (2, 3):
                            d_v(b, 1, 2 * s - 4)
                            d_v(b, 1, 2 * s - 3)
                        if b + 1 < NB:
                            if s == 2:
                                d_alpha(b + 1)
                            if s == 4:
                                d_sums(b + 1)
                            if s in (6, 7):
                                d_v(b + 1, 0, 2 * s - 12)
                                d_v(b + 1, 0, 2 * s - 11)

            cross(1)
            moe(2)
            phase_d()
            cross(4)
            moe(5)
            for s in range(32):
                tail(WORKS - 1, s)

        @block_ctx.scalar
        def _(act):
            A = nc.scalar.activation
            chain = [0]

            def link(ins):
                chain[0] += 1
                ins.then_inc(act_chain, 1)
                act.wait_ge(act_chain, chain[0])

            def tail(w, s):
                ph, b = w // NB, w % NB
                at = tail_steps(w)
                if s == at[0]:
                    act.wait_ge(y_ready, w + 1)
                    if w:
                        act.wait_ge(yt_ready, w)
                    src = bank[5] if ph in (2, 5) else where["y", w]
                    if ph in (1, 4):
                        A(yT[:, :], src[:, :], ACT.Identity, bias=col("bo0" if ph == 1 else "bo1")).then_inc(yT_ready, 1)
                    else:
                        A(yT[:, :], src[:, :], ACT.Copy).then_inc(yT_ready, 1)
                if s == at[4] and w < PF:
                    act.wait_ge(xTp_ready, w + 1)
                    A(xT_all[:, b, :], where["xT", w][:, :], ACT.Copy).then_inc(xT_ready, 1)

            def a_norm_T(b):
                act.wait_ge(sem("a_xnp"), b + 1)
                if b >= 2:
                    act.wait_ge(sem("a_kp"), 8 * (b - 1))
                    act.wait_ge(sem("a_vp"), 8 * (b - 1))
                A(xnT[b % 2], where["a_xn", b][:, :], ACT.Identity, bias=col("ln_b"), scale=col("ln_g"))\
                    .then_inc(sem("a_xnT"), 1)

            def a_v(b, hf, t):
                n = 8 * b + 4 * hf + t
                act.wait_ge(sem("a_vp"), n + 1)
                if b and t == 0:
                    act.wait_ge(sem("a_pv"), 8 * b - 8 + 4 * hf + 4)
                A(v3(vA[hf], NT)[:, t, :], where["a_v", n][:, :], ACT.Copy).then_inc(sem("a_vs"), 1)

            def a_q(g):
                act.wait_ge(sem("a_qp"), g + 1)
                if g >= 2:
                    act.wait_ge(sem("a_s"), 8 * (g - 1))
                A(qTA[g % 2], where["a_qp", g][:, :], ACT.Copy, scale=0.125).then_inc(sem("a_qs"), 1)

            def a_exp(u):
                act.wait_ge(sem("a_mx"), u + 1)
                if u >= 4:
                    act.wait_ge(sem("a_t"), u - 3)
                A(pA[u % 4], bank[u % 3][:, :], ACT.Exp, bias=nmax[:, u % 8:u % 8 + 1],
                  accum_out=rsum[0][:, u % 8:u % 8 + 1]).then_inc(sem("a_e"), 1)

            def a_pt(u):
                h = u // 4
                act.wait_ge(sem("a_t"), u + 1)
                if u >= 16 and u % 8 == 0:
                    act.wait_ge(sem("a_pv"), u // 8 - 1)
                A(v3(ptA[h % 4], NT)[:, :, (u % 4) * P:(u % 4 + 1) * P], v3(bank[3 + u % 2][:, :], NT), ACT.Copy)\
                    .then_inc(sem("a_pt"), 1)

            loaded(act, "small", 7)
            a_norm_T(0)
            a_q(0)
            for t in range(NT):
                a_v(0, 0, t)
            NU = NB * UNITS
            for u in range(NU + 3):
                b, s, g, j = u // UNITS, u % UNITS, u // 8, u % 8
                if u < NU:
                    if b:
                        tail(b - 1, s)
                    if s == 24 and b + 1 < NB:
                        a_norm_T(b + 1)
                    if 48 <= s < 56 and s % 2 and b + 1 < NB:
                        a_v(b + 1, 0, (s - 48) // 2)
                    if 16 <= s < 24 and s % 2:
                        a_v(b, 1, (s - 16) // 2)
                    if j == 0 and g + 1 < 32:
                        a_q(g + 1)
                    a_exp(u)
                if u >= 3:
                    a_pt(u - 3)

            def cross_v(c):
                n = c["n"]
                nh = c["np"] * P // S
                act.wait_ge(sem(n + "_zero"), 2)
                for i in range(NB * nh):
                    act.wait_ge(sem(n + "_vp"), i + 1)
                    b, hf = i // nh, i % nh
                    A(v3(vcB, NB)[0:C, b, hf * S:(hf + 1) * S], where[n + "v", i][0:C, :], ACT.Copy)\
                        .then_inc(sem(n + "_vs"), 1)

            def cross_q(c, b):
                n, np_ = c["n"], c["np"]
                if b:
                    act.wait_ge(sem(n + "_s"), NT * b)
                for p in range(np_):
                    k = np_ * b + p
                    act.wait_ge(sem(n + "_qp"), k + 1)
                    src = where[n + "q", k][:, :]
                    if c["bias"]:
                        i = A(v3(qTB, NPAIR)[:, p, :], src, ACT.Identity, bias=col("bq", p))
                    else:
                        i = A(v3(qTB, NPAIR)[:, p, :], src, ACT.Copy)
                    i.then_inc(sem(n + "_qs"), 1)

            def cross_exp(c, b, t):
                n = c["n"]
                u = NT * b + t
                hs = 2 * c["np"]
                act.wait_ge(sem(n + "_sub"), u + 1)
                p = pB[u % 3][:, 0:hs * C]
                A(p, p, ACT.Exp, scale=0.125).then_inc(sem(n + "_e"), 1)

            def cross_pt(c, b, t):
                n = c["n"]
                nq = c["np"] * 2 // 4
                u = NT * b + t
                if t == 0 and b:
                    act.wait_ge(sem(n + "_pv"), c["np"] * b)
                for q in range(nq):
                    k = nq * u + q
                    act.wait_ge(sem(n + "_t"), k + 1)
                    A(v3(ptB, H)[:, 4 * q:4 * q + 4, t * P:(t + 1) * P], v3(bank[3 + k % 2][:, :], NT), ACT.Copy)\
                        .then_inc(sem(n + "_pt"), 1)

            def cross(ph):
                c = CROSS[ph]
                n, w0 = c["n"], c["w0"]
                if ph == 4:
                    enter(act, ph)
                cross_q(c, 0)
                if ph == 1:
                    enter(act, ph)
                cross_v(c)
                for u in range(NB * NT + 3):
                    b, t = u // NT, u % NT
                    if b < NB and t == 3 and b + 1 < NB:
                        cross_q(c, b + 1)
                    if u < NT:
                        for s in range(3 * u, 3 * u + 3):
                            tail(w0 - 1, s)
                    cross_tail(tail, w0, u)
                    if b < NB:
                        cross_exp(c, b, t)
                    if 2 <= u < NB * NT + 2:
                        cross_pt(c, (u - 2) // NT, (u - 2) % NT)

            def moe_exp(m_, b):
                n = m_["n"]
                act.wait_ge(sem(n + "_d"), b + 1)
                if n == "C":
                    A(lnv[:, 4, :], lnv[:, 3, :], ACT.Exp).then_inc(sem(n + "_e"), 1)
                else:
                    A(rt[:, 2, :, :], rt[:, 1, :, :], ACT.Exp).then_inc(sem(n + "_e"), 1)

            def moe(ph):
                m_ = MOE[ph]
                n, ft = m_["n"], m_["ft"]
                steps = E * ft
                moe_exp(m_, 0)
                enter(act, ph)
                for i in range(NB * steps):
                    b, s = i // steps, i % steps
                    tail(m_["w0"] + b - 1, s)
                    if s == 13 and b + 1 < NB:
                        moe_exp(m_, b + 1)
                    act.wait_ge(sem(n + "_hp"), i + 1)
                    if i >= 3:
                        act.wait_ge(sem(n + "_hw"), i - 2)
                    A(hsC[i % 3], bank[i % 3][:, :], m_["func"], bias=col(m_["b1"], s)).then_inc(sem(n + "_h"), 1)

            def d_softplus(b):
                act.wait_ge(sem("d_az"), b + 1)
                link(A(spD[2], spD[1], ACT.Exp, scale=-1.0))
                A(spD[2], spD[2], ACT.Ln, bias=1.0).then_inc(sem("d_ln"), 1)

            def d_kdec(b):
                act.wait_ge(sem("d_lcs"), b + 1)
                if b >= 2:
                    act.wait_ge(sem("d_kd"), 8 * (b - 1))
                A(kdecD[b % 2], lcD[b % 2][:, 64:128], ACT.Exp, scale=-1.0).then_inc(sem("d_kdec"), 1)

            def d_v(b, hf, t):
                n = 8 * b + 4 * hf + t
                act.wait_ge(sem("d_vp"), n + 1)
                if b and t == 0:
                    act.wait_ge(sem("d_pv"), 8 * b - 8 + 4 * hf + 4)
                A(v3(vD[hf], NT)[:, t, :], where["d_v", n][:, :], ACT.Copy).then_inc(sem("d_vs"), 1)

            def d_decays(g):
                b, p = g // 8, g % 8
                act.wait_ge(sem("d_lp"), g + 1)
                if g >= 3:
                    act.wait_ge(sem("d_st"), g - 2)
                    act.wait_ge(sem("d_qe"), g - 2)
                A(elD[g % 3], bank[0][:, :], ACT.Exp, scale=-1.0).then_inc(sem("d_el"), 1)
                if p == 0:
                    act.wait_ge(sem("d_lcs"), b + 1)
                if g >= 2:
                    act.wait_ge(sem("d_at"), 2 * (g - 1))
                for hh in range(2):
                    act.wait_ge(sem("d_la"), 2 * g + hh + 1)
                    for c in range(NT):
                        k = c * H + 2 * p + hh
                        i = A(dmD[g % 2][:, (2 * c + hh) * P:(2 * c + hh + 1) * P], bank[1 - hh][:, c * P:(c + 1) * P],
                              ACT.Exp, scale=-1.0, bias=lcD[b % 2][:, k:k + 1])
                    i.then_inc(sem("d_dm"), 1)

            def d_tanh(g, i):
                src = where["d_p", g, i][:, :]
                if i < 2:
                    act.wait_ge(sem("d_pp"), 2 * g + i + 1)
                    if g:
                        act.wait_ge(sem("d_silu"), 2 * g - 1 + i)
                    A(tqD[i], src, ACT.Tanh, scale=0.5).then_inc(sem("d_tq"), 1)
                else:
                    act.wait_ge(sem("d_gp_"), g + 1)
                    if g >= 8:
                        act.wait_ge(sem("d_og"), g - 7)
                    A(thD[g % 8], src, ACT.Tanh, scale=0.5).then_inc(sem("d_th"), 1)

            def d_o(g):
                act.wait_ge(sem("d_pv"), g + 1)
                act.wait_ge(sem("d_bs"), g + 1)
                if g >= 12:
                    act.wait_ge(y_ready, PD + (g - 12) // 8 + 1)
                elif g == 0:
                    act.wait_ge(y_ready, PB + 4)
                A(o_slot(PD + g // 8, g % 8), bank[5][:, :], ACT.Copy).then_inc(sem("d_o"), 1)

            def phase_d():
                enter(act, 3)
                d_softplus(0)
                for t in range(NT):
                    d_v(0, 0, t)
                d_kdec(0)
                d_tanh(0, 0)
                d_tanh(0, 1)
                d_decays(0)
                for g in range(32 + 4):
                    b, s = g // 8, g % 8
                    if g + 1 < 32:
                        d_tanh(g + 1, 0)
                        d_tanh(g + 1, 1)
                        d_decays(g + 1)
                    if 1 <= g <= 32:
                        d_tanh(g - 1, 2)
                    if 2 <= g < 34:
                        d_o(g - 2)
                    if g < 32:
                        tail(PD + b - 1, s)
                        if s in (2, 3):
                            d_v(b, 1, 2 * s - 4)
                            d_v(b, 1, 2 * s - 3)
                        if b + 1 < NB:
                            if s == 2:
                                d_softplus(b + 1)
                            if s == 4:
                                d_kdec(b + 1)
                            if s in (6, 7):
                                d_v(b + 1, 0, 2 * s - 12)
                                d_v(b + 1, 0, 2 * s - 11)

            cross(1)
            moe(2)
            phase_d()
            cross(4)
            moe(5)
            for s in range(32):
                tail(WORKS - 1, s)

        @block_ctx.vector
        def _(dve):
            V = nc.vector
            chain = [0]

            def link(ins):
                chain[0] += 1
                ins.then_inc(dve_chain, 1)
                dve.wait_ge(dve_chain, chain[0])

            def ln_stats(src):
                for t in range(NT):
                    i = V.bn_stats(bn[:, t, :], src[:, t, :])
                link(i)
                for t in range(NT):
                    i = V.bn_aggr(mv[:, t, :], bn[:, t, :])
                link(i)
                link(V.tensor_scalar(lnv[:, 0, :], mv[:, :, 1], EPS, None, ALU.add))

            def rsqrt(var, tmp, y):
                link(V.tensor_scalar(tmp.bitcast(U32), var.bitcast(U32), 1, None, ALU.logical_shift_right))
                link(V.tensor_scalar(y.bitcast(U32), tmp.bitcast(U32), -1.0, 1597463007.0, ALU.mult, ALU.add))
                for _ in range(4):
                    link(V.tensor_tensor(tmp, y, y, ALU.mult))
                    link(V.scalar_tensor_tensor(out=tmp, in0=tmp, scalar=-0.5, in1=var, op0=ALU.mult, op1=ALU.mult))
                    link(V.scalar_tensor_tensor(out=y, in0=tmp, scalar=1.5, in1=y, op0=ALU.add, op1=ALU.mult))

            def ln_apply(src, dst):
                rsqrt(lnv[:, 0, :], lnv[:, 2, :], lnv[:, 1, :])
                for t in range(NT):
                    i = V.tensor_scalar(dst[:, t, :], src[:, t, :], mv[:, t, 0:1], lnv[:, 1, t:t + 1],
                                        ALU.subtract, ALU.mult)
                return i

            def tail(w, s):
                ph, b = w // NB, w % NB
                at = tail_steps(w)
                x = x_all[:, 4 * b:4 * b + 4, :]
                if s == at[1]:
                    dve.wait_ge(yt_ready, w + 1)
                    V.tensor_tensor(res[:, :, :], x, v3(where["yt", w][:, :], NT), ALU.add).then_inc(sem("sum_done"), 1)
                    dve.wait_ge(sem("sum_done"), w + 1)
                    ln_stats(res)
                if ph == 1:
                    if s == at[2]:
                        link(ln_apply(res, res))
                        g, bb = (rows[:, ROWS[k][0]:ROWS[k][1]].unsqueeze(1).to_broadcast([P, NT, D]) for k in ("xg", "xb"))
                        link(V.tensor_tensor(res[:, :, :], res[:, :, :], g, ALU.mult))
                        link(V.tensor_tensor(res[:, :, :], res[:, :, :], bb, ALU.add))
                        link(V.tensor_tensor(res[:, :, :], res[:, :, :], x, ALU.add))
                        ln_stats(res)
                    if s == at[3]:
                        ln_apply(res, x).then_inc(x_ready, 1)
                elif s == at[2]:
                    ln_apply(res, x).then_inc(x_ready, 1)

            def split_rows(src, n, dst):
                link(V.tensor_copy(dst[0:n, :], src))
                link(V.tensor_tensor(spl_r[0:n, :], src, dst[0:n, :], ALU.subtract))
                link(V.tensor_copy(spl_m[0:n, :], spl_r[0:n, :]))
                V.tensor_copy(dst[32:32 + n, :], spl_m[0:n, :])
                return V.tensor_tensor(dst[64:64 + n, :], spl_r[0:n, :], spl_m[0:n, :], ALU.subtract)

            def a_k(g):
                dve.wait_ge(sem("a_kp"), g + 1)
                if g >= 2:
                    dve.wait_ge(sem("a_s"), 8 * (g - 1))
                src = where["a_kp", g]
                V.tensor_copy(kzA[g % 2][0:DH, 0:S], src[0:DH, :])
                V.tensor_copy(kzA[g % 2][DH:P, S:2 * S], src[DH:P, :]).then_inc(sem("a_ks"), 1)

            def a_max(u):
                dve.wait_ge(sem("a_s"), u + 1)
                if u >= 8:
                    dve.wait_ge(sem("a_e"), u - 7)
                V.tensor_reduce(nmax[:, u % 8:u % 8 + 1], bank[u % 3][:, :], AX, ALU.max, negate=True)\
                    .then_inc(sem("a_mx"), 1)

            def a_norm(u):
                r = slice(u % 8, u % 8 + 1)
                dve.wait_ge(sem("a_e"), u + 1)
                if u >= 8:
                    dve.wait_ge(sem("a_n"), u - 7)
                V.reciprocal(rsum[1][:, r], rsum[0][:, r]).then_inc(sem("a_r"), 1)

            def a_o(g):
                b = g // 8
                dve.wait_ge(sem("a_pv"), g + 1)
                if b and g % 8 == 0:
                    dve.wait_ge(y_ready, b)
                V.tensor_copy(OT[:, g % 8, :], bank[5][:, :]).then_inc(sem("a_o"), 1)

            loaded(dve, "small", 7)
            V.tensor_copy(ident_b[:, :], ident)
            V.tensor_copy(sel[:, :], work[:, 26000:26016])
            V.tensor_copy(heads[:, :], work[:, 26528:26530])
            V.tensor_copy(mask[:, :], work[:, 26016:26528]).then_inc(consts_ready, 1)
            loaded(dve, "x", 4)
            ln_stats(x_all[:, 0:4, :])
            ln_apply(x_all[:, 0:4, :], v3(xn, NT)).then_inc(sem("a_xn"), 1)
            dve.wait_ge(sem("a_zero"), 1)
            a_k(0)
            NU = NB * UNITS
            for u in range(NU + 1):
                b, s, g, j = u // UNITS, u % UNITS, u // 8, u % 8
                if u < NU:
                    if b:
                        tail(b - 1, s)
                    if b + 1 < NB and s == 22:
                        ln_stats(x_all[:, 4 * b + 4:4 * b + 8, :])
                    if b + 1 < NB and s == 23:
                        dve.wait_ge(sem("a_xnp"), b + 1)
                        ln_apply(x_all[:, 4 * b + 4:4 * b + 8, :], v3(xn, NT)).then_inc(sem("a_xn"), 1)
                    if j == 1 and g + 1 < 32:
                        a_k(g + 1)
                    a_max(u)
                if 1 <= u < NU + 1:
                    a_norm(u - 1)
                if j == 0 and g >= 2:
                    a_o(g - 2)
            a_o(31)

            def cross_k(c):
                n = c["n"]
                dve.wait_ge(sem(n + "_zero"), 1)
                kd = kdB.rearrange("p (q b h c) -> p q b h c", q=NPAIR, b=NB, h=2)
                for p in range(c["np"]):
                    dve.wait_ge(sem(n + "_kp"), p + 1)
                    src = where[n + "k", p]
                    for hh in range(2):
                        r = slice(hh * DH, (hh + 1) * DH)
                        s_ = src[r, 0:NB * C].rearrange("p (b c) -> p b c", b=NB)
                        if c["bias"]:
                            i = V.tensor_scalar(kd[r, p, :, hh, :], s_, col("bk", p)[r, :], None, ALU.add)
                        else:
                            i = V.tensor_copy(kd[r, p, :, hh, :], s_)
                    i.then_inc(sem(n + "_ks"), 1)

            def cross_sub(c, b, t):
                n, np_ = c["n"], c["np"]
                u = NT * b + t
                dve.wait_ge(sem(n + "_s"), u + 1)
                m = statB[u % 2]
                parts = [(q, min(3, np_ - 3 * q)) for q in range((np_ + 2) // 3)]
                for q, k in parts:
                    i = V.tensor_reduce(m[:, 6 * q:6 * q + 2 * k], v3(bank[q][:, 0:2 * k * C], 2 * k), AX, ALU.max)
                link(i)
                if u >= 3:
                    dve.wait_ge(sem(n + "_t"), (np_ // 2) * (u - 2))
                for q, k in parts:
                    i = V.tensor_tensor(v3(pB[u % 3][:, 0:H * C], H)[:, 6 * q:6 * q + 2 * k, :], v3(bank[q][:, 0:2 * k * C], 2 * k),
                                        m[:, 6 * q:6 * q + 2 * k].unsqueeze(2).to_broadcast([P, 2 * k, C]), ALU.subtract)
                i.then_inc(sem(n + "_sub"), 1)

            def cross_norm(c, b, t):
                n, hs = c["n"], 2 * c["np"]
                u = NT * b + t
                dve.wait_ge(sem(n + "_e"), u + 1)
                p = v3(pB[u % 3][:, 0:hs * C], hs)
                if u < 3:
                    dve.wait_ge(sem(n + "_zero"), 3)
                link(V.tensor_reduce(statB[2][:, 0:hs], p, AX, ALU.add))
                link(V.reciprocal(statB[3][:, 0:hs], statB[2][:, 0:hs]))
                V.tensor_tensor(p, p, statB[3][:, 0:hs].unsqueeze(2).to_broadcast([P, hs, C]), ALU.mult)\
                    .then_inc(sem(n + "_n"), 1)

            def cross_o(c, b):
                n, np_ = c["n"], c["np"]
                w = c["w0"] + b
                dve.wait_ge(y_ready, w)
                for p in range(np_):
                    k = np_ * b + p
                    dve.wait_ge(sem(n + "_pv"), k + 1)
                    src = where[n + "o", k][:, :]
                    if c["bias"]:
                        i = V.tensor_scalar(OT[:, p, :], src, col("bv", p), None, ALU.add)
                    else:
                        i = V.tensor_copy(OT[:, p, :], src)
                    i.then_inc(sem(n + "_o"), 1)

            def cross(ph):
                c = CROSS[ph]
                n, w0 = c["n"], c["w0"]
                enter(dve, ph)
                cross_k(c)
                for u in range(NB * NT + 3):
                    b, t = u // NT, u % NT
                    if b < NB:
                        cross_sub(c, b, t)
                    if u < NT:
                        for s in range(3 * u, 3 * u + 3):
                            tail(w0 - 1, s)
                    cross_tail(tail, w0, u)
                    if 1 <= u < NB * NT + 1:
                        cross_norm(c, (u - 1) // NT, (u - 1) % NT)
                    if t == 1 and b >= 1:
                        cross_o(c, b - 1)
                    if u == NB * NT + 1:
                        moe_route1(MOE[ph + 1], 0)

            def bc(ap):
                return ap.to_broadcast([P, 4, 8])

            def moe_route1(m_, b):
                n = m_["n"]
                dve.wait_ge(sem(n + "_lgp"), b + 1)
                lg = rt[:, 0, :, :]
                src = v3(where[n + "lg", b][:, 0:4 * E], 4)
                if n == "C":
                    V.tensor_copy(lg, src).then_inc(sem(n + "_lg"), 1)
                    dve.wait_ge(sem(n + "_lg"), b + 1)
                    for t in range(NT):
                        i = V.max(out=rt[:, 1, t, :], in_=rt[:, 0, t, :])
                    link(i)
                    V.tensor_tensor(lnv[:, 3, :], rt[:, 1, :, 1], rt[:, 1, :, 0], ALU.subtract).then_inc(sem(n + "_d"), 1)
                    for t in range(NT):
                        i = V.max_index(out=ri[:, t, :], in_max=rt[:, 1, t, :], in_values=rt[:, 0, t, :])
                    link(i)
                    link(V.tensor_copy(rt[:, 3, :, :], ri[:, :, :]))
                else:
                    br = rows[:, ROWS["br"][0]:ROWS["br"][1]].unsqueeze(1).to_broadcast([P, 4, 8])
                    V.tensor_tensor(lg, src, br, ALU.add).then_inc(sem(n + "_lg"), 1)
                    dve.wait_ge(sem(n + "_lg"), b + 1)
                    link(V.tensor_reduce(rt[:, 3, :, 0], lg, AX, ALU.max))
                    V.tensor_tensor(rt[:, 1, :, :], lg, bc(rt[:, 3, :, 0:1]), ALU.subtract).then_inc(sem(n + "_d"), 1)

            def moe_route2(m_, b):
                n = m_["n"]
                dve.wait_ge(sem(n + "_e"), b + 1)
                if b:
                    dve.wait_ge(sem(n + "_wTp"), b)
                io = iota.unsqueeze(1).to_broadcast([P, 4, 8])
                if n == "C":
                    e = lnv[:, 4, :]
                    link(V.tensor_scalar(rt[:, 4, :, 0], e, 1.0, None, ALU.add))
                    link(V.reciprocal(rt[:, 5, :, 0], rt[:, 4, :, 0]))
                    link(V.tensor_tensor(rt[:, 5, :, 1], rt[:, 5, :, 0], e, ALU.mult))
                    for k in range(2):
                        link(V.tensor_tensor(rt[:, 6 + k, :, :], io, bc(rt[:, 3, :, k:k + 1]), ALU.is_equal))
                        link(V.tensor_tensor(rt[:, 8 + k, :, :], rt[:, 6 + k, :, :], bc(rt[:, 5, :, k:k + 1]), ALU.mult))
                    V.tensor_tensor(rt[:, 11, :, :], rt[:, 8, :, :], rt[:, 9, :, :], ALU.add).then_inc(sem(n + "_wt"), 1)
                else:
                    link(V.tensor_reduce(rt[:, 4, :, 0], rt[:, 2, :, :], AX, ALU.add))
                    link(V.reciprocal(rt[:, 5, :, 0], rt[:, 4, :, 0]))
                    link(V.tensor_tensor(rt[:, 6, :, :], rt[:, 2, :, :], bc(rt[:, 5, :, 0:1]), ALU.mult))
                    for t in range(NT):
                        i = V.max(out=rt[:, 7, t, :], in_=rt[:, 6, t, :])
                    link(i)
                    for t in range(NT):
                        i = V.max_index(out=ri[:, t, :], in_max=rt[:, 7, t, :], in_values=rt[:, 6, t, :])
                    link(i)
                    link(V.tensor_copy(rt[:, 8, :, :], ri[:, :, :]))
                    link(V.tensor_tensor(rt[:, 9, :, :], io, bc(rt[:, 8, :, 0:1]), ALU.is_equal))
                    V.tensor_tensor(rt[:, 11, :, :], rt[:, 9, :, :], bc(rt[:, 7, :, 0:1]), ALU.mult)\
                        .then_inc(sem(n + "_wt"), 1)

            def moe_route3(m_, b):
                n = m_["n"]
                dve.wait_ge(sem(n + "_wTp"), b + 1)
                src = where[n + "wT", b][0:E, :]
                V.tensor_copy(wT_C[0:E, (b % 2) * S:(b % 2 + 1) * S], src)
                if n == "C":
                    dve.wait_ge(sem("C_zero"), 1)
                split_rows(src, E, wsel_b[b % 2]).then_inc(sem(n + "_sel"), 1)

            def moe(ph):
                m_ = MOE[ph]
                n, ft = m_["n"], m_["ft"]
                steps = E * ft
                moe_route2(m_, 0)
                enter(dve, ph)
                moe_route3(m_, 0)
                for i in range(NB * steps):
                    b, s = i // steps, i % steps
                    tail(m_["w0"] + b - 1, s)
                    if b + 1 < NB:
                        if s == 12:
                            moe_route1(m_, b + 1)
                        if s == 14:
                            moe_route2(m_, b + 1)
                        if s == 15:
                            moe_route3(m_, b + 1)
                    dve.wait_ge(sem(n + "_h"), i + 1)
                    dve.wait_ge(sem(n + "_wb"), i // ft + 1)
                    if i >= 3:
                        k = i - 3
                        if k % steps == steps - 1:
                            dve.wait_ge(y_ready, m_["w0"] + k // steps + 1)
                        else:
                            dve.wait_ge(sem(n + "_c"), k + 1 - k // steps)
                    V.tensor_tensor(hwC[i % 3], hsC[i % 3], bank[3 + (s // ft) % 2][:, :], ALU.mult)\
                        .then_inc(sem(n + "_hw"), 1)

            def d_z(b):
                dve.wait_ge(sem("d_al"), b + 1)
                ba = rows[:, ROWS["ba"][0]:ROWS["ba"][1]].unsqueeze(1).to_broadcast([P, NT, H])
                V.tensor_tensor(v3(spD[0], NT), v3(where["d_al", b][:, 0:64], NT), ba, ALU.add).then_inc(sem("d_z"), 1)
                dve.wait_ge(sem("d_z"), b + 1)
                link(V.tensor_scalar(spD[1], spD[0], -1.0, None, ALU.mult))
                V.tensor_tensor(spD[1], spD[1], spD[0], ALU.max).then_inc(sem("d_az"), 1)

            def d_sp(b):
                dve.wait_ge(sem("d_ln"), b + 1)
                V.scalar_tensor_tensor(out=spD[3], in0=spD[0], scalar=0.0, in1=spD[2], op0=ALU.max, op1=ALU.add)\
                    .then_inc(sem("d_sp"), 1)

            def d_lsel(b):
                dve.wait_ge(sem("d_LT"), b + 1)
                split_rows(where["d_LT", b][0:H, :], H, lsel_b[b % 2]).then_inc(sem("d_lsel"), 1)
                dve.wait_ge(sem("d_lcp"), b + 1)
                V.tensor_copy(lcD[b % 2], where["d_lc", b][:, 0:128]).then_inc(sem("d_lcs"), 1)

            def d_silu(g, i):
                dve.wait_ge(sem("d_tq"), 2 * g + i + 1)
                if g >= 2:
                    dve.wait_ge(sem("d_s"), 2 * (g - 1))
                    if i:
                        dve.wait_ge(sem("d_kt"), g - 1)
                    else:
                        dve.wait_ge(sem("d_qe"), g - 1)
                th = tqD[i]
                out = qTD[g % 2] if i == 0 else kTD[g % 2]
                V.scalar_tensor_tensor(out=out, in0=th, scalar=1.0, in1=where["d_p", g, i][:, :],
                                       op0=ALU.add, op1=ALU.mult).then_inc(sem("d_silu"), 1)

            def d_kd(g):
                b, p = g // 8, g % 8
                dve.wait_ge(sem("d_kt"), g + 1)
                dve.wait_ge(sem("d_kdec"), b + 1)
                if g >= 2:
                    dve.wait_ge(sem("d_dl"), g - 1)
                kdec = v3(kdecD[b % 2], NT)[:, :, 2 * p:2 * p + 2].unsqueeze(3).to_broadcast([P, NT, 2, DH])
                V.tensor_tensor(kdD[g % 2].rearrange("p (c h d) -> p c h d", c=NT, h=2),
                                bank[4][:, :].rearrange("p (c h d) -> p c h d", c=NT, h=2), kdec, ALU.mult)\
                    .then_inc(sem("d_kd"), 1)

            def d_at(g):
                dve.wait_ge(sem("d_dm"), 2 * g + 2)
                if g >= 3:
                    dve.wait_ge(sem("d_pv"), g - 2)
                for c2 in range(2):
                    dve.wait_ge(sem("d_s"), 2 * g + c2 + 1)
                    r = slice(c2 * S, (c2 + 1) * S)
                    V.scalar_tensor_tensor(out=atD[g % 3][:, r], in0=bank[2 + c2][:, :], scalar=0.25, in1=dmD[g % 2][:, r],
                                           op0=ALU.mult, op1=ALU.mult).then_inc(sem("d_at"), 1)

            def d_st(g):
                dve.wait_ge(sem("d_dl"), g + 1)
                dve.wait_ge(sem("d_el"), g + 1)
                if g >= 2:
                    dve.wait_ge(sem("d_pv"), g - 1)
                st, el = v3(stD[g % 2], NT - 1), elD[g % 3]
                halves = [slice(hh * DH, (hh + 1) * DH) for hh in range(2)]
                for r in halves:
                    i = V.tensor_scalar(st[r, :, r], v3(bank[4][:, 0:3 * P], NT - 1)[r, :, r], 0.25, None, ALU.mult)
                link(i)
                for c in (1, 2):
                    for r in halves:
                        i = V.scalar_tensor_tensor(out=st[r, c, r], in0=st[r, c - 1, r], scalar=el[r, c * P + P - 1:c * P + P],
                                                   in1=st[r, c, r], op0=ALU.mult, op1=ALU.add)
                    if c == 1:
                        link(i)
                i.then_inc(sem("d_st"), 1)

            def d_stats(g):
                dve.wait_ge(sem("d_pv"), g + 1)
                V.bn_stats(gn6[:, 0:6], bank[5][:, :]).then_inc(sem("d_bs"), 1)
                dve.wait_ge(sem("d_bs"), g + 1)
                i = V.bn_aggr(gnD[6][:, 0:2], gn6[:, 0:6])
                link(i)
                k = g % 8
                V.tensor_copy(gnD[0][:, k:k + 1], gnD[6][:, 0:1])
                i = V.tensor_copy(gnD[1][:, k:k + 1], gnD[6][:, 1:2])
                if g % 4 == 3:
                    i.then_inc(sem("d_gs"), 1)
                else:
                    link(i)

            def d_spread(k):
                dve.wait_ge(sem("d_gp"), 2 * k + 1)
                dve.wait_ge(sem("d_gs"), 2 * k + 1)
                V.tensor_copy(gnD[7][:, 0:4], where["d_gn", 2 * k][:, 0:4]).then_inc(sem("d_gr"), 1)
                dve.wait_ge(sem("d_gr"), 2 * k + 1)
                r = slice(4 * (k % 2), 4 * (k % 2) + 4)
                link(V.tensor_tensor(gnD[2][:, 0:4], gnD[0][:, r], gnD[7][:, 0:4], ALU.subtract))
                link(V.tensor_tensor(gnD[2][:, 0:4], gnD[2][:, 0:4], gnD[2][:, 0:4], ALU.mult))
                V.tensor_tensor(gnD[2][:, 0:4], gnD[2][:, 0:4], gnD[1][:, r], ALU.add).then_inc(sem("d_gs"), 1)

            def d_gate(k):
                b, p0 = k // 2, 4 * (k % 2)
                dve.wait_ge(sem("d_gp"), 2 * k + 2)
                V.tensor_scalar(gnD[3][:, 0:4], where["d_gn", 2 * k + 1][:, 0:4], EPS, None, ALU.add)\
                    .then_inc(sem("d_gr"), 1)
                dve.wait_ge(sem("d_gr"), 2 * k + 2)
                rsqrt(gnD[3][:, 0:4], gnD[4][:, 8:12], gnD[6][:, 8:12])
                gw, gb = (cols[:, COLS[n][0] + p0:COLS[n][0] + p0 + 4] for n in ("gn_w", "gn_b"))
                A_, B_ = gnD[6][:, 12:16], gnD[5][:, 8:12]
                link(V.scalar_tensor_tensor(out=A_, in0=gw, scalar=0.5, in1=gnD[6][:, 8:12], op0=ALU.mult, op1=ALU.mult))
                link(V.tensor_tensor(B_, gnD[7][:, 0:4], A_, ALU.mult))
                link(V.scalar_tensor_tensor(out=B_, in0=gb, scalar=0.5, in1=B_, op0=ALU.mult, op1=ALU.subtract))
                dve.wait_ge(sem("d_o"), 4 * k + 4)
                dve.wait_ge(sem("d_th"), 4 * k + 4)
                outs = [o_slot(PD + b, p0 + i) for i in range(4)]
                for i, o in enumerate(outs):
                    m = V.tensor_scalar(o, o, A_[:, i:i + 1], B_[:, i:i + 1], ALU.mult, ALU.add)
                link(m)
                for i, o in enumerate(outs):
                    V.scalar_tensor_tensor(out=o, in0=thD[p0 + i], scalar=1.0, in1=o, op0=ALU.add, op1=ALU.mult)\
                        .then_inc(sem("d_og"), 1)

            def phase_d():
                enter(dve, 3)
                dve.wait_ge(sem("d_zero"), 1)
                d_z(0)
                d_sp(0)
                d_lsel(0)
                d_silu(0, 0)
                d_silu(0, 1)
                for g in range(32 + 4):
                    b, s = g // 8, g % 8
                    if 1 <= g <= 32:
                        d_st(g - 1)
                    if g + 1 < 32:
                        d_silu(g + 1, 0)
                        d_silu(g + 1, 1)
                    if g < 32:
                        d_at(g)
                        d_kd(g)
                    if 2 <= g < 34:
                        d_stats(g - 2)
                    if s in (2, 6) and g >= 6:
                        d_spread((g - 6) // 4)
                    if s in (3, 7) and g >= 7:
                        d_gate((g - 7) // 4)
                    if g < 32:
                        tail(PD + b - 1, s)
                        if b + 1 < NB:
                            if s == 2:
                                d_z(b + 1)
                                d_sp(b + 1)
                            if s == 4:
                                d_lsel(b + 1)

            cross(1)
            moe(2)
            phase_d()
            cross(4)
            moe(5)
            for s in range(32):
                tail(WORKS - 1, s)

        @block_ctx.gpsimd
        def _(pool):
            G = nc.gpsimd
            chain = [0]

            def link(ins):
                chain[0] += 1
                ins.then_inc(pool_chain, 1)
                pool.wait_ge(pool_chain, chain[0])

            G.memset(kzA[0], 0.0)
            G.memset(kzA[1], 0.0).then_inc(sem("a_zero"), 1)
            pool.wait_ge(consts_ready, 1)
            G.memset(wselC, 0.0).then_inc(sem("C_zero"), 1)
            for u in range(NB * UNITS):
                pool.wait_ge(sem("a_r"), u + 1)
                G.tensor_tensor(pA[u % 4], pA[u % 4], rsum[1][:, u % 8:u % 8 + 1].to_broadcast([P, S]), ALU.mult)\
                    .then_inc(sem("a_n"), 1)

            def cross(ph):
                c = CROSS[ph]
                n = c["n"]
                if ph == 1:
                    pool.wait_ge(sem("a_pt"), NB * UNITS)
                else:
                    enter(pool, ph)
                kd = kdB.rearrange("p (q b h c) -> p q b h c", q=NPAIR, b=NB, h=2)
                link(G.memset(kd[0:DH, 0:c["np"], :, 1, :], 0.0))
                G.memset(kd[DH:P, 0:c["np"], :, 0, :], 0.0).then_inc(sem(n + "_zero"), 1)
                if ph == 1:
                    enter(pool, ph)
                G.memset(vcB[DH:P, :], 0.0).then_inc(sem(n + "_zero"), 1)
                pool.wait_ge(sem(n + "_zero"), 2)
                if ph == 4:
                    G.memset(wselC, 0.0)
                for i in range(3):
                    z = G.memset(pB[i][:, 2 * c["np"] * C:2 * c["np"] * C + P - C], 0.0)
                z.then_inc(sem(n + "_zero"), 1)

            def phase_d():
                enter(pool, 3)
                G.memset(lselD, 0.0)
                for i in range(2):
                    z = G.memset(stD[i], 0.0)
                z.then_inc(sem("d_zero"), 1)
                for g in range(32):
                    pool.wait_ge(sem("d_silu"), 2 * g + 1)
                    if g >= 2:
                        pool.wait_ge(sem("d_s"), 2 * (g - 1))
                    q = v3(qTD[g % 2], NT).unsqueeze(2).to_broadcast([P, NT, 2, P])
                    own = heads[:, :].unsqueeze(1).unsqueeze(3).to_broadcast([P, NT, 2, P])
                    G.tensor_tensor(qbD[g % 2].rearrange("p (c h i) -> p c h i", c=NT, h=2), q, own, ALU.mult)\
                        .then_inc(sem("d_qb"), 1)
                    pool.wait_ge(sem("d_el"), g + 1)
                    if g >= 3:
                        pool.wait_ge(sem("d_pv"), g - 2)
                    G.tensor_tensor(qeD[g % 3], qTD[g % 2], elD[g % 3], ALU.mult).then_inc(sem("d_qe"), 1)

            cross(1)
            phase_d()
            cross(4)


def kernel(**inputs):
    import numpy as np
    import concourse.bacc as bacc
    from concourse.bass_utils import run_bass_kernel_spmd

    I = {k: np.asarray(v) for k, v in inputs.items()}

    def by_partition(v, n):
        return v.reshape(n, P).T

    arrays = {"x": I["x"]}
    arrays["ctxT"] = I["ctx_1024"].reshape(NB * C, D).T
    for k in ("L0_attn_Wq", "L0_attn_Wk", "L0_attn_Wv", "L0_attn_Wo", "L0_xattn_Wq", "L0_xattn_Wk", "L0_xattn_Wv",
              "L0_xattn_Wo", "L1_attn_Wq", "L1_attn_Wk", "L1_attn_Wv", "L1_attn_Wg", "L1_attn_Wo", "L1_xattn_Wq",
              "L1_xattn_Wk", "L1_xattn_Wv", "L1_xattn_Wo", "L1_ffn_W1", "L1_ffn_W2", "L0_ffn_b2", "L1_ffn_b2"):
        arrays[k] = I[k]
    arrays["w1T"] = I["L0_ffn_w1"].reshape(E * FT0 * P, D).T
    arrays["w2T"] = I["L0_ffn_w2"].transpose(0, 2, 1).reshape(E * FT0 * P, D)
    arrays["cols"] = np.concatenate([by_partition(I[k], n) for k, n in (
        ("L0_attn_ln_gamma", 1), ("L0_attn_ln_beta", 1), ("L0_xattn_bq", 8), ("L0_xattn_bk", 8), ("L0_xattn_bv", 8),
        ("L0_xattn_bo", 1), ("L0_ffn_b1", 32), ("L1_attn_gn_w", 8), ("L1_attn_gn_b", 8), ("L1_xattn_bo", 1),
        ("L1_ffn_b1", 16))], axis=1)
    arrays["rows"] = np.concatenate([I["L0_xattn_ln_gamma"], I["L0_xattn_ln_beta"], I["L1_attn_ba"], I["L1_ffn_br"]])
    arrays["narrow"] = np.concatenate([I["L0_ffn_router_w"].T, I["L1_ffn_Wr"], I["L1_attn_Wa"]], axis=1)

    i = np.arange(P)
    c = np.zeros((P, NCONSTS), np.float32)
    c[:, 0:128] = np.eye(P)
    c[:, 128:256] = i[:, None] <= i[None, :]
    c[:, 256:384] = i[:, None] > i[None, :]
    c[:, 384:512] = (i[:, None] // DH == i[None, :] // DH) * (1.0 / DH)
    c[:, 512:520] = np.arange(E)
    for h in range(H):
        c[[h, 32 + h, 64 + h], 520 + h] = 1.0
    c[:, 536:1048] = np.tile((i[:, None] > i[None, :]) * 1e30, (1, NT))
    c[:, 1048:1050] = i[:, None] // DH == np.arange(2)[None, :]
    arrays["consts"] = c

    nc = bacc.Bacc("TRN2", target_bir_lowering=False, num_devices=1)
    T = {}
    feed = {}
    for k, a in arrays.items():
        a = np.ascontiguousarray(a)
        feed[f"in_{k}"] = a
        T[k] = nc.dram_tensor(f"in_{k}", a.shape, mybir.dt.from_np(a.dtype), kind="ExternalInput").ap()
    T["out"] = nc.dram_tensor("out_0", (NB, S, D), F32, kind="ExternalOutput").ap()
    decoder(nc, T)
    r = run_bass_kernel_spmd(nc, [feed], core_ids=[0])
    return r.results[0]["out_0"]
```

```python
from contextlib import ExitStack

import concourse.bass as bass
from concourse import mybir

P = 128
ALU = mybir.AluOpType
ACT = mybir.ActivationFunctionType
AX = mybir.AxisListType.X
F32 = mybir.dt.float32
BF16 = mybir.dt.bfloat16
U32 = mybir.dt.uint32
F32R = mybir.dt.float32r

NB = 4
S = 512
NT = S // P
D = 128
DH = 64
C = 77
H = 16
NPAIR = H // 2
HX1 = 8
E = 8
FT0 = 4
FT1 = 2
EPS = 1e-5
UNITS = H * NT
PB, PC, PD, PE_, PF = 4, 8, 12, 16, 20
WORKS = 24
WORK = 27296
PW = H * C + P - C + 1

COLS = {}
_n = 0
for _name, _w in (("ln_g", 1), ("ln_b", 1), ("bq", 8), ("bk", 8), ("bv", 8), ("bo0", 1), ("b1_0", 32),
                  ("gn_w", 8), ("gn_b", 8), ("bo1", 1), ("b1_1", 16)):
    COLS[_name] = (_n, _n + _w)
    _n += _w
NCOLS = _n
ROWS = {"xg": (0, 128), "xb": (128, 256), "ba": (256, 272), "br": (272, 280)}
NROWS = 280
CONSTS = {"ident": (0, 128), "upto": (128, 256), "after": (256, 384), "block": (384, 512), "iota": (512, 520),
          "sel": (520, 536), "mask": (536, 1048), "heads": (1048, 1050)}
NCONSTS = 1050
NKEPT = 520


def decoder(nc, T):
    with ExitStack() as ctx:
        def sb(name, shape, dt=F32):
            return ctx.enter_context(nc.sbuf_tensor(name, shape, dt))

        sems = {}

        def sem(name):
            if name not in sems:
                sems[name] = ctx.enter_context(nc.semaphore(name))
            return sems[name]

        bank = [ctx.enter_context(nc.psum_tensor(f"bank{i}", [P, S], F32)) for i in range(8)]
        x_all = sb("x_all", [P, NB * NT, D])
        xT_all = sb("xT_all", [P, NB, S])
        yT = sb("yT", [P, S])
        res = sb("res", [P, NT, D])
        OT = sb("OT", [P, NPAIR, S])
        with nc.sbuf_tensor("W0_low", [P, 8192], F32R) as W0_low:
            pass
        W0 = sb("W0", [P, 8192])
        with nc.sbuf_tensor("W1_low", [P, 5120], F32R) as W1_low:
            pass
        W1 = sb("W1", [P, 5120])
        cols = sb("cols", [P, NCOLS])
        rows = sb("rows", [P, NROWS])
        cst = sb("cst", [P, NKEPT])
        heads = sb("heads", [P, 2])
        mask = sb("mask", [P, S], BF16)
        ident_b = sb("ident_b", [P, P], BF16)
        sel = sb("sel", [P, H], BF16)
        rw = sb("rw", [P, 32])
        b2 = sb("b2", [E, 2, D])
        bn = sb("bn", [P, NT, 6])
        mv = sb("mv", [P, NT, 2])
        lnv = sb("lnv", [P, 6, NT])
        rt = sb("rt", [P, 12, 4, 8])
        ri = sb("ri", [P, 4, 8], U32)
        with nc.sbuf_tensor("split", [P, 12 * S], F32R) as split:
            pass
        work = sb("work", [P, WORK])

        HALF = (slice(0, DH), slice(DH, P))

        def col(name, i=0):
            return cols[:, COLS[name][0] + i:COLS[name][0] + i + 1]

        def const(name, src=cst, start=0):
            a, b = CONSTS[name]
            return src[:, a - start:b - start]

        ident = const("ident")
        upto = const("upto")
        after = const("after")
        block = const("block")
        iota = const("iota")

        def carve(at, n, count=1):
            return [work[:, at + i * n:at + (i + 1) * n] for i in range(count)], at + n * count

        (xn,), a = carve(12 * S, S)
        xnT = [W1[:, 4096 + i * S:4096 + (i + 1) * S] for i in range(2)]
        q1A, q2A, k1A = ([split[:, (4 * i + j) * S:(4 * i + j + 1) * S] for j in range(4)] for i in range(3))
        pA, a = carve(a, S, 5)
        ptA, a = carve(a, NT * S, 4)
        vA, a = carve(a, NT * S, 2)
        rsum, a = carve(a, 8, 2)
        (nmax,), a = carve(a, 8)
        end_a = a
        (kdB,), a = carve(0, NPAIR * NB * 2 * C)
        (vcB,), a = carve(a, NB * H * DH)
        (ptB,), a = carve(a, H * S)
        pB, a = carve(a, PW, 3)
        q_at = a = max(a, end_a)
        (qTB,), a = carve(a, NPAIR * S)
        statB, a = carve(a, 16, 6)
        assert a <= WORK - 1536
        hsC, a = carve(q_at, S, 3)
        hwC, a = carve(a, S, 3)
        (wT_C,), a = carve(WORK - 1536, 2 * S)
        (wselC,), a = carve(a, S)
        masks_in = wT_C[:, 0:NCONSTS - NKEPT]
        ktA, qtA = wT_C[:, 0:S], wT_C[:, S:2 * S]
        vD, a = carve(0, NT * S, 2)
        qTD, a = carve(a, S, 2)
        qbD, a = carve(a, 2 * S, 2)
        kTD, a = carve(a, S, 2)
        qeD, a = carve(a, S, 3)
        elD, a = carve(a, S, 3)
        dmD, a = carve(a, 2 * S, 2)
        atD, a = carve(a, 2 * S, 3)
        kdD, a = carve(a, S, 2)
        stD, a = carve(a, 3 * P, 2)
        oxD, a = carve(a, S, 4)
        thD, a = carve(a, S, 8)
        tqD, a = carve(a, S, 2)
        spD, a = carve(a, 64, 4)
        (lselD,), a = carve(a, S)
        lcD, a = carve(a, 128, 2)
        kdecD, a = carve(a, 64, 2)
        gnD, a = carve(a, 16, 8)
        (gn6,), a = carve(a, 8)
        gateD, a = carve(a, 8, 2)
        assert a <= WORK, a

        wsel_b = [wselC[:, i * 256:(i + 1) * 256].bitcast(BF16) for i in range(2)]
        lsel_b = [lselD[:, i * 256:(i + 1) * 256].bitcast(BF16) for i in range(2)]
        spl_r = sb("spl_r", [16, S])
        spl_m = sb("spl_m", [16, S], BF16)

        def v3(ap, n):
            return ap.rearrange("p (n k) -> p n k", n=n)

        wqA, wkA, wvA, woA = (W0[:, i * 1024:(i + 1) * 1024] for i in range(4))
        wqB, wkB, wvB, woB = (W1[:, i * 1024:(i + 1) * 1024] for i in range(4))
        w1C, w2C = W0[:, 0:4096], W0[:, 4096:8192]
        woD = W1[:, 4096:5120]
        wD_high = W0_low[:, 4096:8192]
        xh_D, xl_D = ([W0_low[:, 2048 + (2 * i + j) * S:2048 + (2 * i + j + 1) * S] for j in range(2)] for i in range(2))
        Q, K, V_, GATE = range(4)
        D_SPLITS = [(V_, 0), (Q, 0), (K, 0), (GATE, 0), (V_, 1), (Q, 1), (K, 1), (GATE, 1)]
        wqE, wkE, wvE, woE = (W0[:, i * 512:(i + 1) * 512] for i in range(4))
        w1F, w2F = W1[:, 0:2048], W1[:, 2048:4096]

        ctxT = sb("ctxT", [P, NB * C])

        def out_w(ph):
            return {0: woA, 1: woB, 3: woD, 4: woE}[ph]

        def o_slot(w, p):
            if w // NB == 3:
                s = (8 * (w % NB) + p) % 12
                return OT[:, s, :] if s < 8 else oxD[s - 8]
            return OT[:, p, :]

        CROSS = {1: dict(n="B", w0=PB, np=NPAIR, wq=wqB, wk=wkB, wv=wvB, bias=True),
                 4: dict(n="E", w0=PE_, np=HX1 // 2, wq=wqE, wk=wkE, wv=wvE, bias=False)}
        xh_M, xl_M = ([split[:, (2 * i + j) * S:(2 * i + j + 1) * S] for j in range(2)] for i in range(2))
        w1_high = split[:, 4 * S:4 * S + 4096]
        MOE = {2: dict(n="C", w0=PC, ft=FT0, w1=w1C, low=W0_low, w2=w2C, b1="b1_0", r=0, func=ACT.Gelu,
                      route=(14, 15, 17, 22)),
               5: dict(n="F", w0=PF, ft=FT1, w1=w1F, low=W1_low, w2=w2F, b1="b1_1", r=1, func=ACT.Relu,
                      route=(8, 9, 10, 13))}

        TAIL = {0: (11, 16, 19, 19, 26), 1: (1, 3, 4, 5, 11), 2: (2, 5, 8, 11, 16), 3: (6, 7, 8, 8, 9),
                4: (1, 3, 4, 5, 8), 5: (2, 4, 7, 7, 11)}

        def spread_norm(w):
            return w < WORKS - 1 and w != PD - 1 and (w + 1) // NB in (0, 2, 5)

        def cross_tail(tail, w0, u):
            for b in range(NB - 1):
                k = u - 4 * b - 6
                if 0 <= k < 5:
                    for s in range(2 * k, 2 * k + 2):
                        tail(w0 + b, s)

        def tail_steps(w):
            if w // NB in (1, 4) and w % NB < NB - 1:
                return (0, 2, 4, 6, 8)
            return (0, 1, 2, 2, 3) if w == PD - 1 else TAIL[min((w + 1) // NB, 5)]

        V_STEPS = ((49, 51, 57, 59), (17, 19, 25, 27))

        def out_pieces(w):
            return 4 if w < NB - 1 else 1

        y_ready, yT_ready, yt_ready = sem("y_ready"), sem("yT_ready"), sem("yt_ready")
        x_ready, xTp_ready, xT_ready = sem("x_ready"), sem("xTp_ready"), sem("xT_ready")
        dve_chain, act_chain, pool_chain = sem("dve_chain"), sem("act_chain"), sem("pool_chain")
        dma_in = {k: sem("dma_" + k) for k in ("x0", "x", "small", "masks", "late", "woA",
                                               "A", "B", "C", "D", "E", "F", "out")}
        consts_ready = sem("consts_ready")

        def loaded(eng, what, n=1):
            eng.wait_ge(dma_in[what], 16 * n)

        DMA_COUNT = {"x": 3, "small": 2, "late": 4, "A": 3, "B": 5, "C": 2, "D": 5, "E": 4, "F": 2}

        ENDS = {0: [("a_pv", 32), ("a_o", 32)],
                1: [("B_s", 16)],
                2: [("y_ready", 12), ("C_hw", 128)],
                3: [("y_ready", 15), ("d_og", 32)],
                4: [("E_s", 16)]}

        def enter(eng, ph):
            for name, value in ENDS[ph - 1]:
                eng.wait_ge(sem(name), value)

        owner = {}
        where = {}

        def take(pe, i, reader, value):
            if i in owner:
                s, n = owner[i]
                pe.wait_ge(s, n)
            owner[i] = (reader, value)
            return bank[i]

        turn = [0]

        def take_next(pe, key, reader, value):
            i = 6 + turn[0] % 2
            turn[0] += 1
            where[key] = bank[i]
            return take(pe, i, reader, value)

        block_ctx = ctx.enter_context(nc.Block())

        @block_ctx.sync
        def _(sp):
            sp.dma_start(x_all[:, 0:4, :], T["x"][0].rearrange("(t p) d -> p t d", p=P)).then_inc(dma_in["x0"], 16)
            for i, n in ((0, "L0_attn_Wq"), (2, "L0_attn_Wv")):
                sp.dma_start(W0[:, i * 1024:(i + 1) * 1024], T[n]).then_inc(dma_in["A"], 16)
            for b in range(1, NB):
                sp.dma_start(x_all[:, 4 * b:4 * b + 4, :], T["x"][b].rearrange("(t p) d -> p t d", p=P))\
                    .then_inc(dma_in["x"], 16)
            sp.dma_start(v3(woA, 8), T["L0_attn_Wo"].rearrange("(n p) d -> p n d", p=P)).then_inc(dma_in["woA"], 16)
            sp.dma_start(rows[:, :], T["rows"].partition_broadcast(P)).then_inc(dma_in["late"], 16)
            sp.dma_start(rw[:, :], T["narrow"]).then_inc(dma_in["late"], 16)
            sp.dma_start(b2[:, 0, :], T["L0_ffn_b2"]).then_inc(dma_in["late"], 16)
            sp.dma_start(b2[:, 1, :], T["L1_ffn_b2"]).then_inc(dma_in["late"], 16)
            sp.dma_start(ctxT[:, :], T["ctxT"]).then_inc(dma_in["B"], 16)
            for i, n in enumerate(("L0_xattn_Wq", "L0_xattn_Wk", "L0_xattn_Wv")):
                sp.dma_start(W1[:, i * 1024:(i + 1) * 1024], T[n]).then_inc(dma_in["B"], 16)
            sp.dma_start(v3(woB, 8), T["L0_xattn_Wo"].rearrange("(n p) d -> p n d", p=P)).then_inc(dma_in["B"], 16)
            sp.wait_ge(y_ready, 4)
            sp.dma_start(w1C, T["w1T"]).then_inc(dma_in["C"], 16)
            sp.dma_start(w2C.rearrange("p (e d) -> p e d", d=D), T["w2T"].rearrange("(e p) d -> p e d", p=P))\
                .then_inc(dma_in["C"], 16)
            sp.wait_ge(y_ready, 8)
            for i, n in enumerate(("L1_attn_Wq", "L1_attn_Wk", "L1_attn_Wv", "L1_attn_Wg")):
                sp.dma_start(W1[:, i * 1024:(i + 1) * 1024], T[n]).then_inc(dma_in["D"], 16)
            sp.dma_start(v3(woD, 8), T["L1_attn_Wo"].rearrange("(n p) d -> p n d", p=P)).then_inc(dma_in["D"], 16)
            sp.wait_ge(y_ready, 12)
            for i, n in enumerate(("L1_xattn_Wq", "L1_xattn_Wk", "L1_xattn_Wv")):
                sp.dma_start(W0[:, i * 512:(i + 1) * 512], T[n]).then_inc(dma_in["E"], 16)
            sp.dma_start(v3(woE, 4), T["L1_xattn_Wo"].rearrange("(n p) d -> p n d", p=P)).then_inc(dma_in["E"], 16)
            sp.wait_ge(y_ready, 16)
            sp.dma_start(w1F.rearrange("p (e h) -> p e h", e=E), T["L1_ffn_W1"].rearrange("e d h -> d e h"))\
                .then_inc(dma_in["F"], 16)
            sp.dma_start(w2F.rearrange("p (e d) -> p e d", d=D),
                         T["L1_ffn_W2"].rearrange("e (t p) d -> p (e t) d", p=P)).then_inc(dma_in["F"], 16)
            for b in range(NB):
                sp.wait_ge(x_ready, PF + b + 1)
                sp.dma_start(T["out"][b].rearrange("(t p) d -> p t d", p=P), x_all[:, 4 * b:4 * b + 4, :])\
                    .then_inc(dma_in["out"], 16)
            sp.wait_ge(dma_in["out"], 16 * NB)

        @block_ctx.tensor
        def _(pe):
            mm = nc.tensor.matmul

            def tail(w, s, last=False):
                ph = w // NB
                at = tail_steps(w)
                k, pieces = s - at[0], out_pieces(w)
                if 0 <= k < pieces and ph in (0, 1, 3, 4):
                    n = 4 if ph == 4 else 8
                    if k == 0:
                        pe.wait_ge(sem({0: "a_o", 1: "B_o", 3: "d_og", 4: "E_o"}[ph]), n * (w % NB + 1))
                        take_next(pe, ("y", w), yT_ready, w + 1)
                    for p in range(k * n // pieces, (k + 1) * n // pieces):
                        m = mm(where["y", w][:, :], out_w(ph)[:, p * P:(p + 1) * P], o_slot(w, p),
                               start=(p == 0), stop=(p == n - 1))
                    if k == pieces - 1:
                        m.then_inc(y_ready, 1)
                if s == at[1]:
                    pe.wait_ge(yT_ready, w + 1)
                    out = take_next(pe, ("yt", w), sem("sum_done"), w + 1)
                    for t in range(NT):
                        m = nc.tensor.transpose(out[:, t * P:(t + 1) * P], yT[:, t * P:(t + 1) * P], ident)
                    m.then_inc(yt_ready, 1)
                if s == at[4] and w < PF:
                    pe.wait_ge(x_ready, w + 1)
                    out = take_next(pe, ("xT", w), xT_ready, w + 1)
                    b = w % NB
                    for t in range(NT):
                        m = nc.tensor.transpose(out[:, t * P:(t + 1) * P], x_all[:, 4 * b + t, :], ident)
                    m.then_inc(xTp_ready, 1)

            def a_norm_T(b):
                pe.wait_ge(sem("a_xn"), b + 1)
                out = take_next(pe, ("a_xn", b), sem("a_xnT"), b + 1)
                for t in range(NT):
                    m = nc.tensor.transpose(out[:, t * P:(t + 1) * P], v3(xn, NT)[:, t, :], ident)
                m.then_inc(sem("a_xnp"), 1)

            def a_v(b, hf, t):
                n = 8 * b + 4 * hf + t
                pe.wait_ge(sem("a_xnT"), b + 1)
                out = take_next(pe, ("a_v", n), sem("a_vs"), n + 1)
                mm(out[:, :], xnT[b % 2][:, t * P:(t + 1) * P], wvA[:, hf * S:(hf + 1) * S], start=True, stop=True)\
                    .then_inc(sem("a_vp"), 1)

            def a_qk(g, w, ready, done):
                b, p = g // 8, g % 8
                pe.wait_ge(sem("a_xnT"), b + 1)
                out = take_next(pe, (ready, g), sem(done), g + 1)
                mm(out[:, :], w[:, p * P:(p + 1) * P], xnT[b % 2], start=True, stop=True).then_inc(sem(ready), 1)

            def a_scores(u):
                g, hh, t = u // 8, (u // 4) % 2, u % 4
                if u % 8 == 0:
                    pe.wait_ge(sem("a_qs"), g + 1)
                    pe.wait_ge(sem("a_qd"), g + 1)
                    pe.wait_ge(sem("a_ks"), g + 1)
                out = take(pe, u % 3, sem("a_e"), u + 1)
                i = 2 * (g % 2) + hh
                k = k1A[i]
                mm(out[:, :], q1A[i][:, t * P:(t + 1) * P], k, start=True, stop=False)
                mm(out[:, :], q2A[i][:, t * P:(t + 1) * P], k, start=False, stop=True).then_inc(sem("a_s"), 1)

            def a_turn(u):
                pe.wait_ge(sem("a_n"), u + 1)
                out = take(pe, 3 + u % 2, sem("a_pt"), u + 1)
                for k in range(NT):
                    m = nc.tensor.transpose(out[:, k * P:(k + 1) * P], pA[u % 5][:, k * P:(k + 1) * P], ident)
                m.then_inc(sem("a_t"), 1)

            def a_out(g, k):
                b, p = g // 8, g % 8
                if k == 0:
                    pe.wait_ge(sem("a_pt"), 8 * g + 8)
                    pe.wait_ge(sem("a_vs"), 8 * b + 4 * (p // 4) + 4)
                    take(pe, 5, sem("a_o"), g + 1)
                for hh in range(2):
                    m = mm(bank[5][hh * DH:(hh + 1) * DH, :], v3(vA[p // 4], NT)[:, k, (2 * (p % 4) + hh) * DH:(2 * (p % 4) + hh + 1) * DH],
                           v3(ptA[(2 * g + hh) % 4], NT)[:, k, :], start=(k == 0), stop=(k == NT - 1))
                if k == NT - 1:
                    m.then_inc(sem("a_pv"), 1)

            loaded(pe, "small", DMA_COUNT["small"])
            a_norm_T(0)
            loaded(pe, "A", DMA_COUNT["A"])
            a_qk(0, wkA, "a_kp", "a_ke")
            a_qk(0, wqA, "a_qp", "a_qe")
            a_qk(1, wkA, "a_kp", "a_ke")
            for t in range(NT):
                a_v(0, 0, t)
            NU = NB * UNITS
            for u in range(NU + 9):
                b, s, g, j = u // UNITS, u % UNITS, u // 8, u % 8
                if u < NU:
                    if u == UNITS:
                        loaded(pe, "woA")
                    if b:
                        tail(b - 1, s)
                    if s == 30 and b + 1 < NB:
                        a_norm_T(b + 1)
                    if j == 2 and g + 1 < 32:
                        a_qk(g + 1, wqA, "a_qp", "a_qe")
                    if j == 4 and g + 2 < 32:
                        a_qk(g + 2, wkA, "a_kp", "a_ke")
                    if s in V_STEPS[0] and b + 1 < NB:
                        a_v(b + 1, 0, V_STEPS[0].index(s))
                    if s in V_STEPS[1]:
                        a_v(b, 1, V_STEPS[1].index(s))
                    a_scores(u)
                if 4 <= u < NU + 4:
                    a_turn(u - 4)
                if u >= 13:
                    h, k = divmod(u - 13, 8)
                    if k < NT and h < 32:
                        a_out(h, k)

            def cross_kv(c):
                n = c["n"]
                for p in range(c["np"]):
                    out = take_next(pe, (n + "k", p), sem(n + "_ks"), p + 1)
                    mm(out[:, 0:NB * C], c["wk"][:, p * P:(p + 1) * P], ctxT[:, :], start=True, stop=True)\
                        .then_inc(sem(n + "_kp"), 1)
                nh = c["np"] * P // S
                for i in range(NB * nh):
                    b, hf = i // nh, i % nh
                    out = take_next(pe, (n + "v", i), sem(n + "_vs"), i + 1)
                    mm(out[0:C, :], ctxT[:, b * C:(b + 1) * C], c["wv"][:, hf * S:(hf + 1) * S], start=True, stop=True)\
                        .then_inc(sem(n + "_vp"), 1)

            def cross_q(c, b):
                n, np_ = c["n"], c["np"]
                pe.wait_ge(xT_ready, c["w0"] - NB + b + 1)
                for p in range(np_):
                    k = np_ * b + p
                    out = take_next(pe, (n + "q", k), sem(n + "_qs"), k + 1)
                    mm(out[:, :], c["wq"][:, p * P:(p + 1) * P], xT_all[:, b, :], start=True, stop=True)\
                        .then_inc(sem(n + "_qp"), 1)

            def cross_scores(c, b, t):
                n, np_ = c["n"], c["np"]
                if t == 0:
                    pe.wait_ge(sem(n + "_qs"), np_ * (b + 1))
                    if b == 0:
                        pe.wait_ge(sem(n + "_ks"), np_)
                u = NT * b + t
                for p in range(np_):
                    if p % 3 == 0:
                        out = take(pe, p // 3, sem(n + "_sub"), u + 1)
                    kd = kdB[:, (p * NB + b) * 2 * C:(p * NB + b + 1) * 2 * C]
                    m = mm(out[:, (p % 3) * 2 * C:(p % 3 + 1) * 2 * C],
                           v3(qTB, NPAIR)[:, p, t * P:(t + 1) * P], kd, start=True, stop=True)
                m.then_inc(sem(n + "_s"), 1)

            def cross_turn(c, b, t):
                n, np_ = c["n"], c["np"]
                u = NT * b + t
                nq = np_ * 2 // 4
                pe.wait_ge(sem(n + "_n"), u + 1)
                for q in range(nq):
                    k = nq * u + q
                    out = take(pe, 3 + k % 2, sem(n + "_pt"), k + 1)
                    for i in range(4):
                        h = 4 * q + i
                        m = nc.tensor.transpose(out[:, i * P:(i + 1) * P], pB[u % 3][:, h * C:h * C + P], ident)
                    m.then_inc(sem(n + "_t"), 1)

            def cross_out(c, b):
                n, np_ = c["n"], c["np"]
                nq = np_ * 2 // 4
                pe.wait_ge(sem(n + "_pt"), nq * NT * (b + 1))
                if b == 0:
                    pe.wait_ge(sem(n + "_vs"), NB * np_ * P // S)
                for p in range(np_):
                    k = np_ * b + p
                    out = take_next(pe, (n + "o", k), sem(n + "_o"), k + 1)
                    for hh in range(2):
                        h = 2 * p + hh
                        m = mm(out[hh * DH:(hh + 1) * DH, :], v3(vcB, NB)[:, b, h * DH:(h + 1) * DH],
                               v3(ptB, H)[:, h, :], start=True, stop=True)
                    m.then_inc(sem(n + "_pv"), 1)

            def cross(ph):
                c = CROSS[ph]
                n, w0 = c["n"], c["w0"]
                loaded(pe, n, DMA_COUNT[n])
                if ph == 1:
                    loaded(pe, "late", DMA_COUNT["late"])
                cross_q(c, 0)
                cross_kv(c)
                for u in range(NB * NT + 3):
                    b, t = u // NT, u % NT
                    if b < NB:
                        cross_scores(c, b, t)
                        if t == 3 and b + 1 < NB:
                            cross_q(c, b + 1)
                    if u < NT:
                        for s in range(3 * u, 3 * u + 3):
                            tail(w0 - 1, s)
                    cross_tail(tail, w0, u)
                    if 2 <= u < NB * NT + 2:
                        cross_turn(c, (u - 2) // NT, (u - 2) % NT)
                    if t == 1 and b >= 1:
                        cross_out(c, b - 1)
                    if u == NB * NT + 1:
                        moe_logits(MOE[ph + 1], 0)

            def moe_logits(m_, b):
                n, r = m_["n"], m_["r"]
                pe.wait_ge(xT_ready, m_["w0"] - NB + b + 1)
                out = take_next(pe, (n + "lg", b), sem(n + "_lg"), b + 1)
                for t in range(NT):
                    m = mm(out[:, t * E:(t + 1) * E], xT_all[:, b, t * P:(t + 1) * P], rw[:, r * E:(r + 1) * E],
                           start=True, stop=True)
                m.then_inc(sem(n + "_lgp"), 1)

            def moe_wT(m_, b):
                n = m_["n"]
                pe.wait_ge(sem(n + "_wt"), b + 1)
                out = take_next(pe, (n + "wT", b), sem(n + "_wTr"), b + 1)
                for t in range(NT):
                    m = nc.tensor.transpose(out[0:E, t * P:(t + 1) * P], rt[:, 11, t, :], ident)
                m.then_inc(sem(n + "_wTp"), 1)

            def moe_h(m_, i):
                n, steps = m_["n"], E * m_["ft"]
                b, s = i // steps, i % steps
                pe.wait_ge(sem(n + "_xs"), b + 1)
                if b == 0:
                    pe.wait_ge(sem(n + "_ws"), s // 4 + 1)
                out = take(pe, i % 3, sem(n + "_h"), i + 1)
                high, low = w1_high[:, s * P:(s + 1) * P], m_["low"][:, s * P:(s + 1) * P]
                mm(out[:, :], high, xh_M[b % 2], start=True, stop=False)
                mm(out[:, :], low, xh_M[b % 2], start=False, stop=False)
                mm(out[:, :], high, xl_M[b % 2], start=False, stop=True).then_inc(sem(n + "_hp"), 1)

            def moe(ph):
                m_ = MOE[ph]
                n, ft, r = m_["n"], m_["ft"], m_["r"]
                steps = E * ft
                loaded(pe, n, DMA_COUNT[n])

                def contract(i):
                    b, k = i // steps, i % steps
                    if k == 0:
                        take(pe, 5, yT_ready, m_["w0"] + b + 1)
                        mm(bank[5][:, :], b2[:, r, :], wT_C[0:E, (b % 2) * S:(b % 2 + 1) * S], start=True, stop=False)
                    pe.wait_ge(sem(n + "_hw"), i + 1)
                    m = mm(bank[5][:, :], m_["w2"][:, k * D:(k + 1) * D], hwC[i % 3], start=False, stop=(k == steps - 1))
                    if k == steps - 1:
                        m.then_inc(y_ready, 1)
                    else:
                        m.then_inc(sem(n + "_c"), 1)

                for i in range(NB * steps + 2):
                    b, s = i // steps, i % steps
                    if b < NB:
                        tail(m_["w0"] + b - 1, s)
                        if b + 1 < NB and s == m_["route"][0]:
                            moe_logits(m_, b + 1)
                        if b + 1 < NB and s == m_["route"][3]:
                            moe_wT(m_, b + 1)
                        if i == 0:
                            moe_h(m_, 0)
                            moe_h(m_, 1)
                            moe_wT(m_, 0)
                        if s % ft == 0:
                            e = s // ft
                            if s == 0:
                                pe.wait_ge(sem(n + "_sel"), b + 1)
                            out = take(pe, 3 + e % 2, sem(n + "_hw"), i + ft)
                            mm(out[:, :], sel[:, e:e + 1].to_broadcast([P, P]), wsel_b[b % 2], start=True, stop=True)\
                                .then_inc(sem(n + "_wb"), 1)
                        if i >= 2:
                            moe_h(m_, i)
                    if i >= 2:
                        contract(i - 2)

            def d_alpha(b):
                pe.wait_ge(xT_ready, PC + b + 1)
                out = take_next(pe, ("d_al", b), sem("d_z"), b + 1)
                for t in range(NT):
                    m = mm(out[:, t * H:(t + 1) * H], xT_all[:, b, t * P:(t + 1) * P], rw[:, 16:32], start=True, stop=True)
                m.then_inc(sem("d_al"), 1)

            def d_sums(b):
                pe.wait_ge(sem("d_sp"), b + 1)
                out = take_next(pe, ("d_LT", b), sem("d_LTr"), b + 1)
                for t in range(NT):
                    m = mm(out[0:H, t * P:(t + 1) * P], v3(spD[3], NT)[:, t, :], upto, start=True, stop=True)
                m.then_inc(sem("d_LT"), 1)
                out = take_next(pe, ("d_lc", b), sem("d_lcs"), b + 1)
                mm(out[:, 0:64], upto, spD[3], start=True, stop=True)
                mm(out[:, 64:128], after, spD[3], start=True, stop=True).then_inc(sem("d_lcp"), 1)

            def d_split_wait(b, which, half):
                pe.wait_ge(sem("d_xs"), b + 1)
                if b == 0:
                    pe.wait_ge(sem("d_ws"), D_SPLITS.index((which, half)) + 1)

            def d_v(b, hf, t):
                n = 8 * b + 4 * hf + t
                d_split_wait(b, V_, hf)
                out = take_next(pe, ("d_v", n), sem("d_vs"), n + 1)
                r, at = slice(t * P, (t + 1) * P), V_ * 1024 + hf * S
                mm(out[:, :], xh_D[b % 2][:, r], wD_high[:, at:at + S], start=True, stop=False)
                mm(out[:, :], xl_D[b % 2][:, r], wD_high[:, at:at + S], start=False, stop=False)
                mm(out[:, :], xh_D[b % 2][:, r], W1_low[:, at:at + S], start=False, stop=True).then_inc(sem("d_vp"), 1)

            def d_decays(g):
                b, p = g // 8, g % 8
                if p == 0:
                    pe.wait_ge(sem("d_lsel"), b + 1)
                out = take(pe, 0, sem("d_el"), g + 1)
                for hh in range(2):
                    m = mm(out[hh * DH:(hh + 1) * DH, :], sel[:, 2 * p + hh:2 * p + hh + 1].to_broadcast([P, DH]),
                           lsel_b[b % 2], start=True, stop=True)
                m.then_inc(sem("d_lp"), 1)

            def d_decay_to(g, hh):
                b, p = g // 8, g % 8
                out = take(pe, 1 - hh, sem("d_dm"), 2 * g + hh + 1)
                mm(out[:, :], sel[:, 2 * p + hh:2 * p + hh + 1].to_broadcast([P, P]), lsel_b[b % 2],
                   start=True, stop=False)
                mm(out[:, :], ident_b[:, :], mask[:, :], start=False, stop=True).then_inc(sem("d_la"), 1)

            def d_proj(g, i):
                b, p = g // 8, g % 8
                which = (Q, K, GATE)[i]
                d_split_wait(b, which, p // 4)
                reader = (sem("d_silu"), 2 * g + i + 1) if i < 2 else (sem("d_th"), g + 1)
                out = take_next(pe, ("d_p", g, i), *reader)
                r = slice(which * 1024 + p * P, which * 1024 + (p + 1) * P)
                mm(out[:, :], wD_high[:, r], xh_D[b % 2], start=True, stop=False)
                mm(out[:, :], W1_low[:, r], xh_D[b % 2], start=False, stop=False)
                mm(out[:, :], wD_high[:, r], xl_D[b % 2], start=False, stop=True)\
                    .then_inc(sem("d_gp_" if i == 2 else "d_pp"), 1)

            def d_scores(g):
                pe.wait_ge(sem("d_qb"), g + 1)
                for c2 in range(2):
                    out = take(pe, 2 + c2, sem("d_at"), 2 * g + c2 + 1)
                    for c in (2 * c2, 2 * c2 + 1):
                        m = mm(out[:, (c % 2) * 256:(c % 2 + 1) * 256], kTD[g % 2][:, c * P:(c + 1) * P],
                               qbD[g % 2][:, c * 256:(c + 1) * 256], start=True, stop=True)
                    m.then_inc(sem("d_s"), 1)

            def d_kturn(g):
                pe.wait_ge(sem("d_silu"), 2 * g + 2)
                out = take(pe, 4, sem("d_kd"), g + 1)
                for c in range(NT):
                    m = nc.tensor.transpose(out[:, c * P:(c + 1) * P], kTD[g % 2][:, c * P:(c + 1) * P], ident)
                m.then_inc(sem("d_kt"), 1)

            def d_state(g):
                b, p = g // 8, g % 8
                pe.wait_ge(sem("d_kd"), g + 1)
                pe.wait_ge(sem("d_vs"), 8 * b + 4 * (p // 4) + 4)
                out = take(pe, 4, sem("d_st"), g + 1)
                for c in range(NT - 1):
                    m = mm(out[:, c * P:(c + 1) * P], kdD[g % 2][:, c * P:(c + 1) * P],
                           v3(vD[p // 4], NT)[:, c, (p % 4) * P:(p % 4 + 1) * P], start=True, stop=True)
                m.then_inc(sem("d_dl"), 1)

            def d_out(g):
                p = g % 8
                pe.wait_ge(sem("d_at"), 2 * g + 2)
                pe.wait_ge(sem("d_st"), g + 1)
                pe.wait_ge(sem("d_qe"), g + 1)
                out = take(pe, 5, sem("d_o"), g + 1)
                for c in range(NT):
                    if c:
                        mm(out[:, c * P:(c + 1) * P], stD[g % 2][:, (c - 1) * P:c * P], qeD[g % 3][:, c * P:(c + 1) * P],
                           start=True, stop=False, skip_group_check=True)
                    for hh in range(2):
                        at = c * 256 + hh * P
                        m = mm(out[hh * DH:(hh + 1) * DH, c * P:(c + 1) * P],
                               v3(vD[p // 4], NT)[:, c, (p % 4) * P + hh * DH:(p % 4) * P + (hh + 1) * DH],
                               atD[g % 3][:, at:at + P], start=(c == 0), stop=True, skip_group_check=True)
                m.then_inc(sem("d_pv"), 1)

            def d_mean(k, i):
                pe.wait_ge(sem("d_gs"), 2 * k + i + 1)
                out = take_next(pe, ("d_gn", 2 * k + i), sem("d_gr"), 2 * k + i + 1)
                src = gnD[0][:, 4 * (k % 2):4 * (k % 2) + 4] if i == 0 else gnD[2][:, 0:4]
                mm(out[:, 0:4], block, src, start=True, stop=True).then_inc(sem("d_gp"), 1)

            def phase_d():
                loaded(pe, "D", DMA_COUNT["D"])
                d_alpha(0)
                for t in range(NT):
                    d_v(0, 0, t)
                d_sums(0)
                d_proj(0, 0)
                d_proj(0, 1)
                d_decays(0)
                d_decay_to(0, 0)
                d_decay_to(0, 1)
                for g in range(32 + 4):
                    b, s = g // 8, g % 8
                    if 1 <= g <= 32:
                        d_state(g - 1)
                    if g + 1 < 32:
                        d_proj(g + 1, 0)
                        d_proj(g + 1, 1)
                        d_decays(g + 1)
                        d_decay_to(g + 1, 0)
                    if g < 32:
                        d_scores(g)
                    if g + 1 < 32:
                        d_decay_to(g + 1, 1)
                    if 1 <= g <= 32:
                        d_proj(g - 1, 2)
                    if g < 32:
                        d_kturn(g)
                    if 2 <= g < 34:
                        d_out(g - 2)
                    if s in (2, 6) and g >= 6:
                        d_mean((g - 6) // 4, 0)
                    if s in (3, 7) and g >= 7:
                        d_mean((g - 7) // 4, 1)
                    if g >= 16:
                        tail(PD + b - 2, s + 8)
                    if g < 32:
                        tail(PD + b - 1, s)
                        if s in (2, 3):
                            d_v(b, 1, 2 * s - 4)
                            d_v(b, 1, 2 * s - 3)
                        if b + 1 < NB:
                            if s == 2:
                                d_alpha(b + 1)
                            if s == 4:
                                d_sums(b + 1)
                            if s in (6, 7):
                                d_v(b + 1, 0, 2 * s - 12)
                                d_v(b + 1, 0, 2 * s - 11)

            cross(1)
            moe(2)
            phase_d()
            cross(4)
            moe(5)
            for s in range(32):
                tail(WORKS - 1, s)

        @block_ctx.scalar
        def _(act):
            A = nc.scalar.activation
            chain = [0]

            def link(ins):
                chain[0] += 1
                ins.then_inc(act_chain, 1)
                act.wait_ge(act_chain, chain[0])

            def tail(w, s):
                ph, b = w // NB, w % NB
                at = tail_steps(w)
                if s == at[0] + out_pieces(w) - 1:
                    act.wait_ge(y_ready, w + 1)
                    if w:
                        act.wait_ge(yt_ready, w)
                    src = bank[5] if ph in (2, 5) else where["y", w]
                    if ph in (1, 4):
                        A(yT[:, :], src[:, :], ACT.Identity, bias=col("bo0" if ph == 1 else "bo1")).then_inc(yT_ready, 1)
                    else:
                        A(yT[:, :], src[:, :], ACT.Copy).then_inc(yT_ready, 1)
                if s == at[4] and w < PF:
                    act.wait_ge(xTp_ready, w + 1)
                    A(xT_all[:, b, :], where["xT", w][:, :], ACT.Copy).then_inc(xT_ready, 1)

            def a_norm_T(b):
                act.wait_ge(sem("a_xnp"), b + 1)
                if b >= 2:
                    act.wait_ge(sem("a_kp"), 8 * (b - 1))
                    act.wait_ge(sem("a_vp"), 8 * (b - 1))
                A(xnT[b % 2], where["a_xn", b][:, :], ACT.Identity, bias=col("ln_b"), scale=col("ln_g"))\
                    .then_inc(sem("a_xnT"), 1)

            def a_v(b, hf, t):
                n = 8 * b + 4 * hf + t
                act.wait_ge(sem("a_vp"), n + 1)
                if b and t == 0:
                    act.wait_ge(sem("a_pv"), 8 * b - 8 + 4 * hf + 4)
                A(v3(vA[hf], NT)[:, t, :], where["a_v", n][:, :], ACT.Copy).then_inc(sem("a_vs"), 1)

            def a_evac(g, proj, dst, free, done, scale):
                act.wait_ge(sem(proj), g + 1)
                if g:
                    act.wait_ge(sem(free), g)
                A(dst, where[proj, g][:, :], ACT.Copy, scale=scale).then_inc(sem(done), 1)

            def a_k(g):
                a_evac(g, "a_kp", ktA, "a_ks", "a_ke", 1.0)

            def a_q(g):
                if g:
                    act.wait_ge(sem("a_qd"), g)
                a_evac(g, "a_qp", qtA, "a_qs", "a_qe", 0.125)

            def a_qdup(g, hh):
                act.wait_ge(sem("a_qe"), g + 1)
                if g >= 2:
                    act.wait_ge(sem("a_s"), 8 * (g - 1))
                m = A(q2A[2 * (g % 2) + hh][HALF[1 - hh], :], qtA[HALF[hh], :], ACT.Copy)
                if hh:
                    m.then_inc(sem("a_qd"), 1)

            def a_exp(u):
                act.wait_ge(sem("a_mx"), u + 1)
                if u >= 5:
                    act.wait_ge(sem("a_t"), u - 4)
                A(pA[u % 5], bank[u % 3][:, :], ACT.Exp, bias=nmax[:, u % 8:u % 8 + 1],
                  accum_out=rsum[0][:, u % 8:u % 8 + 1]).then_inc(sem("a_e"), 1)

            def a_pt(u):
                h = u // 4
                act.wait_ge(sem("a_t"), u + 1)
                if u >= 16 and u % 8 == 0:
                    act.wait_ge(sem("a_pv"), u // 8 - 1)
                A(v3(ptA[h % 4], NT)[:, :, (u % 4) * P:(u % 4 + 1) * P], v3(bank[3 + u % 2][:, :], NT), ACT.Copy)\
                    .then_inc(sem("a_pt"), 1)

            def a_o(g):
                act.wait_ge(sem("a_pv"), g + 1)
                if g >= 8 and g % 8 == 0:
                    act.wait_ge(y_ready, g // 8)
                A(OT[:, g % 8, :], bank[5][:, :], ACT.Copy).then_inc(sem("a_o"), 1)

            act.dma_start(cst[:, :], T["consts"][:, 0:NKEPT]).then_inc(dma_in["small"], 16)
            act.dma_start(cols[:, :], T["cols"]).then_inc(dma_in["small"], 16)
            act.dma_start(W0[:, 1024:2048], T["L0_attn_Wk"]).then_inc(dma_in["A"], 16)
            act.dma_start(masks_in, T["consts"][:, NKEPT:NCONSTS]).then_inc(dma_in["masks"], 16)
            loaded(act, "small", DMA_COUNT["small"])
            a_norm_T(0)
            act.wait_ge(consts_ready, 1)
            a_k(0)
            a_q(0)
            a_qdup(0, 0)
            a_qdup(0, 1)
            a_k(1)
            for t in range(NT):
                a_v(0, 0, t)
            NU = NB * UNITS
            for u in range(NU + 4):
                b, s, g, j = u // UNITS, u % UNITS, u // 8, u % 8
                if u < NU:
                    if b:
                        tail(b - 1, s)
                    if s == 30 and b + 1 < NB:
                        a_norm_T(b + 1)
                    if s in V_STEPS[0] and b + 1 < NB:
                        a_v(b + 1, 0, V_STEPS[0].index(s))
                    if s in V_STEPS[1]:
                        a_v(b, 1, V_STEPS[1].index(s))
                    a_exp(u)
                    if g + 1 < 32:
                        if j == 2:
                            a_q(g + 1)
                        if j in (3, 4):
                            a_qdup(g + 1, j - 3)
                    if j == 5 and g + 2 < 32:
                        a_k(g + 2)
                if j == 1 and g >= 2:
                    a_o(g - 2)
                if u >= 4:
                    a_pt(u - 4)
            a_o(31)

            def cross_v(c):
                n = c["n"]
                nh = c["np"] * P // S
                act.wait_ge(sem(n + "_zero"), 2)
                for i in range(NB * nh):
                    act.wait_ge(sem(n + "_vp"), i + 1)
                    b, hf = i // nh, i % nh
                    A(v3(vcB, NB)[0:C, b, hf * S:(hf + 1) * S], where[n + "v", i][0:C, :], ACT.Copy)\
                        .then_inc(sem(n + "_vs"), 1)

            def cross_q(c, b):
                n, np_ = c["n"], c["np"]
                if b:
                    act.wait_ge(sem(n + "_s"), NT * b)
                for p in range(np_):
                    k = np_ * b + p
                    act.wait_ge(sem(n + "_qp"), k + 1)
                    src = where[n + "q", k][:, :]
                    if c["bias"]:
                        i = A(v3(qTB, NPAIR)[:, p, :], src, ACT.Identity, bias=col("bq", p))
                    else:
                        i = A(v3(qTB, NPAIR)[:, p, :], src, ACT.Copy)
                    i.then_inc(sem(n + "_qs"), 1)

            def cross_exp(c, b, t):
                n = c["n"]
                u = NT * b + t
                hs = 2 * c["np"]
                act.wait_ge(sem(n + "_sub"), u + 1)
                p = pB[u % 3][:, 0:hs * C]
                A(p, p, ACT.Exp, scale=0.125).then_inc(sem(n + "_e"), 1)

            def cross_o(c, b):
                n, np_ = c["n"], c["np"]
                act.wait_ge(y_ready, c["w0"] + b)
                for p in range(np_):
                    k = np_ * b + p
                    act.wait_ge(sem(n + "_pv"), k + 1)
                    src = where[n + "o", k][:, :]
                    if c["bias"]:
                        i = A(OT[:, p, :], src, ACT.Identity, bias=col("bv", p))
                    else:
                        i = A(OT[:, p, :], src, ACT.Copy)
                    i.then_inc(sem(n + "_o"), 1)

            def cross_pt(c, b, t):
                n = c["n"]
                nq = c["np"] * 2 // 4
                u = NT * b + t
                if t == 0 and b:
                    act.wait_ge(sem(n + "_pv"), c["np"] * b)
                for q in range(nq):
                    k = nq * u + q
                    act.wait_ge(sem(n + "_t"), k + 1)
                    A(v3(ptB, H)[:, 4 * q:4 * q + 4, t * P:(t + 1) * P], v3(bank[3 + k % 2][:, :], NT), ACT.Copy)\
                        .then_inc(sem(n + "_pt"), 1)

            def cross(ph):
                c = CROSS[ph]
                n, w0 = c["n"], c["w0"]
                if ph == 4:
                    enter(act, ph)
                cross_q(c, 0)
                if ph == 1:
                    enter(act, ph)
                cross_v(c)
                for u in range(NB * NT + 3):
                    b, t = u // NT, u % NT
                    if b < NB and t == 3 and b + 1 < NB:
                        cross_q(c, b + 1)
                    if u < NT:
                        for s in range(3 * u, 3 * u + 3):
                            tail(w0 - 1, s)
                    cross_tail(tail, w0, u)
                    if 2 <= u < NB * NT + 2:
                        cross_pt(c, (u - 2) // NT, (u - 2) % NT)
                    if b < NB:
                        cross_exp(c, b, t)
                    if t == 1 and b >= 1:
                        cross_o(c, b - 1)

            def moe_exp(m_, b):
                n = m_["n"]
                act.wait_ge(sem(n + "_d"), b + 1)
                if n == "C":
                    A(lnv[:, 4, :], lnv[:, 3, :], ACT.Exp).then_inc(sem(n + "_e"), 1)
                else:
                    A(rt[:, 2, :, :], rt[:, 1, :, :], ACT.Exp).then_inc(sem(n + "_e"), 1)

            def moe(ph):
                m_ = MOE[ph]
                n, ft = m_["n"], m_["ft"]
                steps = E * ft
                moe_exp(m_, 0)
                enter(act, ph)
                for i in range(NB * steps):
                    b, s = i // steps, i % steps
                    tail(m_["w0"] + b - 1, s)
                    if s == m_["route"][1] and b + 1 < NB:
                        moe_exp(m_, b + 1)
                    act.wait_ge(sem(n + "_hp"), i + 1)
                    if i >= 3:
                        act.wait_ge(sem(n + "_hw"), i - 2)
                    A(hsC[i % 3], bank[i % 3][:, :], m_["func"], bias=col(m_["b1"], s)).then_inc(sem(n + "_h"), 1)

            def d_softplus(b):
                act.wait_ge(sem("d_az"), b + 1)
                link(A(spD[2], spD[1], ACT.Exp, scale=-1.0))
                A(spD[2], spD[2], ACT.Ln, bias=1.0).then_inc(sem("d_ln"), 1)

            def d_kdec(b):
                act.wait_ge(sem("d_lcs"), b + 1)
                if b >= 2:
                    act.wait_ge(sem("d_kd"), 8 * (b - 1))
                A(kdecD[b % 2], lcD[b % 2][:, 64:128], ACT.Exp, scale=-1.0).then_inc(sem("d_kdec"), 1)

            def d_v(b, hf, t):
                n = 8 * b + 4 * hf + t
                act.wait_ge(sem("d_vp"), n + 1)
                if b and t == 0:
                    act.wait_ge(sem("d_pv"), 8 * b - 8 + 4 * hf + 4)
                A(v3(vD[hf], NT)[:, t, :], where["d_v", n][:, :], ACT.Copy).then_inc(sem("d_vs"), 1)

            def d_decays(g):
                b, p = g // 8, g % 8
                act.wait_ge(sem("d_lp"), g + 1)
                if g >= 3:
                    act.wait_ge(sem("d_st"), g - 2)
                    act.wait_ge(sem("d_qe"), g - 2)
                A(elD[g % 3], bank[0][:, :], ACT.Exp, scale=-1.0).then_inc(sem("d_el"), 1)
                if p == 0:
                    act.wait_ge(sem("d_lcs"), b + 1)
                if g >= 2:
                    act.wait_ge(sem("d_at"), 2 * (g - 1))
                for hh in range(2):
                    act.wait_ge(sem("d_la"), 2 * g + hh + 1)
                    for c in range(NT):
                        k = c * H + 2 * p + hh
                        i = A(dmD[g % 2][:, (2 * c + hh) * P:(2 * c + hh + 1) * P], bank[1 - hh][:, c * P:(c + 1) * P],
                              ACT.Exp, scale=-1.0, bias=lcD[b % 2][:, k:k + 1])
                    i.then_inc(sem("d_dm"), 1)

            def d_tanh(g, i):
                src = where["d_p", g, i][:, :]
                if i < 2:
                    act.wait_ge(sem("d_pp"), 2 * g + i + 1)
                    if g:
                        act.wait_ge(sem("d_silu"), 2 * g - 1 + i)
                    A(tqD[i], src, ACT.Tanh, scale=0.5).then_inc(sem("d_tq"), 1)
                else:
                    act.wait_ge(sem("d_gp_"), g + 1)
                    if g >= 8:
                        act.wait_ge(sem("d_og"), g - 7)
                    A(thD[g % 8], src, ACT.Tanh, scale=0.5).then_inc(sem("d_th"), 1)

            def d_o(g):
                act.wait_ge(sem("d_pv"), g + 1)
                act.wait_ge(sem("d_bs"), g + 1)
                if g >= 12:
                    act.wait_ge(y_ready, PD + (g - 12) // 8 + 1)
                elif g == 0:
                    act.wait_ge(y_ready, PB + 4)
                A(o_slot(PD + g // 8, g % 8), bank[5][:, :], ACT.Copy).then_inc(sem("d_o"), 1)

            def d_affine(k):
                act.wait_ge(sem("d_AB"), k + 1)
                act.wait_ge(sem("d_o"), 4 * k + 4)
                b, p0 = k // 2, 4 * (k % 2)
                for i in range(4):
                    o = o_slot(PD + b, p0 + i)
                    A(o, o, ACT.Identity, scale=gateD[k % 2][:, i:i + 1], bias=gateD[k % 2][:, 4 + i:5 + i])\
                        .then_inc(sem("d_on"), 1)

            def phase_d():
                enter(act, 3)
                d_softplus(0)
                for t in range(NT):
                    d_v(0, 0, t)
                d_kdec(0)
                d_tanh(0, 0)
                d_tanh(0, 1)
                d_decays(0)
                for g in range(32 + 4):
                    b, s = g // 8, g % 8
                    if g + 1 < 32:
                        d_tanh(g + 1, 0)
                        d_tanh(g + 1, 1)
                        d_decays(g + 1)
                    if 1 <= g <= 32:
                        d_tanh(g - 1, 2)
                    if 2 <= g < 34:
                        d_o(g - 2)
                    if s in (0, 4) and g >= 8:
                        d_affine((g - 8) // 4)
                    if g >= 16:
                        tail(PD + b - 2, s + 8)
                    if g < 32:
                        tail(PD + b - 1, s)
                        if s in (2, 3):
                            d_v(b, 1, 2 * s - 4)
                            d_v(b, 1, 2 * s - 3)
                        if b + 1 < NB:
                            if s == 2:
                                d_softplus(b + 1)
                            if s == 4:
                                d_kdec(b + 1)
                            if s in (6, 7):
                                d_v(b + 1, 0, 2 * s - 12)
                                d_v(b + 1, 0, 2 * s - 11)
                d_affine(7)

            cross(1)
            moe(2)
            phase_d()
            cross(4)
            moe(5)
            for s in range(32):
                tail(WORKS - 1, s)

        @block_ctx.vector
        def _(dve):
            V = nc.vector
            chain = [0]

            def link(ins):
                chain[0] += 1
                ins.then_inc(dve_chain, 1)
                dve.wait_ge(dve_chain, chain[0])

            def ln_stats(src):
                for t in range(NT):
                    i = V.bn_stats(bn[:, t, :], src[:, t, :])
                link(i)
                for t in range(NT):
                    i = V.bn_aggr(mv[:, t, :], bn[:, t, :])
                link(i)
                link(V.tensor_scalar(lnv[:, 0, :], mv[:, :, 1], EPS, None, ALU.add))

            def rsqrt(var, tmp, y):
                link(V.tensor_scalar(tmp.bitcast(U32), var.bitcast(U32), 1, None, ALU.logical_shift_right))
                link(V.tensor_scalar(y.bitcast(U32), tmp.bitcast(U32), -1.0, 1597463007.0, ALU.mult, ALU.add))
                for _ in range(3):
                    link(V.tensor_tensor(tmp, y, y, ALU.mult))
                    link(V.scalar_tensor_tensor(out=tmp, in0=tmp, scalar=-0.5, in1=var, op0=ALU.mult, op1=ALU.mult))
                    link(V.scalar_tensor_tensor(out=y, in0=tmp, scalar=1.5, in1=y, op0=ALU.add, op1=ALU.mult))

            def ln_rstd():
                rsqrt(lnv[:, 0, :], lnv[:, 2, :], lnv[:, 1, :])

            def ln_apply(src, dst, rstd=True):
                if rstd:
                    ln_rstd()
                for t in range(NT):
                    i = V.tensor_scalar(dst[:, t, :], src[:, t, :], mv[:, t, 0:1], lnv[:, 1, t:t + 1],
                                        ALU.subtract, ALU.mult)
                return i

            def tail(w, s):
                ph, b = w // NB, w % NB
                at = tail_steps(w)
                x = x_all[:, 4 * b:4 * b + 4, :]
                if s == at[1]:
                    dve.wait_ge(yt_ready, w + 1)
                    V.tensor_tensor(res[:, :, :], x, v3(where["yt", w][:, :], NT), ALU.add).then_inc(sem("sum_done"), 1)
                    if not spread_norm(w):
                        dve.wait_ge(sem("sum_done"), w + 1)
                        ln_stats(res)
                if spread_norm(w):
                    if s == at[1] + 1:
                        dve.wait_ge(sem("sum_done"), w + 1)
                        ln_stats(res)
                    if s == at[1] + 2:
                        ln_rstd()
                    if s == at[2] and ph != 1:
                        ln_apply(res, x, rstd=False).then_inc(x_ready, 1)
                    if s == at[2] and ph == 1:
                        ln_apply(res, res, rstd=False).then_inc(sem("B_own"), 1)
                    if ph == 1 and s == at[3]:
                        dve.wait_ge(sem("B_sum2"), b + 1)
                        ln_stats(res)
                    if ph == 1 and s == at[3] + 1:
                        ln_rstd()
                    if ph == 1 and s == at[3] + 2:
                        ln_apply(res, x, rstd=False).then_inc(x_ready, 1)
                elif ph == 1:
                    if s == at[2]:
                        ln_apply(res, res).then_inc(sem("B_own"), 1)
                    if s == at[3]:
                        dve.wait_ge(sem("B_sum2"), b + 1)
                        ln_stats(res)
                        ln_apply(res, x).then_inc(x_ready, 1)
                elif s == at[2]:
                    ln_apply(res, x).then_inc(x_ready, 1)

            def split_rows(src, n, dst, read):
                link(V.tensor_copy(dst[0:n, :], src))
                V.tensor_tensor(spl_r[0:n, :], src, dst[0:n, :], ALU.subtract).then_inc(sem(read[0]), 1)
                dve.wait_ge(sem(read[0]), read[1])
                link(V.tensor_copy(spl_m[0:n, :], spl_r[0:n, :]))
                V.tensor_copy(dst[32:32 + n, :], spl_m[0:n, :])
                return V.tensor_tensor(dst[64:64 + n, :], spl_r[0:n, :], spl_m[0:n, :], ALU.subtract)

            def a_split(g, step):
                tiles = [(2 * (g % 2) + hh, HALF[hh], HALF[1 - hh]) for hh in range(2)]
                if step == 0:
                    dve.wait_ge(sem("a_ke"), g + 1)
                    if g >= 2:
                        dve.wait_ge(sem("a_s"), 8 * (g - 1))
                    for i, own, other in tiles:
                        m = V.tensor_copy(k1A[i][own, :], ktA[own, :])
                    link(m)
                elif step in (1, 2):
                    i, own, other = tiles[step - 1]
                    m = V.tensor_tensor(k1A[i][other, :], ktA[own, :], k1A[i][own, :].bitcast(F32), ALU.subtract)
                    if step == 2:
                        m.then_inc(sem("a_ks"), 1)
                elif step == 3:
                    dve.wait_ge(sem("a_qe"), g + 1)
                    for i, own, other in tiles:
                        m = V.tensor_copy(q1A[i][own, :], qtA[own, :])
                    link(m)
                elif step in (4, 5):
                    i, own, other = tiles[step - 4]
                    m = V.tensor_tensor(q2A[i][own, :], qtA[own, :], q1A[i][own, :].bitcast(F32), ALU.subtract)
                    if step == 5:
                        link(m)
                else:
                    for i, own, other in tiles:
                        m = V.tensor_copy(q1A[i][other, :], q2A[i][own, :].bitcast(F32))
                    m.then_inc(sem("a_qs"), 1)

            def a_max(u):
                dve.wait_ge(sem("a_s"), u + 1)
                if u >= 8:
                    dve.wait_ge(sem("a_e"), u - 7)
                V.tensor_reduce(nmax[:, u % 8:u % 8 + 1], bank[u % 3][:, :], AX, ALU.max, negate=True)\
                    .then_inc(sem("a_mx"), 1)

            def a_norm(u):
                r = slice(u % 8, u % 8 + 1)
                dve.wait_ge(sem("a_e"), u + 1)
                if u >= 8:
                    dve.wait_ge(sem("a_n"), u - 7)
                V.reciprocal(rsum[1][:, r], rsum[0][:, r]).then_inc(sem("a_r"), 1)

            loaded(dve, "x0")
            ln_stats(x_all[:, 0:4, :])
            ln_apply(x_all[:, 0:4, :], v3(xn, NT)).then_inc(sem("a_xn"), 1)
            loaded(dve, "small", DMA_COUNT["small"])
            loaded(dve, "masks")
            V.tensor_copy(ident_b[:, :], ident)
            V.tensor_copy(sel[:, :], const("sel", masks_in, NKEPT))
            V.tensor_copy(heads[:, :], const("heads", masks_in, NKEPT))
            V.tensor_copy(mask[:, :], const("mask", masks_in, NKEPT)).then_inc(consts_ready, 1)
            for step in range(7):
                a_split(0, step)
            NU = NB * UNITS
            for u in range(NU + 1):
                b, s, g, j = u // UNITS, u % UNITS, u // 8, u % 8
                if u >= 1:
                    a_norm(u - 1)
                if u < NU:
                    a_max(u)
                if j <= 6 and g + 1 < 32:
                    a_split(g + 1, j)
                if u < NU:
                    if b:
                        tail(b - 1, s)
                    if u == 22:
                        loaded(dve, "x", DMA_COUNT["x"])
                    if b + 1 < NB and s == 23:
                        ln_stats(x_all[:, 4 * b + 4:4 * b + 8, :])
                    if b + 1 < NB and s == 24:
                        ln_rstd()
                    if b + 1 < NB and s == 25:
                        dve.wait_ge(sem("a_xnp"), b + 1)
                        ln_apply(x_all[:, 4 * b + 4:4 * b + 8, :], v3(xn, NT), rstd=False).then_inc(sem("a_xn"), 1)

            def cross_k(c):
                n = c["n"]
                dve.wait_ge(sem(n + "_zero"), 1)
                kd = kdB.rearrange("p (q b h c) -> p q b h c", q=NPAIR, b=NB, h=2)
                for p in range(c["np"]):
                    dve.wait_ge(sem(n + "_kp"), p + 1)
                    src = where[n + "k", p]
                    for hh in range(2):
                        r = slice(hh * DH, (hh + 1) * DH)
                        s_ = src[r, 0:NB * C].rearrange("p (b c) -> p b c", b=NB)
                        if c["bias"]:
                            i = V.tensor_scalar(kd[r, p, :, hh, :], s_, col("bk", p)[r, :], None, ALU.add)
                        else:
                            i = V.tensor_copy(kd[r, p, :, hh, :], s_)
                    i.then_inc(sem(n + "_ks"), 1)

            def cross_sub(c, b, t):
                n, np_ = c["n"], c["np"]
                u = NT * b + t
                dve.wait_ge(sem(n + "_s"), u + 1)
                m = statB[u % 2]
                parts = [(q, min(3, np_ - 3 * q)) for q in range((np_ + 2) // 3)]
                for q, k in parts:
                    i = V.tensor_reduce(m[:, 6 * q:6 * q + 2 * k], v3(bank[q][:, 0:2 * k * C], 2 * k), AX, ALU.max)
                link(i)
                if u >= 3:
                    dve.wait_ge(sem(n + "_t"), (np_ // 2) * (u - 2))
                for q, k in parts:
                    i = V.tensor_tensor(v3(pB[u % 3][:, 0:H * C], H)[:, 6 * q:6 * q + 2 * k, :], v3(bank[q][:, 0:2 * k * C], 2 * k),
                                        m[:, 6 * q:6 * q + 2 * k].unsqueeze(2).to_broadcast([P, 2 * k, C]), ALU.subtract)
                i.then_inc(sem(n + "_sub"), 1)

            def cross_norm(c, b, t):
                n, hs = c["n"], 2 * c["np"]
                u = NT * b + t
                dve.wait_ge(sem(n + "_e"), u + 1)
                p = v3(pB[u % 3][:, 0:hs * C], hs)
                if u >= 3:
                    dve.wait_ge(sem(n + "_n"), u - 2)
                link(V.tensor_reduce(statB[2][:, 0:hs], p, AX, ALU.add))
                V.reciprocal(statB[3 + u % 3][:, 0:hs], statB[2][:, 0:hs]).then_inc(sem(n + "_r"), 1)

            def cross(ph):
                c = CROSS[ph]
                n, w0 = c["n"], c["w0"]
                enter(dve, ph)
                if ph == 1:
                    loaded(dve, "late", DMA_COUNT["late"])
                cross_k(c)
                for u in range(NB * NT + 3):
                    b, t = u // NT, u % NT
                    if b < NB:
                        cross_sub(c, b, t)
                    if 1 <= u < NB * NT + 1:
                        cross_norm(c, (u - 1) // NT, (u - 1) % NT)
                    if u < NT:
                        for s in range(3 * u, 3 * u + 3):
                            tail(w0 - 1, s)
                    cross_tail(tail, w0, u)
                    if u == NB * NT:
                        m_ = MOE[ph + 1]
                        enter(dve, ph + 1)
                        loaded(dve, m_["n"], DMA_COUNT[m_["n"]])
                        moe_split_x(m_, 0)
                        moe_split_w(m_, 0)
                    if u == NB * NT + 1:
                        moe_route1(MOE[ph + 1], 0)

            def bc(ap):
                return ap.to_broadcast([P, 4, 8])

            def split_to(high, low, src):
                link(V.tensor_copy(high, src))
                return V.tensor_tensor(low, src, high.bitcast(F32), ALU.subtract)

            def moe_split_x(m_, b):
                n = m_["n"]
                dve.wait_ge(xT_ready, m_["w0"] - NB + b + 1)
                if b >= 2:
                    dve.wait_ge(sem(n + "_hp"), (b - 1) * E * m_["ft"])
                split_to(xh_M[b % 2], xl_M[b % 2], xT_all[:, b, :]).then_inc(sem(n + "_xs"), 1)

            def moe_split_w(m_, c):
                if c < E * m_["ft"] // 4:
                    r = slice(4 * c * P, (4 * c + 4) * P)
                    split_to(w1_high[:, r], m_["low"][:, r], m_["w1"][:, r]).then_inc(sem(m_["n"] + "_ws"), 1)

            def moe_route1(m_, b):
                n = m_["n"]
                dve.wait_ge(sem(n + "_lgp"), b + 1)
                lg = rt[:, 0, :, :]
                src = v3(where[n + "lg", b][:, 0:4 * E], 4)
                if n == "C":
                    V.tensor_copy(lg, src).then_inc(sem(n + "_lg"), 1)
                    dve.wait_ge(sem(n + "_lg"), b + 1)
                    for t in range(NT):
                        i = V.max(out=rt[:, 1, t, :], in_=rt[:, 0, t, :])
                    link(i)
                    V.tensor_tensor(lnv[:, 3, :], rt[:, 1, :, 1], rt[:, 1, :, 0], ALU.subtract).then_inc(sem(n + "_d"), 1)
                    for t in range(NT):
                        i = V.max_index(out=ri[:, t, :], in_max=rt[:, 1, t, :], in_values=rt[:, 0, t, :])
                    link(i)
                    link(V.tensor_copy(rt[:, 3, :, :], ri[:, :, :]))
                else:
                    br = rows[:, ROWS["br"][0]:ROWS["br"][1]].unsqueeze(1).to_broadcast([P, 4, 8])
                    V.tensor_tensor(lg, src, br, ALU.add).then_inc(sem(n + "_lg"), 1)
                    dve.wait_ge(sem(n + "_lg"), b + 1)
                    link(V.tensor_reduce(rt[:, 3, :, 0], lg, AX, ALU.max))
                    V.tensor_tensor(rt[:, 1, :, :], lg, bc(rt[:, 3, :, 0:1]), ALU.subtract).then_inc(sem(n + "_d"), 1)

            def moe_route2(m_, b):
                n = m_["n"]
                dve.wait_ge(sem(n + "_e"), b + 1)
                if b:
                    dve.wait_ge(sem(n + "_wTp"), b)
                io = iota.unsqueeze(1).to_broadcast([P, 4, 8])
                if n == "C":
                    e = lnv[:, 4, :]
                    link(V.tensor_scalar(rt[:, 4, :, 0], e, 1.0, None, ALU.add))
                    link(V.reciprocal(rt[:, 5, :, 0], rt[:, 4, :, 0]))
                    link(V.tensor_tensor(rt[:, 5, :, 1], rt[:, 5, :, 0], e, ALU.mult))
                    for k in range(2):
                        link(V.tensor_tensor(rt[:, 6 + k, :, :], io, bc(rt[:, 3, :, k:k + 1]), ALU.is_equal))
                        link(V.tensor_tensor(rt[:, 8 + k, :, :], rt[:, 6 + k, :, :], bc(rt[:, 5, :, k:k + 1]), ALU.mult))
                    V.tensor_tensor(rt[:, 11, :, :], rt[:, 8, :, :], rt[:, 9, :, :], ALU.add).then_inc(sem(n + "_wt"), 1)
                else:
                    link(V.tensor_reduce(rt[:, 4, :, 0], rt[:, 2, :, :], AX, ALU.add))
                    link(V.reciprocal(rt[:, 5, :, 0], rt[:, 4, :, 0]))
                    link(V.tensor_tensor(rt[:, 6, :, :], rt[:, 2, :, :], bc(rt[:, 5, :, 0:1]), ALU.mult))
                    for t in range(NT):
                        i = V.max(out=rt[:, 7, t, :], in_=rt[:, 6, t, :])
                    link(i)
                    for t in range(NT):
                        i = V.max_index(out=ri[:, t, :], in_max=rt[:, 7, t, :], in_values=rt[:, 6, t, :])
                    link(i)
                    link(V.tensor_copy(rt[:, 8, :, :], ri[:, :, :]))
                    link(V.tensor_tensor(rt[:, 9, :, :], io, bc(rt[:, 8, :, 0:1]), ALU.is_equal))
                    V.tensor_tensor(rt[:, 11, :, :], rt[:, 9, :, :], bc(rt[:, 7, :, 0:1]), ALU.mult)\
                        .then_inc(sem(n + "_wt"), 1)

            def moe_route3(m_, b):
                n = m_["n"]
                dve.wait_ge(sem(n + "_wTp"), b + 1)
                src = where[n + "wT", b][0:E, :]
                V.tensor_copy(wT_C[0:E, (b % 2) * S:(b % 2 + 1) * S], src)
                if n == "C":
                    dve.wait_ge(sem("C_zero"), 1)
                split_rows(src, E, wsel_b[b % 2], (n + "_wTr", b + 1)).then_inc(sem(n + "_sel"), 1)

            def moe(ph):
                m_ = MOE[ph]
                n, ft = m_["n"], m_["ft"]
                steps = E * ft
                enter(dve, ph)
                c = CROSS[ph - 1]
                dve.wait_ge(sem(c["n"] + "_pv"), NB * c["np"])
                moe_route2(m_, 0)
                moe_route3(m_, 0)
                moe_split_w(m_, 1)
                for i in range(NB * steps):
                    b, s = i // steps, i % steps
                    tail(m_["w0"] + b - 1, s)
                    if b + 1 < NB:
                        if s == m_["route"][0]:
                            moe_route1(m_, b + 1)
                        if s == m_["route"][2]:
                            moe_route2(m_, b + 1)
                        if s == m_["route"][3]:
                            moe_route3(m_, b + 1)
                        if s == m_["route"][3] + 1:
                            moe_split_x(m_, b + 1)
                    if b == 0 and s % 4 == 0:
                        moe_split_w(m_, s // 4 + 2)
                    dve.wait_ge(sem(n + "_h"), i + 1)
                    dve.wait_ge(sem(n + "_wb"), i // ft + 1)
                    if i >= 3:
                        k = i - 3
                        if k % steps == steps - 1:
                            dve.wait_ge(y_ready, m_["w0"] + k // steps + 1)
                        else:
                            dve.wait_ge(sem(n + "_c"), k + 1 - k // steps)
                    V.tensor_tensor(hwC[i % 3], hsC[i % 3], bank[3 + (s // ft) % 2][:, :], ALU.mult)\
                        .then_inc(sem(n + "_hw"), 1)

            def d_split_x(b):
                dve.wait_ge(xT_ready, PC + b + 1)
                if b >= 2:
                    dve.wait_ge(sem("d_gp_"), 8 * (b - 1))
                split_to(xh_D[b % 2], xl_D[b % 2], xT_all[:, b, :]).then_inc(sem("d_xs"), 1)

            def d_split_w(i):
                which, half = D_SPLITS[i]
                r = slice(which * 1024 + half * S, which * 1024 + (half + 1) * S)
                split_to(wD_high[:, r], W1_low[:, r], W1[:, r]).then_inc(sem("d_ws"), 1)

            def d_z(b):
                dve.wait_ge(sem("d_al"), b + 1)
                ba = rows[:, ROWS["ba"][0]:ROWS["ba"][1]].unsqueeze(1).to_broadcast([P, NT, H])
                V.tensor_tensor(v3(spD[0], NT), v3(where["d_al", b][:, 0:64], NT), ba, ALU.add).then_inc(sem("d_z"), 1)
                dve.wait_ge(sem("d_z"), b + 1)
                link(V.tensor_scalar(spD[1], spD[0], -1.0, None, ALU.mult))
                V.tensor_tensor(spD[1], spD[1], spD[0], ALU.max).then_inc(sem("d_az"), 1)

            def d_sp(b):
                dve.wait_ge(sem("d_ln"), b + 1)
                V.scalar_tensor_tensor(out=spD[3], in0=spD[0], scalar=0.0, in1=spD[2], op0=ALU.max, op1=ALU.add)\
                    .then_inc(sem("d_sp"), 1)

            def d_lsel(b):
                dve.wait_ge(sem("d_LT"), b + 1)
                split_rows(where["d_LT", b][0:H, :], H, lsel_b[b % 2], ("d_LTr", b + 1)).then_inc(sem("d_lsel"), 1)
                dve.wait_ge(sem("d_lcp"), b + 1)
                V.tensor_copy(lcD[b % 2], where["d_lc", b][:, 0:128]).then_inc(sem("d_lcs"), 1)

            def d_silu(g, i):
                dve.wait_ge(sem("d_tq"), 2 * g + i + 1)
                if g >= 2:
                    dve.wait_ge(sem("d_s"), 2 * (g - 1))
                    if i:
                        dve.wait_ge(sem("d_kt"), g - 1)
                    else:
                        dve.wait_ge(sem("d_qe"), g - 1)
                th = tqD[i]
                out = qTD[g % 2] if i == 0 else kTD[g % 2]
                V.scalar_tensor_tensor(out=out, in0=th, scalar=1.0, in1=where["d_p", g, i][:, :],
                                       op0=ALU.add, op1=ALU.mult).then_inc(sem("d_silu"), 1)

            def d_kd(g):
                b, p = g // 8, g % 8
                dve.wait_ge(sem("d_kt"), g + 1)
                dve.wait_ge(sem("d_kdec"), b + 1)
                if g >= 2:
                    dve.wait_ge(sem("d_dl"), g - 1)
                kdec = v3(kdecD[b % 2], NT)[:, :, 2 * p:2 * p + 2].unsqueeze(3).to_broadcast([P, NT, 2, DH])
                V.tensor_tensor(kdD[g % 2].rearrange("p (c h d) -> p c h d", c=NT, h=2),
                                bank[4][:, :].rearrange("p (c h d) -> p c h d", c=NT, h=2), kdec, ALU.mult)\
                    .then_inc(sem("d_kd"), 1)

            def d_at(g):
                dve.wait_ge(sem("d_dm"), 2 * g + 2)
                if g >= 3:
                    dve.wait_ge(sem("d_pv"), g - 2)
                for c2 in range(2):
                    dve.wait_ge(sem("d_s"), 2 * g + c2 + 1)
                    r = slice(c2 * S, (c2 + 1) * S)
                    V.scalar_tensor_tensor(out=atD[g % 3][:, r], in0=bank[2 + c2][:, :], scalar=0.25, in1=dmD[g % 2][:, r],
                                           op0=ALU.mult, op1=ALU.mult).then_inc(sem("d_at"), 1)

            def d_st(g):
                dve.wait_ge(sem("d_dl"), g + 1)
                dve.wait_ge(sem("d_el"), g + 1)
                if g >= 2:
                    dve.wait_ge(sem("d_pv"), g - 1)
                st, el = v3(stD[g % 2], NT - 1), elD[g % 3]
                halves = [slice(hh * DH, (hh + 1) * DH) for hh in range(2)]
                for r in halves:
                    i = V.tensor_scalar(st[r, :, r], v3(bank[4][:, 0:3 * P], NT - 1)[r, :, r], 0.25, None, ALU.mult)
                link(i)
                for c in (1, 2):
                    for r in halves:
                        i = V.scalar_tensor_tensor(out=st[r, c, r], in0=st[r, c - 1, r], scalar=el[r, c * P + P - 1:c * P + P],
                                                   in1=st[r, c, r], op0=ALU.mult, op1=ALU.add)
                    if c == 1:
                        link(i)
                i.then_inc(sem("d_st"), 1)

            def d_stats(g):
                dve.wait_ge(sem("d_pv"), g + 1)
                V.bn_stats(gn6[:, 0:6], bank[5][:, :]).then_inc(sem("d_bs"), 1)
                dve.wait_ge(sem("d_bs"), g + 1)
                i = V.bn_aggr(gnD[6][:, 0:2], gn6[:, 0:6])
                link(i)
                k = g % 8
                V.tensor_copy(gnD[0][:, k:k + 1], gnD[6][:, 0:1])
                i = V.tensor_copy(gnD[1][:, k:k + 1], gnD[6][:, 1:2])
                if g % 4 == 3:
                    i.then_inc(sem("d_gs"), 1)
                else:
                    link(i)

            def d_spread(k):
                dve.wait_ge(sem("d_gp"), 2 * k + 1)
                dve.wait_ge(sem("d_gs"), 2 * k + 1)
                V.tensor_copy(gnD[7][:, 0:4], where["d_gn", 2 * k][:, 0:4]).then_inc(sem("d_gr"), 1)
                dve.wait_ge(sem("d_gr"), 2 * k + 1)
                r = slice(4 * (k % 2), 4 * (k % 2) + 4)
                link(V.tensor_tensor(gnD[2][:, 0:4], gnD[0][:, r], gnD[7][:, 0:4], ALU.subtract))
                link(V.tensor_tensor(gnD[2][:, 0:4], gnD[2][:, 0:4], gnD[2][:, 0:4], ALU.mult))
                V.tensor_tensor(gnD[2][:, 0:4], gnD[2][:, 0:4], gnD[1][:, r], ALU.add).then_inc(sem("d_gs"), 1)

            def d_var(k):
                dve.wait_ge(sem("d_gp"), 2 * k + 2)
                V.tensor_scalar(gnD[3][:, 0:4], where["d_gn", 2 * k + 1][:, 0:4], EPS, None, ALU.add)\
                    .then_inc(sem("d_gr"), 1)

            def d_gate(k):
                b, p0 = k // 2, 4 * (k % 2)
                dve.wait_ge(sem("d_gr"), 2 * k + 2)
                rsqrt(gnD[3][:, 0:4], gnD[4][:, 8:12], gnD[6][:, 8:12])
                gw, gb = (cols[:, COLS[n][0] + p0:COLS[n][0] + p0 + 4] for n in ("gn_w", "gn_b"))
                A_, B_ = gateD[k % 2][:, 0:4], gateD[k % 2][:, 4:8]
                link(V.scalar_tensor_tensor(out=A_, in0=gw, scalar=0.5, in1=gnD[6][:, 8:12], op0=ALU.mult, op1=ALU.mult))
                link(V.tensor_tensor(B_, gnD[7][:, 0:4], A_, ALU.mult))
                V.scalar_tensor_tensor(out=B_, in0=gb, scalar=0.5, in1=B_, op0=ALU.mult, op1=ALU.subtract)\
                    .then_inc(sem("d_AB"), 1)

            def d_gated(k, pairs):
                b, p0 = k // 2, 4 * (k % 2)
                for i in pairs:
                    dve.wait_ge(sem("d_on"), 4 * k + i + 1)
                    o = o_slot(PD + b, p0 + i)
                    V.scalar_tensor_tensor(out=o, in0=thD[p0 + i], scalar=1.0, in1=o, op0=ALU.add, op1=ALU.mult)\
                        .then_inc(sem("d_og"), 1)

            def phase_d():
                enter(dve, 3)
                dve.wait_ge(sem("d_zero"), 1)
                loaded(dve, "D", DMA_COUNT["D"])
                d_split_x(0)
                d_split_w(0)
                d_z(0)
                d_split_w(1)
                d_sp(0)
                d_split_w(2)
                d_lsel(0)
                d_silu(0, 0)
                d_silu(0, 1)
                for g in range(32 + 4):
                    b, s = g // 8, g % 8
                    if 1 <= g <= 32:
                        d_st(g - 1)
                    if g + 1 < 32:
                        d_silu(g + 1, 0)
                        d_silu(g + 1, 1)
                    if g < 32:
                        d_at(g)
                        d_kd(g)
                    for i in range(3 + 2 * g, min(5 + 2 * g, len(D_SPLITS))):
                        d_split_w(i)
                    if s == 5 and b + 1 < NB:
                        d_split_x(b + 1)
                    if 2 <= g < 34:
                        d_stats(g - 2)
                    if s in (2, 6) and g >= 6:
                        d_spread((g - 6) // 4)
                    if s in (3, 7) and g >= 7:
                        d_var((g - 7) // 4)
                    if s in (1, 5) and g >= 9:
                        d_gated((g - 9) // 4, (0, 1, 2, 3))
                    if g >= 16:
                        tail(PD + b - 2, s + 8)
                    if g < 32:
                        tail(PD + b - 1, s)
                        if b + 1 < NB:
                            if s == 2:
                                d_z(b + 1)
                                d_sp(b + 1)
                            if s == 4:
                                d_lsel(b + 1)
                    if s in (3, 7) and g >= 7:
                        d_gate((g - 7) // 4)
                d_gated(7, (0, 1, 2, 3))

            cross(1)
            moe(2)
            phase_d()
            cross(4)
            moe(5)
            for s in range(32):
                tail(WORKS - 1, s)

        @block_ctx.gpsimd
        def _(pool):
            G = nc.gpsimd
            chain = [0]

            def link(ins):
                chain[0] += 1
                ins.then_inc(pool_chain, 1)
                pool.wait_ge(pool_chain, chain[0])

            pool.wait_ge(consts_ready, 1)
            G.memset(wselC, 0.0).then_inc(sem("C_zero"), 1)
            for u in range(NB * UNITS):
                pool.wait_ge(sem("a_r"), u + 1)
                G.tensor_tensor(pA[u % 5], pA[u % 5], rsum[1][:, u % 8:u % 8 + 1].to_broadcast([P, S]), ALU.mult)\
                    .then_inc(sem("a_n"), 1)

            def tail(w, s):
                b = w % NB
                if w // NB == 1 and s == tail_steps(w)[2]:
                    pool.wait_ge(sem("B_own"), b + 1)
                    g, bb = (rows[:, ROWS[k][0]:ROWS[k][1]].unsqueeze(1).to_broadcast([P, NT, D]) for k in ("xg", "xb"))
                    link(G.tensor_tensor(res[:, :, :], res[:, :, :], g, ALU.mult))
                    link(G.tensor_tensor(res[:, :, :], res[:, :, :], bb, ALU.add))
                    G.tensor_tensor(res[:, :, :], res[:, :, :], x_all[:, 4 * b:4 * b + 4, :], ALU.add)\
                        .then_inc(sem("B_sum2"), 1)

            def cross(ph):
                c = CROSS[ph]
                n = c["n"]
                if ph == 1:
                    loaded(pool, "late", DMA_COUNT["late"])
                    pool.wait_ge(sem("a_pt"), NB * UNITS)
                else:
                    enter(pool, ph)
                kd = kdB.rearrange("p (q b h c) -> p q b h c", q=NPAIR, b=NB, h=2)
                link(G.memset(kd[0:DH, 0:c["np"], :, 1, :], 0.0))
                G.memset(kd[DH:P, 0:c["np"], :, 0, :], 0.0).then_inc(sem(n + "_zero"), 1)
                if ph == 1:
                    enter(pool, ph)
                G.memset(vcB[DH:P, :], 0.0).then_inc(sem(n + "_zero"), 1)
                pool.wait_ge(sem(n + "_zero"), 2)
                if ph == 4:
                    G.memset(wselC, 0.0)
                for i in range(3):
                    z = G.memset(pB[i][:, 2 * c["np"] * C:2 * c["np"] * C + P - C], 0.0)
                z.then_inc(sem(n + "_zero"), 1)
                hs = 2 * c["np"]
                for u in range(NB * NT + 3):
                    if 1 <= u < NB * NT + 1:
                        pool.wait_ge(sem(n + "_r"), u)
                        i = (u - 1) % 3
                        p = v3(pB[i][:, 0:hs * C], hs)
                        G.tensor_tensor(p, p, statB[3 + i][:, 0:hs].unsqueeze(2).to_broadcast([P, hs, C]), ALU.mult)\
                            .then_inc(sem(n + "_n"), 1)
                    cross_tail(tail, c["w0"], u)
                for s in range(12):
                    tail(c["w0"] + NB - 1, s)

            def phase_d():
                enter(pool, 3)
                G.memset(lselD, 0.0)
                for i in range(2):
                    z = G.memset(stD[i], 0.0)
                z.then_inc(sem("d_zero"), 1)
                for g in range(32):
                    pool.wait_ge(sem("d_silu"), 2 * g + 1)
                    if g >= 2:
                        pool.wait_ge(sem("d_s"), 2 * (g - 1))
                    q = v3(qTD[g % 2], NT).unsqueeze(2).to_broadcast([P, NT, 2, P])
                    own = heads[:, :].unsqueeze(1).unsqueeze(3).to_broadcast([P, NT, 2, P])
                    G.tensor_tensor(qbD[g % 2].rearrange("p (c h i) -> p c h i", c=NT, h=2), q, own, ALU.mult)\
                        .then_inc(sem("d_qb"), 1)
                    pool.wait_ge(sem("d_el"), g + 1)
                    if g >= 3:
                        pool.wait_ge(sem("d_pv"), g - 2)
                    G.tensor_tensor(qeD[g % 3], qTD[g % 2], elD[g % 3], ALU.mult).then_inc(sem("d_qe"), 1)

            cross(1)
            phase_d()
            cross(4)


def kernel(**inputs):
    import numpy as np
    import concourse.bacc as bacc
    from concourse.bass_utils import run_bass_kernel_spmd

    I = {k: np.asarray(v) for k, v in inputs.items()}

    def by_partition(v, n):
        return v.reshape(n, P).T

    arrays = {"x": I["x"]}
    arrays["ctxT"] = I["ctx_1024"].reshape(NB * C, D).T
    for k in ("L0_attn_Wq", "L0_attn_Wk", "L0_attn_Wv", "L0_attn_Wo", "L0_xattn_Wq", "L0_xattn_Wk", "L0_xattn_Wv",
              "L0_xattn_Wo", "L1_attn_Wq", "L1_attn_Wk", "L1_attn_Wv", "L1_attn_Wg", "L1_attn_Wo", "L1_xattn_Wq",
              "L1_xattn_Wk", "L1_xattn_Wv", "L1_xattn_Wo", "L1_ffn_W1", "L1_ffn_W2", "L0_ffn_b2", "L1_ffn_b2"):
        arrays[k] = I[k]
    arrays["w1T"] = I["L0_ffn_w1"].reshape(E * FT0 * P, D).T
    arrays["w2T"] = I["L0_ffn_w2"].transpose(0, 2, 1).reshape(E * FT0 * P, D)
    arrays["cols"] = np.concatenate([by_partition(I[k], n) for k, n in (
        ("L0_attn_ln_gamma", 1), ("L0_attn_ln_beta", 1), ("L0_xattn_bq", 8), ("L0_xattn_bk", 8), ("L0_xattn_bv", 8),
        ("L0_xattn_bo", 1), ("L0_ffn_b1", 32), ("L1_attn_gn_w", 8), ("L1_attn_gn_b", 8), ("L1_xattn_bo", 1),
        ("L1_ffn_b1", 16))], axis=1)
    arrays["rows"] = np.concatenate([I["L0_xattn_ln_gamma"], I["L0_xattn_ln_beta"], I["L1_attn_ba"], I["L1_ffn_br"]])
    arrays["narrow"] = np.concatenate([I["L0_ffn_router_w"].T, I["L1_ffn_Wr"], I["L1_attn_Wa"]], axis=1)

    i = np.arange(P)
    c = np.zeros((P, NCONSTS), np.float32)
    c[:, 0:128] = np.eye(P)
    c[:, 128:256] = i[:, None] <= i[None, :]
    c[:, 256:384] = i[:, None] > i[None, :]
    c[:, 384:512] = (i[:, None] // DH == i[None, :] // DH) * (1.0 / DH)
    c[:, 512:520] = np.arange(E)
    for h in range(H):
        c[[h, 32 + h, 64 + h], 520 + h] = 1.0
    c[:, 536:1048] = np.tile((i[:, None] > i[None, :]) * 1e30, (1, NT))
    c[:, 1048:1050] = i[:, None] // DH == np.arange(2)[None, :]
    arrays["consts"] = c

    nc = bacc.Bacc("TRN2", target_bir_lowering=False, num_devices=1)
    T = {}
    feed = {}
    for k, a in arrays.items():
        a = np.ascontiguousarray(a)
        feed[f"in_{k}"] = a
        T[k] = nc.dram_tensor(f"in_{k}", a.shape, mybir.dt.from_np(a.dtype), kind="ExternalInput").ap()
    T["out"] = nc.dram_tensor("out_0", (NB, S, D), F32, kind="ExternalOutput").ap()
    decoder(nc, T)
    r = run_bass_kernel_spmd(nc, [feed], core_ids=[0])
    return r.results[0]["out_0"]
```
